# Optimizing a Trainium2 kernel written in Bass

```python
import numpy as np
import jax
import jax.numpy as jnp

def _softmax(x, axis=-1):
    return jax.nn.softmax(x, axis=axis)

def _gelu(x):
    return jax.nn.gelu(x, approximate=True)

def _silu(x):
    return jax.nn.silu(x)

def _sigmoid(x):
    return jax.nn.sigmoid(x)

def _layernorm(x, axis=-1, eps=1e-05):
    m = jnp.mean(x, axis=axis, keepdims=True)
    v = jnp.var(x, axis=axis, keepdims=True)
    return (x - m) / jnp.sqrt(v + eps)

def _scatter_add(tgt, idx, src, axis=0):
    return tgt.at[idx].add(src)

def _segment_sum(src, seg, n):
    return jax.ops.segment_sum(src, seg, n)
kernel_name = 'mk_decoder_preln_d2_seqx_r4_453f10'

def setup_inputs(seed: int=0):
    np.random.seed(seed)
    _w = jnp.asarray

    def _rec_inputs():
        import jax
        import jax.numpy as jnp
        _rk = jax.random.key(seed)
        x = -0.0002928 + 1 * jax.random.normal(jax.random.fold_in(_rk, 1), (8, 256, 256), jnp.float32)
        _lenS = 256 - jax.random.randint(jax.random.fold_in(_rk, 7), (8,), 0, max(1, 256 // 4) + 1, jnp.int32)
        _lenS2 = 77 - jax.random.randint(jax.random.fold_in(_rk, 8), (8,), 0, max(1, 77 // 4) + 1, jnp.int32)
        _ctx_1024P = jax.random.normal(jax.random.fold_in(_rk, 11), (8, 16, 256), jnp.float32)
        _ctx_1024c = jax.random.dirichlet(jax.random.fold_in(_rk, 511), 0.3 * jnp.ones((16,), jnp.float32), (8, 77))
        _ctx_1024t = jnp.einsum('bsk,bkd->bsd', _ctx_1024c, _ctx_1024P)
        _ctx_1024t = _ctx_1024t * jax.lax.rsqrt(jnp.mean(jnp.square(_ctx_1024t)) + 1e-12) * 0.953939
        ctx_1024 = -1.39393e-06 + 0.999914 * (_ctx_1024t + 0.3 * jax.random.normal(jax.random.fold_in(_rk, 611), (8, 77, 256), jnp.float32))
        return (x, ctx_1024)
    x, ctx_1024 = _rec_inputs()

    def _L0_attn_setup():
        import jax, jax.numpy as jnp
        import numpy as np
        import math
        B, T, C = (8, 512, 256)
        DIM_ATT, DIM_FFN = (256, 1024)
        N_LAYER, LAYER_ID = (12, 1)
        EPS = 1e-05

        def layer_norm(x, w, b):
            mu = jnp.mean(x, axis=-1, keepdims=True)
            var = jnp.mean(jnp.square(x - mu), axis=-1, keepdims=True)
            return (x - mu) * jax.lax.rsqrt(var + EPS) * w + b

        def time_shift(x):
            return jnp.pad(x, ((0, 0), (1, 0), (0, 0)))[:, :-1, :]

        def wkv(time_decay, time_first, k, v):
            w = -jnp.exp(time_decay)
            u = time_first

            def step(carry, kv_t):
                aa, bb, pp = carry
                kt, vt = kv_t
                ww = u + kt
                qq = jnp.maximum(pp, ww)
                e1 = jnp.exp(pp - qq)
                e2 = jnp.exp(ww - qq)
                y = (e1 * aa + e2 * vt) / (e1 * bb + e2)
                ww2 = pp + w
                qq2 = jnp.maximum(ww2, kt)
                e1b = jnp.exp(ww2 - qq2)
                e2b = jnp.exp(kt - qq2)
                return ((e1b * aa + e2b * vt, e1b * bb + e2b, qq2), y)
            init = (jnp.zeros_like(k[:, 0]), jnp.zeros_like(k[:, 0]), jnp.full_like(k[:, 0], -1e+38))
            kT = jnp.swapaxes(k, 0, 1)
            vT = jnp.swapaxes(v, 0, 1)
            _, yT = jax.lax.scan(step, init, (kT, vT))
            return jnp.swapaxes(yT, 0, 1)
        key = jax.random.key(seed)
        ks = jax.random.split(key, 16)
        r01 = LAYER_ID / (N_LAYER - 1)
        r1a0 = 1.0 - LAYER_ID / N_LAYER
        ddd = (np.arange(C, dtype=np.float32) / C)[None, None, :]
        decay_speed = -5.0 + 8.0 * (np.arange(DIM_ATT, dtype=np.float32) / (DIM_ATT - 1)) ** (0.7 + 1.3 * r01)
        zigzag = np.array([(i + 1) % 3 - 1 for i in range(DIM_ATT)], dtype=np.float32) * 0.5

        def lin(k, out_d, in_d):
            return jax.random.normal(k, (out_d, in_d), jnp.float32) * (1.0 / math.sqrt(in_d))
        return {'x': jax.random.normal(ks[0], (B, T, C), jnp.float32), 'ln1_w': jnp.ones((C,), jnp.float32), 'ln1_b': jnp.zeros((C,), jnp.float32), 'ln2_w': jnp.ones((C,), jnp.float32), 'ln2_b': jnp.zeros((C,), jnp.float32), 'att_tmk': jnp.asarray(ddd ** r1a0), 'att_tmv': jnp.asarray(ddd ** r1a0 + 0.3 * r01), 'att_tmr': jnp.asarray(ddd ** (0.5 * r1a0)), 'time_decay': jnp.asarray(decay_speed), 'time_first': jnp.asarray(np.full(DIM_ATT, math.log(0.3), np.float32) + zigzag), 'Wk': lin(ks[1], DIM_ATT, C), 'Wv': lin(ks[2], DIM_ATT, C), 'Wr': lin(ks[3], DIM_ATT, C), 'Wo': lin(ks[4], C, DIM_ATT), 'ffn_tmk': jnp.asarray(ddd ** r1a0), 'ffn_tmr': jnp.asarray(ddd ** r1a0), 'Wkey': lin(ks[5], DIM_FFN, C), 'Wrec': lin(ks[6], C, C), 'Wval': lin(ks[7], C, DIM_FFN)}
    _L0_attn_all = _L0_attn_setup()
    _L0_attn_in = {k: v for k, v in _L0_attn_all.items() if k in ('ln1_w', 'ln1_b', 'ln2_w', 'ln2_b', 'att_tmk', 'att_tmv', 'att_tmr', 'time_decay', 'time_first', 'Wk', 'Wv', 'Wr', 'Wo', 'ffn_tmk', 'ffn_tmr', 'Wkey', 'Wrec', 'Wval')}
    del _L0_attn_all

    def _L0_xattn_setup():
        import jax, jax.numpy as jnp
        import numpy as np
        import math
        H = 16
        D_MODEL = 256
        D_K = D_MODEL // H

        def _split_heads(x):
            b, s, _ = x.shape
            return x.reshape(b, s, H, D_K).transpose(0, 2, 1, 3)
        key = jax.random.key(seed)
        ks = jax.random.split(key, 11)
        B, S = (2, 512)
        scale = 1.0 / math.sqrt(D_MODEL)
        inp = {'query': jax.random.normal(ks[0], (B, S, D_MODEL), dtype=jnp.float32), 'key': jax.random.normal(ks[1], (B, S, D_MODEL), dtype=jnp.float32), 'value': jax.random.normal(ks[2], (B, S, D_MODEL), dtype=jnp.float32), 'Wq': jax.random.normal(ks[3], (D_MODEL, D_MODEL), dtype=jnp.float32) * scale, 'bq': jnp.zeros((D_MODEL,), dtype=jnp.float32), 'Wk': jax.random.normal(ks[4], (D_MODEL, D_MODEL), dtype=jnp.float32) * scale, 'bk': jnp.zeros((D_MODEL,), dtype=jnp.float32), 'Wv': jax.random.normal(ks[5], (D_MODEL, D_MODEL), dtype=jnp.float32) * scale, 'bv': jnp.zeros((D_MODEL,), dtype=jnp.float32), 'Wo': jax.random.normal(ks[6], (D_MODEL, D_MODEL), dtype=jnp.float32) * scale, 'bo': jnp.zeros((D_MODEL,), dtype=jnp.float32)}
        return inp
    _L0_xattn_all = _L0_xattn_setup()
    _L0_xattn_in = {k: v for k, v in _L0_xattn_all.items() if k in ('Wq', 'bq', 'Wk', 'bk', 'Wv', 'bv', 'Wo', 'bo')}
    del _L0_xattn_all

    def _L0_ffn_setup():
        import jax, jax.numpy as jnp
        import numpy as np
        INT8_MAX = 127.0

        def _absmax_scale(x, axes):
            amax = jnp.max(jnp.abs(x), axis=axes, keepdims=True)
            return jnp.maximum(amax, 1e-12) / INT8_MAX
        key = jax.random.key(seed)
        k1, k2 = jax.random.split(key)
        lhs = jax.random.normal(k1, (4, 2048, 256), dtype=jnp.float32)
        rhs = jax.random.normal(k2, (256, 256), dtype=jnp.float32)
        return {'lhs': lhs, 'rhs': rhs}
    _L0_ffn_all = _L0_ffn_setup()
    _L0_ffn_in = {k: v for k, v in _L0_ffn_all.items() if k in ('rhs',)}
    del _L0_ffn_all

    def _L1_attn_setup():
        import jax, jax.numpy as jnp
        import numpy as np
        BATCH, SEQ, D_MODEL = (2, 1024, 256)
        D_STATE, EXPAND = (64, 2)
        D_INNER = D_MODEL * EXPAND

        def _silu(v):
            return v * jax.nn.sigmoid(v)
        key = jax.random.key(seed)
        ks = jax.random.split(key, 12)
        s = 0.02
        return {'x': jax.random.normal(ks[0], (BATCH, SEQ, D_MODEL), dtype=jnp.float32), 'W_in': jax.random.normal(ks[1], (D_MODEL, 2 * D_INNER), dtype=jnp.float32) * s, 'b_in': jnp.zeros((2 * D_INNER,), dtype=jnp.float32), 'W_xp': jax.random.normal(ks[2], (D_INNER, D_STATE), dtype=jnp.float32) * s, 'b_xp': jnp.zeros((D_STATE,), dtype=jnp.float32), 'W_dt': jax.random.normal(ks[3], (D_INNER, D_MODEL), dtype=jnp.float32) * s, 'b_dt': jnp.zeros((D_MODEL,), dtype=jnp.float32), 'W_out': jax.random.normal(ks[4], (D_INNER, D_MODEL), dtype=jnp.float32) * s, 'b_out': jnp.zeros((D_MODEL,), dtype=jnp.float32), 'A_log': jax.random.normal(ks[5], (D_STATE,), dtype=jnp.float32), 'D': jax.random.normal(ks[6], (D_MODEL,), dtype=jnp.float32)}
    _L1_attn_all = _L1_attn_setup()
    _L1_attn_in = {k: v for k, v in _L1_attn_all.items() if k in ('W_in', 'b_in', 'W_xp', 'b_xp', 'W_dt', 'b_dt', 'W_out', 'b_out', 'A_log', 'D')}
    del _L1_attn_all

    def _L1_xattn_setup():
        import jax, jax.numpy as jnp
        import numpy as np
        D = 256
        H = 16
        E = 8
        DK = D // H
        B, S = (2, 512)
        key = jax.random.key(seed)
        ks = jax.random.split(key, 16)
        sc = 1.0 / np.sqrt(D)
        inp = {'query': jax.random.normal(ks[0], (B, S, D), jnp.float32), 'key': jax.random.normal(ks[1], (B, S, D), jnp.float32), 'value': jax.random.normal(ks[2], (B, S, D), jnp.float32), 'Wq': jax.random.normal(ks[3], (D, D), jnp.float32) * sc, 'bq': jax.random.normal(ks[4], (D,), jnp.float32) * sc, 'Wk': jax.random.normal(ks[5], (D, D), jnp.float32) * sc, 'bk': jax.random.normal(ks[6], (D,), jnp.float32) * sc, 'Wv': jax.random.normal(ks[7], (D, D), jnp.float32) * sc, 'bv': jax.random.normal(ks[8], (D,), jnp.float32) * sc, 'We': jax.random.normal(ks[9], (E, D, D), jnp.float32) * sc, 'be': jax.random.normal(ks[10], (E, D), jnp.float32) * sc, 'Wo': jax.random.normal(ks[11], (D, D), jnp.float32) * sc, 'bo': jax.random.normal(ks[12], (D,), jnp.float32) * sc}
        return inp
    _L1_xattn_all = _L1_xattn_setup()
    _L1_xattn_in = {k: v for k, v in _L1_xattn_all.items() if k in ('Wq', 'bq', 'Wk', 'bk', 'Wv', 'bv', 'We', 'be', 'Wo', 'bo')}
    del _L1_xattn_all

    def _L1_ffn_setup():
        import jax, jax.numpy as jnp
        import numpy as np
        B, S, DIM = (2, 512, 256)
        HID = 512
        E, NSH, TOPK = (8, 2, 2)

        def _ffn(x, w1, w2, w3):
            return jax.nn.silu(x @ w1.T) * (x @ w3.T) @ w2.T
        key = jax.random.key(seed)
        ks = jax.random.split(key, 8)
        sc = 0.02
        return {'x': jax.random.normal(ks[0], (B, S, DIM), jnp.float32), 'router_w': jax.random.normal(ks[1], (E, DIM), jnp.float32) * sc, 'expert_bias': jnp.zeros((E,), jnp.float32), 'w1': jax.random.normal(ks[2], (E, HID, DIM), jnp.float32) * sc, 'w3': jax.random.normal(ks[3], (E, HID, DIM), jnp.float32) * sc, 'w2': jax.random.normal(ks[4], (E, DIM, HID), jnp.float32) * sc, 'sw1': jax.random.normal(ks[5], (NSH, HID, DIM), jnp.float32) * sc, 'sw3': jax.random.normal(ks[6], (NSH, HID, DIM), jnp.float32) * sc, 'sw2': jax.random.normal(ks[7], (NSH, DIM, HID), jnp.float32) * sc}
    _L1_ffn_all = _L1_ffn_setup()
    _L1_ffn_in = {k: v for k, v in _L1_ffn_all.items() if k in ('router_w', 'expert_bias', 'w1', 'w3', 'w2', 'sw1', 'sw3', 'sw2')}
    del _L1_ffn_all
    return {'x': x, 'ctx_1024': ctx_1024, 'L0_attn_ln1_w': _L0_attn_in['ln1_w'], 'L0_attn_ln1_b': _L0_attn_in['ln1_b'], 'L0_attn_ln2_w': _L0_attn_in['ln2_w'], 'L0_attn_ln2_b': _L0_attn_in['ln2_b'], 'L0_attn_att_tmk': _L0_attn_in['att_tmk'], 'L0_attn_att_tmv': _L0_attn_in['att_tmv'], 'L0_attn_att_tmr': _L0_attn_in['att_tmr'], 'L0_attn_time_decay': _L0_attn_in['time_decay'], 'L0_attn_time_first': _L0_attn_in['time_first'], 'L0_attn_Wk': _L0_attn_in['Wk'], 'L0_attn_Wv': _L0_attn_in['Wv'], 'L0_attn_Wr': _L0_attn_in['Wr'], 'L0_attn_Wo': _L0_attn_in['Wo'], 'L0_attn_ffn_tmk': _L0_attn_in['ffn_tmk'], 'L0_attn_ffn_tmr': _L0_attn_in['ffn_tmr'], 'L0_attn_Wkey': _L0_attn_in['Wkey'], 'L0_attn_Wrec': _L0_attn_in['Wrec'], 'L0_attn_Wval': _L0_attn_in['Wval'], 'L0_xattn_Wq': _L0_xattn_in['Wq'], 'L0_xattn_bq': _L0_xattn_in['bq'], 'L0_xattn_Wk': _L0_xattn_in['Wk'], 'L0_xattn_bk': _L0_xattn_in['bk'], 'L0_xattn_Wv': _L0_xattn_in['Wv'], 'L0_xattn_bv': _L0_xattn_in['bv'], 'L0_xattn_Wo': _L0_xattn_in['Wo'], 'L0_xattn_bo': _L0_xattn_in['bo'], 'L0_ffn_rhs': _L0_ffn_in['rhs'], 'L1_attn_W_in': _L1_attn_in['W_in'], 'L1_attn_b_in': _L1_attn_in['b_in'], 'L1_attn_W_xp': _L1_attn_in['W_xp'], 'L1_attn_b_xp': _L1_attn_in['b_xp'], 'L1_attn_W_dt': _L1_attn_in['W_dt'], 'L1_attn_b_dt': _L1_attn_in['b_dt'], 'L1_attn_W_out': _L1_attn_in['W_out'], 'L1_attn_b_out': _L1_attn_in['b_out'], 'L1_attn_A_log': _L1_attn_in['A_log'], 'L1_attn_D': _L1_attn_in['D'], 'L1_xattn_Wq': _L1_xattn_in['Wq'], 'L1_xattn_bq': _L1_xattn_in['bq'], 'L1_xattn_Wk': _L1_xattn_in['Wk'], 'L1_xattn_bk': _L1_xattn_in['bk'], 'L1_xattn_Wv': _L1_xattn_in['Wv'], 'L1_xattn_bv': _L1_xattn_in['bv'], 'L1_xattn_We': _L1_xattn_in['We'], 'L1_xattn_be': _L1_xattn_in['be'], 'L1_xattn_Wo': _L1_xattn_in['Wo'], 'L1_xattn_bo': _L1_xattn_in['bo'], 'L1_ffn_router_w': _L1_ffn_in['router_w'], 'L1_ffn_expert_bias': _L1_ffn_in['expert_bias'], 'L1_ffn_w1': _L1_ffn_in['w1'], 'L1_ffn_w3': _L1_ffn_in['w3'], 'L1_ffn_w2': _L1_ffn_in['w2'], 'L1_ffn_sw1': _L1_ffn_in['sw1'], 'L1_ffn_sw3': _L1_ffn_in['sw3'], 'L1_ffn_sw2': _L1_ffn_in['sw2']}

def reference(x, ctx_1024, L0_attn_ln1_w, L0_attn_ln1_b, L0_attn_ln2_w, L0_attn_ln2_b, L0_attn_att_tmk, L0_attn_att_tmv, L0_attn_att_tmr, L0_attn_time_decay, L0_attn_time_first, L0_attn_Wk, L0_attn_Wv, L0_attn_Wr, L0_attn_Wo, L0_attn_ffn_tmk, L0_attn_ffn_tmr, L0_attn_Wkey, L0_attn_Wrec, L0_attn_Wval, L0_xattn_Wq, L0_xattn_bq, L0_xattn_Wk, L0_xattn_bk, L0_xattn_Wv, L0_xattn_bv, L0_xattn_Wo, L0_xattn_bo, L0_ffn_rhs, L1_attn_W_in, L1_attn_b_in, L1_attn_W_xp, L1_attn_b_xp, L1_attn_W_dt, L1_attn_b_dt, L1_attn_W_out, L1_attn_b_out, L1_attn_A_log, L1_attn_D, L1_xattn_Wq, L1_xattn_bq, L1_xattn_Wk, L1_xattn_bk, L1_xattn_Wv, L1_xattn_bv, L1_xattn_We, L1_xattn_be, L1_xattn_Wo, L1_xattn_bo, L1_ffn_router_w, L1_ffn_expert_bias, L1_ffn_w1, L1_ffn_w3, L1_ffn_w2, L1_ffn_sw1, L1_ffn_sw3, L1_ffn_sw2):
    import jax
    import jax.numpy as jnp

    def _L0_attn_ref(x, ln1_w, ln1_b, ln2_w, ln2_b, att_tmk, att_tmv, att_tmr, time_decay, time_first, Wk, Wv, Wr, Wo, ffn_tmk, ffn_tmr, Wkey, Wrec, Wval):
        import jax, jax.numpy as jnp
        import numpy as np
        import math
        B, T, C = (8, 512, 256)
        DIM_ATT, DIM_FFN = (256, 1024)
        N_LAYER, LAYER_ID = (12, 1)
        EPS = 1e-05

        def layer_norm(x, w, b):
            mu = jnp.mean(x, axis=-1, keepdims=True)
            var = jnp.mean(jnp.square(x - mu), axis=-1, keepdims=True)
            return (x - mu) * jax.lax.rsqrt(var + EPS) * w + b

        def time_shift(x):
            return jnp.pad(x, ((0, 0), (1, 0), (0, 0)))[:, :-1, :]

        def wkv(time_decay, time_first, k, v):
            w = -jnp.exp(time_decay)
            u = time_first

            def step(carry, kv_t):
                aa, bb, pp = carry
                kt, vt = kv_t
                ww = u + kt
                qq = jnp.maximum(pp, ww)
                e1 = jnp.exp(pp - qq)
                e2 = jnp.exp(ww - qq)
                y = (e1 * aa + e2 * vt) / (e1 * bb + e2)
                ww2 = pp + w
                qq2 = jnp.maximum(ww2, kt)
                e1b = jnp.exp(ww2 - qq2)
                e2b = jnp.exp(kt - qq2)
                return ((e1b * aa + e2b * vt, e1b * bb + e2b, qq2), y)
            init = (jnp.zeros_like(k[:, 0]), jnp.zeros_like(k[:, 0]), jnp.full_like(k[:, 0], -1e+38))
            kT = jnp.swapaxes(k, 0, 1)
            vT = jnp.swapaxes(v, 0, 1)
            _, yT = jax.lax.scan(step, init, (kT, vT))
            return jnp.swapaxes(yT, 0, 1)
        h = layer_norm(x, ln1_w, ln1_b)
        hh = time_shift(h)
        xk = h * att_tmk + hh * (1 - att_tmk)
        xv = h * att_tmv + hh * (1 - att_tmv)
        xr = h * att_tmr + hh * (1 - att_tmr)
        k = xk @ Wk.T
        v = xv @ Wv.T
        sr = jax.nn.sigmoid(xr @ Wr.T)
        rwkv = sr * wkv(time_decay, time_first, k, v)
        x = x + rwkv @ Wo.T
        h = layer_norm(x, ln2_w, ln2_b)
        hh = time_shift(h)
        xk = h * ffn_tmk + hh * (1 - ffn_tmk)
        xr = h * ffn_tmr + hh * (1 - ffn_tmr)
        kk = jnp.square(jax.nn.relu(xk @ Wkey.T))
        kv = kk @ Wval.T
        x = x + jax.nn.sigmoid(xr @ Wrec.T) * kv
        return x

    def _L0_xattn_ref(query, key, value, Wq, bq, Wk, bk, Wv, bv, Wo, bo):
        import jax, jax.numpy as jnp
        import numpy as np
        import math
        H = 16
        D_MODEL = 256
        D_K = D_MODEL // H

        def _split_heads(x):
            b, s, _ = x.shape
            return x.reshape(b, s, H, D_K).transpose(0, 2, 1, 3)
        q = _split_heads(query @ Wq.T + bq)
        k = _split_heads(key @ Wk.T + bk)
        v = _split_heads(value @ Wv.T + bv)
        scores = jnp.einsum('bhqd,bhkd->bhqk', q, k) / math.sqrt(D_K)
        attn = jax.nn.softmax(scores, axis=-1)
        ctx = jnp.einsum('bhqk,bhkd->bhqd', attn, v)
        b, h, s, d = ctx.shape
        ctx = ctx.transpose(0, 2, 1, 3).reshape(b, s, h * d)
        return ctx @ Wo.T + bo

    def _L0_ffn_ref(lhs, rhs):
        import jax, jax.numpy as jnp
        import numpy as np
        INT8_MAX = 127.0

        def _absmax_scale(x, axes):
            amax = jnp.max(jnp.abs(x), axis=axes, keepdims=True)
            return jnp.maximum(amax, 1e-12) / INT8_MAX
        lhs_scale = _absmax_scale(lhs, (2,))
        rhs_scale = _absmax_scale(rhs, (0,))
        q_lhs = jnp.clip(jnp.round(lhs / lhs_scale), -INT8_MAX, INT8_MAX).astype(jnp.int8)
        q_rhs = jnp.clip(jnp.round(rhs / rhs_scale), -INT8_MAX, INT8_MAX).astype(jnp.int8)
        acc = jax.lax.dot_general(q_lhs, q_rhs, (((2,), (0,)), ((), ())), preferred_element_type=jnp.int32)
        return acc.astype(jnp.float32) * lhs_scale * rhs_scale

    def _L1_attn_ref(x, W_in, b_in, W_xp, b_xp, W_dt, b_dt, W_out, b_out, A_log, D):
        import jax, jax.numpy as jnp
        import numpy as np
        BATCH, SEQ, D_MODEL = (2, 1024, 256)
        D_STATE, EXPAND = (64, 2)
        D_INNER = D_MODEL * EXPAND

        def _silu(v):
            return v * jax.nn.sigmoid(v)
        xr = x @ W_in + b_in
        x_inner, res = jnp.split(xr, 2, axis=-1)
        x_inner = _silu(x_inner)
        A = -jnp.exp(A_log)
        delta = jax.nn.softplus(x_inner @ W_dt + b_dt)
        mean_delta = delta.mean(axis=-1)
        a = jnp.exp(A[None, None, :] * mean_delta[..., None])
        bx = x_inner @ W_xp + b_xp

        def step(state, inp):
            a_t, bx_t = inp
            state = a_t * state + bx_t
            return (state, state.sum(axis=-1))
        init = jnp.zeros((x.shape[0], D_STATE), dtype=x.dtype)
        _, s_sum = jax.lax.scan(step, init, (a.transpose(1, 0, 2), bx.transpose(1, 0, 2)))
        s_sum = s_sum.T
        y = s_sum[..., None] * x_inner
        y = y * _silu(res)
        out = y @ W_out + b_out + x * D
        return out

    def _L1_xattn_ref(query, key, value, Wq, bq, Wk, bk, Wv, bv, We, be, Wo, bo):
        import jax, jax.numpy as jnp
        import numpy as np
        D = 256
        H = 16
        E = 8
        DK = D // H
        B, S = (2, 512)
        b = query.shape[0]
        Q = (query @ Wq.T + bq).reshape(b, -1, H, DK).transpose(0, 2, 1, 3)
        K = (key @ Wk.T + bk).reshape(b, -1, H, DK).transpose(0, 2, 1, 3)
        V = (value @ Wv.T + bv).reshape(b, -1, H, DK).transpose(0, 2, 1, 3)
        scores = jnp.einsum('bhqd,bhkd->bhqk', Q, K) / jnp.sqrt(jnp.asarray(DK, Q.dtype))
        attn = jax.nn.softmax(scores, axis=-1)
        out = jnp.einsum('bhqk,bhkd->bhqd', attn, V)
        out = out.transpose(0, 2, 1, 3).reshape(b, -1, D)
        expert = jnp.einsum('bsd,eod->ebso', out, We) + be[:, None, None, :]
        expert = expert.mean(axis=0)
        return expert @ Wo.T + bo

    def _L1_ffn_ref(x, router_w, expert_bias, w1, w3, w2, sw1, sw3, sw2):
        import jax, jax.numpy as jnp
        import numpy as np
        B, S, DIM = (2, 512, 256)
        HID = 512
        E, NSH, TOPK = (8, 2, 2)

        def _ffn(x, w1, w2, w3):
            return jax.nn.silu(x @ w1.T) * (x @ w3.T) @ w2.T
        bs, sl, d = x.shape
        xf = x.reshape(-1, d)
        shared = jnp.zeros_like(xf)
        for i in range(sw1.shape[0]):
            shared = shared + _ffn(xf, sw1[i], sw2[i], sw3[i])
        logits = xf @ router_w.T + expert_bias
        rw, sel = jax.lax.top_k(logits, TOPK)
        rw = jax.nn.softmax(rw.astype(jnp.float32), axis=-1).astype(x.dtype)
        onehot = jax.nn.one_hot(sel, E, dtype=x.dtype)
        combine = jnp.einsum('tk,tke->te', rw, onehot)

        def body(acc, ew):
            e1, e3, e2, cw = ew
            acc = acc + cw[:, None] * _ffn(xf, e1, e2, e3)
            return (acc, None)
        out, _ = jax.lax.scan(body, jnp.zeros_like(xf), (w1, w3, w2, combine.T))
        out = out + shared
        return out.reshape(bs, sl, -1)
    x = x + _L0_attn_ref(_layernorm(x, axis=-1), L0_attn_ln1_w, L0_attn_ln1_b, L0_attn_ln2_w, L0_attn_ln2_b, L0_attn_att_tmk, L0_attn_att_tmv, L0_attn_att_tmr, L0_attn_time_decay, L0_attn_time_first, L0_attn_Wk, L0_attn_Wv, L0_attn_Wr, L0_attn_Wo, L0_attn_ffn_tmk, L0_attn_ffn_tmr, L0_attn_Wkey, L0_attn_Wrec, L0_attn_Wval)
    x = x + _L0_xattn_ref(_layernorm(x, axis=-1), ctx_1024, ctx_1024, L0_xattn_Wq, L0_xattn_bq, L0_xattn_Wk, L0_xattn_bk, L0_xattn_Wv, L0_xattn_bv, L0_xattn_Wo, L0_xattn_bo)
    x = x + _L0_ffn_ref(_layernorm(x, axis=-1), L0_ffn_rhs)
    x = x + _L1_attn_ref(_layernorm(x, axis=-1), L1_attn_W_in, L1_attn_b_in, L1_attn_W_xp, L1_attn_b_xp, L1_attn_W_dt, L1_attn_b_dt, L1_attn_W_out, L1_attn_b_out, L1_attn_A_log, L1_attn_D)
    x = x + _L1_xattn_ref(_layernorm(x, axis=-1), ctx_1024, ctx_1024, L1_xattn_Wq, L1_xattn_bq, L1_xattn_Wk, L1_xattn_bk, L1_xattn_Wv, L1_xattn_bv, L1_xattn_We, L1_xattn_be, L1_xattn_Wo, L1_xattn_bo)
    x = x + _L1_ffn_ref(_layernorm(x, axis=-1), L1_ffn_router_w, L1_ffn_expert_bias, L1_ffn_w1, L1_ffn_w3, L1_ffn_w2, L1_ffn_sw1, L1_ffn_sw3, L1_ffn_sw2)
    return x

_drawn_inputs = setup_inputs


def setup_inputs(seed=0):
    import zlib

    import numpy as np

    out = dict(_drawn_inputs(seed))
    spreads = {'L0_attn_ln1_w': (1.0, 0.2),
     'L0_attn_ln1_b': (0.0, 0.1),
     'L0_attn_ln2_w': (1.0, 0.2),
     'L0_attn_ln2_b': (0.0, 0.1),
     'L0_xattn_bq': (0.0, 0.534),
     'L0_xattn_bk': (0.0, 0.8),
     'L0_xattn_bv': (0.0, 0.1),
     'L0_xattn_bo': (0.0, 0.1),
     'L1_attn_b_in': (0.0, 0.8),
     'L1_attn_b_xp': (0.0, 0.8),
     'L1_attn_b_dt': (0.0, 0.8),
     'L1_attn_b_out': (0.0, 0.8),
     'L1_ffn_expert_bias': (0.0, 0.8)}
    factors = {'L0_attn_time_first': 3.003,
     'L1_attn_W_in': 8.0,
     'L1_attn_W_xp': 8.0,
     'L1_attn_W_dt': 8.0,
     'L1_attn_W_out': 8.0,
     'L1_attn_A_log': 8.0,
     'L1_xattn_Wq': 8.0,
     'L1_xattn_bq': 8.0,
     'L1_xattn_Wk': 8.0,
     'L1_xattn_bk': 8.0,
     'L1_xattn_Wv': 4.67,
     'L1_xattn_bv': 8.0,
     'L1_xattn_We': 4.656,
     'L1_xattn_be': 8.0,
     'L1_xattn_Wo': 4.557,
     'L1_xattn_bo': 8.0,
     'L1_ffn_router_w': 8.0,
     'L1_ffn_w1': 8.0,
     'L1_ffn_w3': 8.0,
     'L1_ffn_w2': 8.0,
     'L1_ffn_sw1': 8.0,
     'L1_ffn_sw3': 8.0,
     'L1_ffn_sw2': 8.0}
    for name, (base, spread) in spreads.items():
        noise = np.random.default_rng([zlib.crc32(name.encode()), seed]).standard_normal(out[name].shape)
        drawn = base * np.exp(spread * noise) if base else spread * noise
        out[name] = jnp.asarray(drawn.astype(out[name].dtype))
    for name, factor in factors.items():
        out[name] = (out[name] * factor).astype(out[name].dtype)
    return out
```

```python
from contextlib import ExitStack

import concourse.bass as bass
from concourse import mybir

F32 = mybir.dt.float32
FR = mybir.dt.float32r
BF = mybir.dt.bfloat16
ACT = mybir.ActivationFunctionType
ALU = mybir.AluOpType
AX = mybir.AxisListType

P = 128
NB = 8
S = 256
D = 256
C = D // P
J = S // P
H = 16
DK = D // H
HC = H // C
KEYS = 77
KP = 78
F1 = 1024
DI = 512
NS = 64
E = 8
NE = 10
HID = 512
EPS = 1e-5
ROUND = 12582912.0
LOWEST = -1e38

VECS = {}
for _name, _cols in (
    ("ln1_w", 2), ("ln1_b", 2), ("ln2_w", 2), ("ln2_b", 2), ("tmk", 2), ("tmv", 2), ("tmr", 2),
    ("decay", 2), ("first", 2), ("ftmk", 2), ("ftmr", 2), ("bq0", 2), ("bk0", 2), ("bq1", 2), ("bk1", 2),
    ("b_in", 8), ("b_dt", 2), ("b_xp", 1), ("a_log", 1),
):
    VECS[_name] = (sum(n for _, n in VECS.values()), _cols)
NVEC = sum(n for _, n in VECS.values())

ROWS = ("bv0", "bo0", "b_out", "skip", "bv1", "bo1")
NROW = len(ROWS) * D + E

GROUPS = [
    (0, [("wk", C, D), ("wv", C, D), ("wr", C, D), ("wo", C, D)]),
    (4096, [("wkey", C, F1)]),
    (8192, [("wval", F1 // P, D)]),
    (12288, [("wrec", C, D)]),
    (13312, [("aq0", C, D), ("ak0", C, D), ("av0", C, D), ("ao0", C, D)]),
    (0, [("aq1", C, D), ("ak1", C, D), ("av1", C, D)]),
    (4096, [("w_in", C, 2 * DI)]),
    (8192, [("w_dt", DI // P, D), ("w_out", DI // P, D)]),
    (12288, [("w_xp", DI // P, NS)]),
]
GSIZE = [sum(c * n for _, c, n in ws) for _, ws in GROUPS]
EARLY = 5
MSIZE = 2 * C * HID + HID // P * D
ACTS = 17408
FR_SIZE = 25600


def pipeline(eng, steps, start=2, n=NB, base=0):
    deepest = max(lag for _, lag in steps)
    assert start % 2 == 0 and n % 2 == 0 and start >= deepest
    for t in range(start):
        for step, lag in steps:
            if t >= lag:
                step(base + t - lag, (t - lag) % 2)
    if start < n:
        with eng.Fori(0, (n - start) // 2) as i:
            for u in range(2):
                for step, lag in steps:
                    step(i * 2 + (base + start + u - lag), (u - lag) % 2)
    for t in range(n, n + deepest):
        for step, lag in steps:
            if t - lag < n:
                step(base + t - lag, (t - lag) % 2)


def over_experts(eng, step):
    def expert(e, ue):
        step(e, ue, 0, 0)
        step(e, ue, 1, 1)
        with eng.Fori(0, NB // 2 - 1) as i:
            for u in range(2):
                step(e, ue, i * 2 + (2 + u), u)

    for e in range(2):
        expert(e, e)
    with eng.Fori(1, NE // 2 - 1) as p:
        for ue in range(2):
            expert(p * 2 + ue, ue)
    for e in range(NE - 2, NE):
        expert(e, e % 2)


def before(e, b):
    if isinstance(b, int) and b == 0:
        return e - 1, NB - 1
    return e, b - 1


def first_step(e, b):
    return isinstance(e, int) and isinstance(b, int) and e == 0 and b == 0


def released(eng, sem, b, depth=2, per=1):
    if isinstance(b, int) and b < depth:
        return
    eng.wait_ge(sem, (b - (depth - 1)) * per)


class Chain:

    def __init__(self, eng, sem, per, base=0):
        self.eng, self.sem, self.per, self.base = eng, sem, per, base

    def begin(self, b):
        self.b, self.n = b, 0

    def done(self, ins):
        ins.then_inc(self.sem, 1)
        self.n += 1

    def wait(self):
        self.eng.wait_ge(self.sem, self.b * self.per + (self.base + self.n))

    def end(self):
        assert self.n == self.per, (self.n, self.per)


def build(nc, a, out, last_stage=99):
    ctx = ExitStack()
    with ctx:
        def sb(name, shape, dt=F32):
            return ctx.enter_context(nc.sbuf_tensor(name, shape, dt))

        sems = {}

        def sem(name):
            if name not in sems:
                sems[name] = ctx.enter_context(nc.semaphore(name))
            return sems[name]

        PS = ctx.enter_context(nc.psum_tensor("PS", [P, 8, 512], F32))

        def bank(k, inner=256):
            return PS[:, k, :].rearrange("p (c n) -> p c n", n=inner)

        FRA = sb("FRA", [P, FR_SIZE], FR)
        X = sb("X", [P, NB, J, D])
        XN = sb("XN", [P, NB, J, D])
        RAW = sb("RAW", [P, 2, 2048])
        VEC = sb("VEC", [P, NVEC])
        ROW = sb("ROW", [P, NROW])
        IDENT = sb("IDENT", [P, P])
        MASK = sb("MASK", [P, HC])
        LOWER = sb("LOWER", [P, E, E])
        ONES = sb("ONES", [P, P])
        MEANW = sb("MEANW", [P, NS])
        HALF = sb("HALF", [P, J])
        ZERO = sb("ZERO", [P, 1])
        WD = sb("WD", [P, C])
        AD = sb("AD", [P, 1])
        CT = sb("CT", [P, C, NB, KP])
        ARENA_SIZE = 10500
        ARENA = sb("ARENA", [P, ARENA_SIZE])

        def cut(t, off, dims):
            n = 1
            for d in dims:
                n *= d
            v = t[:, off:off + n]
            if len(dims) == 2:
                v = v.rearrange("p (a b) -> p a b", b=dims[1])
            if len(dims) == 3:
                v = v.rearrange("p (a b c) -> p a b c", b=dims[1], c=dims[2])
            return v

        def split(off, *dims):
            n = 1
            for d in dims:
                n *= d
            return cut(FRA, off, dims), cut(FRA, off + n, dims)

        def plan(t, limit):
            at = [0]

            def take(*dims):
                n = 1
                for d in dims:
                    n *= d
                v = cut(t, at[0], dims)
                at[0] += n
                assert at[0] <= limit, at[0]
                return v
            return take

        def plan_split(first, limit=FR_SIZE):
            at = [first]

            def take(*dims):
                v = split(at[0], *dims)
                n = 2
                for d in dims:
                    n *= d
                at[0] += n
                assert at[0] <= limit, at[0]
                return v
            return take

        def vec(name, c=0, rows=P):
            at = VECS[name][0] + c
            return VEC[0:rows, at:at + 1]

        def row(name, rows=P):
            at = ROWS.index(name) * D
            return ROW[0:rows, at:at + D]

        W = {}
        for (first, ws), size in zip(GROUPS, GSIZE):
            at = 0
            for name, c, n in ws:
                W[name] = (cut(FRA, first + at, (c, n)), cut(FRA, first + size + at, (c, n)))
                at += c * n

        def f(ap):
            return ap.bitcast(F32)

        NORMS = ("n0", "n1", "n2", "n3", "n4", "n5", "n6", "n7")
        BN2 = [[sb(f"BN{n}{u}", [P, J, 6]) for u in range(2)] for n in range(2)]
        AG2 = [[sb(f"AG{n}{u}", [P, J, 2]) for u in range(2)] for n in range(2)]
        BN = {t: BN2[n % 2] for n, t in enumerate(NORMS)}
        AG = {t: AG2[n % 2] for n, t in enumerate(NORMS)}
        MEAN = {t: sb(f"MEAN_{t}", [P, NB, J]) for t in NORMS}
        VAR = {t: sb(f"VAR_{t}", [P, NB, J]) for t in NORMS}
        RSTD = {t: sb(f"RSTD_{t}", [P, NB, J]) for t in NORMS}

        def norm_sem(kind, tag):
            n = NORMS.index(tag)
            return sem(f"{kind}{n % 2}"), n // 2 * NB * {"stats": 5, "var": 1, "rstd": 1}[kind]

        def wait_norm(eng, kind, tag, count):
            which, base = norm_sem(kind, tag)
            eng.wait_ge(which, count + base)

        XN_FLAT = XN[:, :, :, :].rearrange("p b j d -> p (b j d)")

        take = plan(ARENA, ARENA_SIZE)
        XT = [take(J, D) for _ in range(2)]
        AFTER_XT = 2 * J * D
        HT = [take(C, S + 1) for _ in range(2)]
        DIFF = take(C, S)
        MIX = [take(C, S) for _ in range(3)]
        KB = [take(C, S) for _ in range(2)]
        UK = [take(C, S) for _ in range(2)]
        EZ = [take(C, S) for _ in range(2)]
        T1, T2, T3 = take(C, S), take(C, S), take(C, S)
        PPX, AA, BB = take(C, S + 1), take(C, S + 1), take(C, S + 1)
        take = plan_split(ACTS)
        MIXS = [[take(C, S) for _ in range(3)] for _ in range(2)]
        RW = [take(C, S) for _ in range(2)]


        take = plan(ARENA, ARENA_SIZE)
        take(2, J, D), take(2, C, S + 1), take(C, S), take(2, C, S)
        SIG = [take(J, D) for _ in range(2)]
        GATED = take(J, D)
        RELU = take(4, 2, S)
        KK = take(4, 2, S)
        take = plan_split(ACTS)
        FMIXS = [[take(C, S) for _ in range(2)] for _ in range(2)]
        KKS = take(4, 2, S)

        take = plan(ARENA, ARENA_SIZE)
        take(2, J, D)
        PROB = [take(H, KEYS) for _ in range(J)]
        PT = take(H, P)
        VAL = [take(H, DK + 1) for _ in range(2)]
        OUTN = take(D)
        PEAK, RDEN = [take(H) for _ in range(J)], [take(H) for _ in range(J)]
        take = plan_split(ACTS)
        XS = take(C, S)
        QS = [take(C, S) for _ in range(2)]
        CS = take(C, KP)
        KS = take(C, KP)
        KBD = take(C, HC, KP)
        OS = take(C, P)

        QW = sb("QW", [P, C, D], BF)
        QSCALE = sb("QSCALE", [P, D])
        take = plan(ARENA, ARENA_SIZE)
        take(2, J, D)
        XQ = [take(J, D) for _ in range(2)]
        QOUT = [take(J, D) for _ in range(2)]
        LS, LR = [take(J) for _ in range(2)], [take(J) for _ in range(2)]
        take(6500 - 3080)
        RHS_T, RHS_Q, QDIAG = take(C, D), take(C, D), take(C, P)
        QMAX = take(3, C)
        QX = [sb(f"QX{u}", [P, C, S], BF) for u in range(2)]

        take = plan(ARENA, ARENA_SIZE)
        take(2, J, D)
        XI = [take(DI // P, S) for _ in range(2)]
        RES = take(DI // P, S)
        GI = [take(DI // P, S) for _ in range(2)]
        YF = take(DI // P, S)
        DT, DTA, SP_ = take(C, S), take(C, S), take(C, S)
        BX, AT, ST = take(S), take(S), take(S)
        SKIP = take(J, D)
        take = plan_split(ACTS)
        FXS = take(C, S)
        XIS = take(DI // P, S)
        YS = take(DI // P, S)

        take = plan(ARENA, ARENA_SIZE)
        take(2, J, D)
        XF = [take(C, S) for _ in range(2)]
        SILU = take(HID // P, S)
        HB = [take(HID // P, S) for _ in range(2)]
        LOGIT, LOGIT_E, CHOSEN, RANK = take(NB * J, E), take(NB * J, E), take(NB * J, E), take(NB * J, E)
        TOP, SHARE = take(NB * J), take(NB * J)
        ABOVE, TIED = XN_FLAT[:, 0:1024].rearrange("p (t e o) -> p t e o", e=E, o=E), \
            XN_FLAT[:, 1024:2048].rearrange("p (t e o) -> p t e o", e=E, o=E)
        CW = take(NE, NB, J)
        RW8 = cut(ARENA, 7000 + MSIZE, (C, E))
        MRAW = cut(ARENA, 7000, (MSIZE,))
        MW = []
        for at in (4096, 10240):
            hi, lo = FRA[:, at:at + MSIZE], FRA[:, at + MSIZE:at + 2 * MSIZE]
            MW.append({
                "all": (hi, lo),
                "w1": tuple(t[:, 0:C * HID].rearrange("p (c n) -> p c n", n=HID) for t in (hi, lo)),
                "w3": tuple(t[:, C * HID:2 * C * HID].rearrange("p (c n) -> p c n", n=HID) for t in (hi, lo)),
                "w2": tuple(t[:, 2 * C * HID:MSIZE].rearrange("p (c n) -> p c n", n=D) for t in (hi, lo)),
            })
        XFS = tuple(FRA[:, 16384 + n * C * NB * S:16384 + (n + 1) * C * NB * S].rearrange("p (c b n) -> p c b n", c=C, b=NB)
                    for n in range(2))
        HS = [split(2048 * u, HID // P, S) for u in range(2)]

        WE = XN[:, :, :, :].rearrange("p b j d -> p (b j d)").rearrange("p (c e d) -> p c e d", c=C, e=E)
        WO2 = RAW[:, 0, 0:C * D].rearrange("p (c n) -> p c n", n=D)
        BE = RAW[:, 0, 1024:1024 + C * E].rearrange("p (c e) -> p c e", e=E)
        BSUM = RAW[:, 0, 1100:1100 + C]
        BWIDE = RAW[:, 0, 1200:1200 + C * P].rearrange("p (c n) -> p c n", n=P)
        FOLD = RAW[:, 0, 1500:1500 + C * D].rearrange("p (c n) -> p c n", n=D)
        W["ao1"] = (cut(FRA, 3072, (C, D)), cut(FRA, 3584, (C, D)))

        block = ctx.enter_context(nc.Block())

        LAST_DONE = "d0_done"

        KEY = PS[:, 6, 0:C * KP].rearrange("p (c n) -> p c n", n=KP)
        VALP = PS[:, 6, 160:160 + D]
        PV = PS[:, 7, 0:H * (DK + 1)].rearrange("p (h n) -> p h n", n=DK + 1)

        def mm3(pe, out, lhs, rhs, first, last):
            pe.matmul(out, lhs[0], rhs[0], start=first, stop=False)
            pe.matmul(out, lhs[0], rhs[1], start=False, stop=False)
            return pe.matmul(out, lhs[1], rhs[0], start=False, stop=last)

        def at_(pair, *idx):
            return pair[0][idx], pair[1][idx]

        def cols(m):
            return slice(m * P, (m + 1) * P)

        def feature_major(pe, out, w, x, ms, kc=C):
            for i, m in enumerate(ms):
                for k in range(kc):
                    last = mm3(pe, out[:, i, :], at_(w, slice(None), k, cols(m)), at_(x, slice(None), k, slice(None)),
                               k == 0, k == kc - 1)
            return last

        def token_major(pe, out, w, x, kc=C, js=range(J)):
            for i, j in enumerate(js):
                for k in range(kc):
                    last = mm3(pe, out[:, i, :], at_(x, slice(None), k, cols(j)), at_(w, slice(None), k, slice(None)),
                               k == 0, k == kc - 1)
            return last

        @block.sync
        def _(sp):
            sp.dma_start(X[:, :, :, :], a["x"]).then_inc(sem("x_loaded"), 16)
            sp.dma_start(VEC[:, :], a["vec"]).then_inc(sem("const_loaded"), 16)
            sp.dma_start(ROW[:, :], a["row"].partition_broadcast(P)).then_inc(sem("const_loaded"), 16)
            sp.dma_start(IDENT[:, :], a["ident"]).then_inc(sem("const_loaded"), 16)
            sp.dma_start(MASK[:, :], a["mask"]).then_inc(sem("const_loaded"), 16)
            sp.dma_start(LOWER[:, :, :], a["lower"].partition_broadcast(P)).then_inc(sem("const_loaded"), 16)
            sp.dma_start(CT[:, :, :, :], a["ctx"]).then_inc(sem("ctx_loaded"), 16)
            for g in range(EARLY):
                if g >= 2:
                    sp.wait_ge(sem("w_lo"), g - 1)
                sp.dma_start(RAW[:, g % 2, 0:GSIZE[g]], a[f"g{g}"]).then_inc(sem(f"w_loaded{g % 2}"), 16)
            sp.wait_ge(sem("c_done"), NB)
            sp.dma_start(RHS_T, a["rhs_t"]).then_inc(sem("rhs_loaded"), 16)
            sp.dma_start(XN[:, :, :, :], a["we"]).then_inc(sem("we_loaded"), 16)
            for g in range(EARLY, len(GROUPS)):
                sp.wait_ge(sem("w_lo"), g - 1)
                sp.dma_start(RAW[:, g % 2, 0:GSIZE[g]], a[f"g{g}"]).then_inc(sem(f"w_loaded{g % 2}"), 16)
            sp.wait_ge(sem("w_lo"), len(GROUPS))
            sp.dma_start(WO2, a["wo2"]).then_inc(sem("we_loaded"), 16)
            sp.dma_start(BE, a["be"]).then_inc(sem("we_loaded"), 16)
            sp.wait_ge(sem("f_added"), NB)
            sp.dma_start(RW8, a["router"]).then_inc(sem("router_loaded"), 16)
            sp.dma_start(MRAW, a["moe"][0]).then_inc(sem("m_loaded"), 16)
            with sp.Fori(1, NE) as e:
                sp.wait_ge(sem("m_w_lo"), e)
                sp.dma_start(MRAW, a["moe"][bass.ds(e, 1), :, :].rearrange("a p n -> (a p) n")).then_inc(sem("m_loaded"), 16)
            sp.wait_ge(sem("m_acc"), 2 * J + NE * NB * J)
            sp.dma_start(out, X[:, :, :, :]).then_inc(sem("out_stored"), 16)
            sp.wait_ge(sem("out_stored"), 16)

        @block.gpsimd
        def _(pool):
            pool.memset(HALF[:, :], -0.5).then_inc(sem("pool_const"), 1)
            pool.memset(ONES[:, :], 1.0).then_inc(sem("pool_const"), 1)
            pool.memset(MEANW[:, :], 1.0 / D).then_inc(sem("pool_const"), 1)
            for t in (HT[0], HT[1], AA, BB):
                pool.memset(t[:, :, 0:1], 0.0).then_inc(sem("pool_const"), 1)
            pool.memset(PPX[:, :, 0:1], LOWEST).then_inc(sem("pool_const"), 1)
            pool.wait_ge(sem("pool_const"), 8)

            def rstd(tag, base=0):
                def step(turn, u):
                    b = turn - base
                    wait_norm(pool, "var", tag, b + 1)
                    pool.tensor_tensor(RSTD[tag][:, b, :], VAR[tag][:, b, :], HALF[:, :],
                                       ALU.pow).then_inc(norm_sem("rstd", tag)[0], 1)
                return step

            def weights_lo(g):
                first, size = GROUPS[g][0], GSIZE[g]
                pool.wait_ge(sem("w_hi"), g + 1)
                pool.tensor_tensor(FRA[:, first + size:first + 2 * size], RAW[:, g % 2, 0:size],
                                   f(FRA[:, first:first + size]), ALU.subtract).then_inc(sem("w_lo"), 1)

            pipeline(pool, [(rstd("n0"), 0), (rstd("n1"), 1)])
            for g in range(EARLY):
                weights_lo(g)
            pipeline(pool, [(rstd("n2"), 0)])

            def c_residual(b, u):
                pool.wait_ge(sem("b_done"), b + 1)
                pool.tensor_tensor(X[:, b, :, :], X[:, b, :, :], XN[:, b, :, :], ALU.add).then_inc(sem("c_residual"), 1)

            def c_square(b, u):
                for q in range(4):
                    pool.wait_ge(sem("c_relu"), b * 4 + (q + 1))
                    released(pool, sem("c_kk"), b, depth=1, per=4)
                    pool.tensor_tensor(KK[:, q], RELU[:, q], RELU[:, q], ALU.mult).then_inc(sem("c_square"), 1)

            pipeline(pool, [(c_residual, 0), (c_square, 0), (rstd("n3"), 1)])

            def attention(k, tag):
                s, base = "d_", NB * k

                def bias(b, u):
                    pool.wait_ge(sem(s + "xt"), b + 1)
                    pool.tensor_tensor(X[:, b - base, :, :], X[:, b - base, :, :],
                                       row(f"bo{k}").unsqueeze(1).broadcast_to([P, J, D]), ALU.add).then_inc(sem(s + "bias"), 1)

                def spread(b, u):
                    pool.wait_ge(sem(s + "k_lo"), (b + 1) * 2)
                    released(pool, sem(s + "score"), b, depth=1, per=J)
                    for part in range(2):
                        for c in range(C):
                            ins = pool.tensor_tensor(
                                KBD[part][:, c], f(KS[part][:, c:c + 1, :]).broadcast_to([P, HC, KP]),
                                MASK[:, :].unsqueeze(2).broadcast_to([P, HC, KP]), ALU.mult)
                            ins.then_inc(sem(s + "spread"), 1)

                pipeline(pool, [(bias, 0), (spread, 0), (rstd(tag, base), 2)], base=base)

            pool.wait_ge(sem("const_loaded"), 80)
            attention(0, "n4")

            for g in range(EARLY, len(GROUPS)):
                weights_lo(g)

            pipeline(pool, [(rstd("n5"), 0)])

            pool.wait_ge(sem("we_loaded"), 48)
            for n, e in enumerate(range(1, E)):
                if n:
                    pool.wait_ge(sem("we_sum"), n)
                pool.tensor_tensor(WE[:, :, 0, :], WE[:, :, 0, :], WE[:, :, e, :], ALU.add).then_inc(sem("we_sum"), 1)

            def f_gate(b, u):
                pool.wait_ge(sem("f_silu"), (b + 1) * 8)
                released(pool, sem("f_y"), b)
                pool.tensor_tensor(GI[u], XI[u], RES, ALU.mult).then_inc(sem("f_gate"), 1)

            def f_skip(b, u):
                pool.wait_ge(sem("f_xt"), b + 1)
                released(pool, sem("f_skipped"), b, depth=1)
                for j in range(J):
                    pool.tensor_tensor(SKIP[:, j, :], XT[u][:, j, :], row("skip"), ALU.mult).then_inc(sem("f_skip"), 1)
                pool.wait_ge(sem("f_skip"), b * 4 + 2)
                for j in range(J):
                    pool.tensor_tensor(SKIP[:, j, :], SKIP[:, j, :], row("b_out"), ALU.add).then_inc(sem("f_skip"), 1)
                pool.wait_ge(sem("f_skip"), b * 4 + 4)
                pool.tensor_tensor(X[:, b, :, :], X[:, b, :, :], SKIP, ALU.add).then_inc(sem("f_skipped"), 1)

            pipeline(pool, [(f_skip, 0), (f_gate, 0), (rstd("n6"), 1)])

            attention(1, "n7")

            for e in range(2):
                pool.wait_ge(sem("m_w_hi"), e + 1)
                pool.tensor_tensor(MW[e]["all"][1], MRAW, f(MW[e]["all"][0]), ALU.subtract).then_inc(sem("m_w_lo"), 1)
            with pool.Fori(1, NE // 2) as p:
                for ue in range(2):
                    pool.wait_ge(sem("m_w_hi"), p * 2 + (ue + 1))
                    pool.tensor_tensor(MW[ue]["all"][1], MRAW, f(MW[ue]["all"][0]), ALU.subtract).then_inc(sem("m_w_lo"), 1)

        @block.scalar
        def _(act):
            act.wait_ge(sem("const_loaded"), 80)
            act.activation(WD[:, :], VEC[:, VECS["decay"][0]:VECS["decay"][0] + C], ACT.Exp).then_inc(sem("decay_exp"), 1)

            def weights_hi(g):
                first, size = GROUPS[g][0], GSIZE[g]
                act.wait_ge(sem(f"w_loaded{g % 2}"), 16 * (g // 2 + 1))
                act.activation(FRA[:, first:first + size], RAW[:, g % 2, 0:size], ACT.Copy).then_inc(sem("w_hi"), 1)

            for g in range(EARLY):
                weights_hi(g)
            act.wait_ge(sem("pool_const"), 8)

            def h_t(b, u):
                act.wait_ge(sem("b_t"), b + 1)
                released(act, sem("b_mixed"), b, per=3)
                for c in range(C):
                    ins = act.activation(HT[u][:, c, 1:S + 1], bank(6)[:, c, :], ACT.Identity,
                                         bias=vec("ln1_b", c), scale=vec("ln1_w", c))
                    ins.then_inc(sem("b_ht"), 1)

            def mix_hi(b, u):
                for m in range(3):
                    act.wait_ge(sem("b_mixed"), b * 3 + (m + 1))
                    act.activation(MIXS[u][m][0], MIX[m], ACT.Copy).then_inc(sem("b_mix_hi"), 1)

            def kvr(b, u):
                act.wait_ge(sem("b_kvr"), b * 3 + 1)
                act.activation(KB[u], bank(u), ACT.Copy).then_inc(sem("b_k"), 1)
                for c in range(C):
                    act.activation(UK[u][:, c, :], bank(u)[:, c, :], ACT.Identity,
                                   bias=vec("first", c)).then_inc(sem("b_k"), 1)
                act.wait_ge(sem("b_kvr"), b * 3 + 3)
                act.activation(EZ[u], bank(4 + u), ACT.Exp, scale=-1.0).then_inc(sem("b_k"), 1)

            def wkv_exp(b, u):
                act.wait_ge(sem("b_e_state"), b + 1)
                act.activation(T3, T3, ACT.Exp).then_inc(sem("b_exp"), 1)
                act.activation(KB[u], KB[u], ACT.Exp).then_inc(sem("b_exp"), 1)
                act.wait_ge(sem("b_e_out"), b + 1)
                act.activation(T2, T2, ACT.Exp).then_inc(sem("b_exp"), 1)
                act.activation(UK[u], UK[u], ACT.Exp).then_inc(sem("b_exp"), 1)
                act.wait_ge(sem("b_y"), b + 1)
                act.activation(RW[u][0], T3, ACT.Copy).then_inc(sem("b_y_hi"), 1)

            pipeline(act, [(h_t, 0), (wkv_exp, 1), (mix_hi, 0), (kvr, 0)])

            def c_h(b, u):
                act.wait_ge(sem("c_t"), b + 1)
                released(act, sem("c_mixed"), b, per=2)
                for c in range(C):
                    act.activation(HT[u][:, c, 1:S + 1], bank(6)[:, c, :], ACT.Identity,
                                   bias=vec("ln2_b", c), scale=vec("ln2_w", c)).then_inc(sem("c_ht"), 1)

            def c_mix_hi(b, u):
                for m in range(2):
                    act.wait_ge(sem("c_mixed"), b * 2 + (m + 1))
                    act.activation(FMIXS[u][m][0], MIX[m], ACT.Copy).then_inc(sem("c_mix_hi"), 1)

            def c_gate(b, u):
                act.wait_ge(sem("c_rec"), b + 1)
                released(act, sem("c_gated"), b)
                act.activation(SIG[u], bank(5), ACT.Sigmoid).then_inc(sem("c_sig"), 1)

            def c_relu(b, u):
                for q in range(4):
                    act.wait_ge(sem("c_key"), b * 4 + (q + 1))
                    released(act, sem("c_square"), b, depth=1, per=4)
                    act.activation(RELU[:, q], bank(q), ACT.Relu).then_inc(sem("c_relu"), 1)
                for q in range(4):
                    act.wait_ge(sem("c_relu"), b * 4 + (q + 1))
                    released(act, sem("c_val"), b, depth=1)
                    act.activation(KKS[0][:, q], RELU[:, q], ACT.Square).then_inc(sem("c_kk_hi"), 1)

            pipeline(act, [(c_h, 0), (c_mix_hi, 0), (c_relu, 0), (c_gate, 0)])

            def attention(k):
                s, base = "d_", NB * k

                def x_hi(b, u):
                    act.wait_ge(sem(s + "t"), b + 1)
                    released(act, sem(s + "q"), b, depth=1)
                    act.activation(XS[0], bank(6), ACT.Copy).then_inc(sem(s + "x_hi"), 1)

                def ctx_hi(b, u):
                    released(act, sem(s + "kv"), b, depth=1)
                    act.activation(CS[0], CT[:, :, b - base, :], ACT.Copy).then_inc(sem(s + "ctx_hi"), 1)

                def q_hi(b, u):
                    act.wait_ge(sem(s + "q"), b + 1)
                    for c in range(C):
                        act.activation(QS[u][0][:, c, :], bank(6)[:, c, :], ACT.Identity,
                                       bias=vec(f"bq{k}", c)).then_inc(sem(s + "q_hi"), 1)

                def k_hi(b, u):
                    act.wait_ge(sem(s + "kv"), b + 1)
                    released(act, sem(s + "spread"), b, depth=1, per=4)
                    for c in range(C):
                        act.activation(KS[0][:, c, :], KEY[:, c, :], ACT.Identity,
                                       bias=vec(f"bk{k}", c)).then_inc(sem(s + "k_hi"), 1)

                def exps(j):
                    def step(b, u):
                        act.wait_ge(sem(s + "centred"), b * J + (j + 1))
                        act.activation(PROB[j], PROB[j], ACT.Exp, scale=DK ** -0.5).then_inc(sem(s + "exp"), 1)
                    return step

                def pt(j, half):
                    def step(b, u):
                        for r in (2 * half, 2 * half + 1):
                            act.wait_ge(sem(s + "pt"), (b * J + j) * 4 + (r + 1))
                            act.activation(PT[0:KEYS, 4 * r:4 * r + 4, :], bank(4 + r % 2, P)[0:KEYS],
                                           ACT.Copy).then_inc(sem(s + "pt_read"), 1)
                    return step

                def o_hi(j):
                    def step(b, u):
                        act.wait_ge(sem(s + "ot"), b * J + (j + 1))
                        act.activation(OS[0], bank(7, P)[:, 0:2, :], ACT.Copy).then_inc(sem(s + "o_hi"), 1)
                    return step

                pipeline(act, [(o_hi(0), 2), (pt(1, 0), 2), (exps(0), 1), (ctx_hi, 0), (x_hi, 0), (pt(1, 1), 2), (q_hi, 0),
                               (k_hi, 0), (o_hi(1), 2), (pt(0, 0), 1), (exps(1), 1), (pt(0, 1), 1)], base=base)

            act.wait_ge(sem("ctx_loaded"), 16)
            attention(0)

            for g in range(EARLY, len(GROUPS)):
                weights_hi(g)

            act.wait_ge(sem("rhs_t"), 1)
            act.activation(QW[:, :, :], bank(4), ACT.Copy).then_inc(sem("qw"), 1)
            act.wait_ge(sem("rhs_b"), 1)
            act.activation(QSCALE[:, :], PS[:, 5, 0:D], ACT.Copy).then_inc(sem("qw"), 1)

            def e_q(b, u):
                act.wait_ge(sem("e_t"), b + 1)
                released(act, sem("e_prod"), b)
                act.activation(QX[u][:, :, :], bank(6 + u), ACT.Copy).then_inc(sem("e_qx"), 1)

            pipeline(act, [(e_q, 0)])

            act.wait_ge(sem("fold"), 1)
            act.activation(FOLD, bank(0), ACT.Copy, scale=1.0 / E).then_inc(sem("folded"), 1)
            act.wait_ge(sem("folded"), 1)
            act.activation(W["ao1"][0], FOLD, ACT.Copy).then_inc(sem("folded"), 1)

            act.wait_ge(sem("const_loaded"), 80)
            act.activation(AD[0:NS, :], vec("a_log", rows=NS), ACT.Exp).then_inc(sem("a_exp"), 1)

            def f_x_hi(b, u):
                act.wait_ge(sem("f_t"), b + 1)
                released(act, sem("f_in"), b, depth=1, per=4)
                act.activation(FXS[0], bank(6), ACT.Copy).then_inc(sem("f_x_hi"), 1)

            def f_dt(b, u):
                act.wait_ge(sem("f_dt"), b + 1)
                for c in range(C):
                    act.activation(DT[:, c, :], bank(4)[:, c, :], ACT.Identity, bias=vec("b_dt", c)).then_inc(sem("f_dt_read"), 1)
                    act.activation(DTA[:, c, :], bank(4)[:, c, :], ACT.Abs, bias=vec("b_dt", c)).then_inc(sem("f_dt_read"), 1)
                act.wait_ge(sem("f_xp"), b + 1)
                act.activation(BX[0:NS, :], PS[0:NS, 5, 0:S], ACT.Identity, bias=vec("b_xp", rows=NS)).then_inc(sem("f_bx"), 1)
                act.wait_ge(sem("f_dt_read"), (b + 1) * 4)
                act.activation(DTA, DTA, ACT.Exp, scale=-1.0).then_inc(sem("f_exp"), 1)
                act.wait_ge(sem("f_exp"), b + 1)
                act.activation(DTA, DTA, ACT.Ln, bias=1.0).then_inc(sem("f_ln"), 1)
                act.wait_ge(sem("f_mean"), b + 1)
                act.activation(AT[0:NS, :], PS[0:NS, 5, S:2 * S], ACT.Exp, scale=AD[0:NS, :]).then_inc(sem("f_decay"), 1)

            def f_silu(b, u):
                for q in range(4):
                    act.wait_ge(sem("f_in"), b * 4 + (q + 1))
                    if q == 2:
                        released(act, sem("f_gate"), b, depth=1)
                    for c in range(C):
                        m = 2 * q + c
                        dst = XI[u][:, m, :] if m < 4 else RES[:, m - 4, :]
                        act.activation(dst, bank(q)[:, c, :], ACT.Silu, bias=vec("b_in", m)).then_inc(sem("f_silu"), 1)
                act.wait_ge(sem("f_silu"), b * 8 + 4)
                released(act, sem("f_xp"), b, depth=1)
                act.activation(XIS[0], XI[u], ACT.Copy).then_inc(sem("f_xi_hi"), 1)

            def f_y_hi(b, u):
                act.wait_ge(sem("f_y"), b + 1)
                released(act, sem("f_out"), b, depth=1)
                act.activation(YS[0], YF, ACT.Copy).then_inc(sem("f_y_hi"), 1)

            act.wait_ge(sem("a"), 1)
            pipeline(act, [(f_x_hi, 0), (f_dt, 1), (f_silu, 0), (f_y_hi, 1)])

            act.wait_ge(sem("f_out"), NB)
            attention(1)

            act.sem_inc(sem("m_h_hi"), 2)

            def m_x_hi(b, u):
                act.wait_ge(sem("m_t"), b + 1)
                released(act, sem("m_logit"), b)
                act.activation(XF[u], bank(6 + u), ACT.Copy).then_inc(sem("m_xf"), 1)
                act.activation(XFS[0][:, :, b, :], bank(6 + u), ACT.Copy).then_inc(sem("m_x_hi"), 1)

            def m_weights_hi(e, ue):
                act.wait_ge(sem("m_loaded"), (e + 1) * 16)
                if not (isinstance(e, int) and e < 2):
                    act.wait_ge(sem("m_y"), (e - 1) * NB + 2)
                act.activation(MW[ue]["all"][0], MRAW, ACT.Copy).then_inc(sem("m_w_hi"), 1)

            pipeline(act, [(m_x_hi, 0)])
            m_weights_hi(0, 0)
            act.wait_ge(sem("m_centred"), 1)
            act.activation(LOGIT_E, LOGIT, ACT.Exp).then_inc(sem("m_exp"), 1)

            def m_step(e, ue, b, u):
                n = e * NB + b
                for m in range(HID // P):
                    act.wait_ge(sem("m_hid"), n * 4 + (m + 1))
                    act.activation(SILU[:, m, :], bank(m)[:, 0, :], ACT.Silu).then_inc(sem("m_silu"), 1)
                act.wait_ge(sem("m_h"), n * 4 + 12)
                act.wait_ge(sem("m_y"), n + 1)
                act.activation(HS[u][0], HB[u], ACT.Copy).then_inc(sem("m_h_hi"), 1)
                if isinstance(b, int) and b == 1 and not (isinstance(e, int) and e == NE - 1):
                    m_weights_hi(e + 1, 1 - ue)

            over_experts(act, m_step)


        @block.tensor
        def _(pe):
            def transposes(tag, read, per, k=6):
                def step(b, u):
                    pe.wait_ge(sem(f"{tag}_xt"), b + 1)
                    released(pe, sem(read), b, depth=1, per=per)
                    for c in range(C):
                        for j in range(J):
                            ins = pe.transpose(bank(k)[:, c, cols(j)], XT[u][:, j, cols(c)], IDENT[:, :])
                    ins.then_inc(sem(f"{tag}_t"), 1)
                return step

            def b_project(b, u):
                released(pe, sem("b_y"), b)
                for m, name in enumerate(("wk", "wv", "wr")):
                    pe.wait_ge(sem("b_mix_lo"), b * 3 + (m + 1))
                    feature_major(pe, bank(2 * m + u), W[name], MIXS[u][m], range(C)).then_inc(sem("b_kvr"), 1)

            def b_out(b, u):
                pe.wait_ge(sem("b_y_lo"), b + 1)
                released(pe, sem("b_done"), b, depth=1)
                token_major(pe, bank(7), W["wo"], RW[u]).then_inc(sem("b_o"), 1)

            pe.wait_ge(sem("const_loaded"), 80)
            pe.wait_ge(sem("w_lo"), 1)
            pipeline(pe, [(transposes("b", "b_ht", 2), 0), (b_out, 1), (b_project, 0)])

            def c_values(b, u):
                pe.wait_ge(sem("c_kk"), (b + 1) * 4)
                released(pe, sem("c_gated"), b, depth=1)
                token_major(pe, bank(4), W["wval"], (KKS[0].rearrange("p q m n -> p (q m) n"),
                                                     KKS[1].rearrange("p q m n -> p (q m) n")),
                            kc=F1 // P).then_inc(sem("c_val"), 1)

            def c_keys(b, u):
                pe.wait_ge(sem("c_mix_lo"), b * 2 + 1)
                for q in range(4):
                    released(pe, sem("c_relu"), b, depth=1, per=4)
                    feature_major(pe, bank(q), W["wkey"], FMIXS[u][0], (2 * q, 2 * q + 1)).then_inc(sem("c_key"), 1)
                pe.wait_ge(sem("c_mix_lo"), b * 2 + 2)
                released(pe, sem("c_sig"), b, depth=1)
                token_major(pe, bank(5), W["wrec"], FMIXS[u][1]).then_inc(sem("c_rec"), 1)

            pe.wait_ge(sem("w_lo"), 4)
            pe.wait_ge(sem("b_done"), NB)
            pipeline(pe, [(transposes("c", "c_ht", 2), 0), (c_values, 1), (c_keys, 0)])

            def attention(k):
                s, base = "d_", NB * k
                wq, wk, wv, wo = (W[f"a{m}{k}"] for m in "qkvo")

                def t(b, u):
                    pe.wait_ge(sem(s + "xt"), b + 1)
                    released(pe, sem(s + "v"), b, depth=1)
                    for c in range(C):
                        for j in range(J):
                            ins = pe.transpose(bank(6)[:, c, cols(j)], XT[u][:, j, cols(c)], IDENT[:, :])
                    ins.then_inc(sem(s + "t"), 1)

                def q(b, u):
                    pe.wait_ge(sem(s + "x_lo"), b + 1)
                    feature_major(pe, bank(6), wq, XS, range(C)).then_inc(sem(s + "q"), 1)

                def kv(b, u):
                    pe.wait_ge(sem(s + "ctx_lo"), b + 1)
                    pe.wait_ge(sem(s + "q_lo"), (b + 1) * 2)
                    feature_major(pe, KEY, wk, CS, range(C))
                    for c in range(C):
                        ins = mm3(pe, VALP[0:KP, :], at_(CS, slice(None), c, slice(None)), at_(wv, slice(None), c, slice(None)),
                                  c == 0, c == C - 1)
                    ins.then_inc(sem(s + "kv"), 1)

                def scores(j):
                    def step(b, u):
                        pe.wait_ge(sem(s + "q_lo"), (b + 1) * 2)
                        pe.wait_ge(sem(s + "spread"), (b + 1) * 4)
                        if j:
                            pe.wait_ge(sem(s + "centred"), b * J + j)
                        else:
                            released(pe, sem(s + "centred"), b, depth=1, per=J)
                        for c in range(C):
                            for g in range(2):
                                heads = (slice(None), c, slice(4 * g, 4 * g + 4), slice(None))
                                ins = mm3(pe, PS[:, 2 * c + g, 0:4 * KP].rearrange("p (h n) -> p h n", n=KP),
                                          at_(QS[u], slice(None), c, cols(j)), at_(KBD, *heads), True, True)
                        ins.then_inc(sem(s + "score"), 1)
                    return step

                def pt(j, half):
                    def step(b, u):
                        pe.wait_ge(sem(s + "exp"), b * J + (j + 1))
                        for r in (2 * half, 2 * half + 1):
                            if not (isinstance(b, int) and b == 0 and j == 0 and r < 2):
                                pe.wait_ge(sem(s + "pt_read"), b * J * 4 + (j * 4 + r - 1))
                            for h in range(4):
                                ins = pe.transpose(PS[0:KEYS, 4 + r % 2, cols(h)], PROB[j][:, 4 * r + h, :], IDENT[:, :])
                            ins.then_inc(sem(s + "pt"), 1)
                    return step

                def weigh(j):
                    def step(b, u):
                        pe.wait_ge(sem(s + "pt_read"), (b * J + j) * 4 + 4)
                        pe.wait_ge(sem(s + "v"), b + 1)
                        if j:
                            pe.wait_ge(sem(s + "added"), b * J + j)
                        else:
                            released(pe, sem(s + "added"), b, depth=1, per=J)
                        for h in range(H):
                            ins = pe.matmul(PV[:, h, :], PT[0:KEYS, h, :], VAL[u][0:KEYS, h, :], start=True, stop=True)
                        ins.then_inc(sem(s + "pv"), 1)
                    return step

                def ot(j):
                    def step(b, u):
                        pe.wait_ge(sem(s + "o"), b * J + (j + 1))
                        for c in range(C):
                            ins = pe.transpose(bank(7, P)[:, c, :], OUTN[:, cols(c)], IDENT[:, :])
                        ins.then_inc(sem(s + "ot"), 1)
                    return step

                def project(j):
                    def step(b, u):
                        pe.wait_ge(sem(s + "o_lo"), b * J + (j + 1))
                        for c in range(C):
                            ins = mm3(pe, bank(7)[:, 1, :], at_(OS, slice(None), c, slice(None)),
                                      at_(wo, slice(None), c, slice(None)), c == 0, c == C - 1)
                        ins.then_inc(sem(s + "proj"), 1)
                    return step

                pipeline(pe, [(scores(0), 1), (ot(0), 2), (pt(1, 0), 2), (project(0), 2), (t, 0), (pt(1, 1), 2), (q, 0),
                              (weigh(1), 2),
                              (scores(1), 1), (kv, 0), (ot(1), 2), (pt(0, 0), 1), (project(1), 2), (pt(0, 1), 1),
                              (weigh(0), 1)], base=base)

            pe.wait_ge(sem("w_lo"), EARLY)
            attention(0)

            pe.wait_ge(sem("rhs_q"), 1)
            pe.wait_ge(sem("d_added"), NB * J)
            for c in range(C):
                for n in range(C):
                    ins = pe.transpose(bank(4)[:, c, cols(n)], RHS_Q[:, n, cols(c)], IDENT[:, :])
            ins.then_inc(sem("rhs_t"), 1)
            pe.wait_ge(sem("rhs_diag"), 1)
            for n in range(C):
                ins = pe.matmul(PS[:, 5, cols(n)], ONES[:, :], QDIAG[:, n, :], start=True, stop=True)
            ins.then_inc(sem("rhs_b"), 1)

            def e_t(b, u):
                pe.wait_ge(sem("e_xt"), b + 1)
                released(pe, sem("e_qx"), b)
                for c in range(C):
                    for j in range(J):
                        ins = pe.transpose(bank(6 + u)[:, c, cols(j)], XQ[u][:, j, cols(c)], IDENT[:, :])
                ins.then_inc(sem("e_t"), 1)

            def e_prod(b, u):
                pe.wait_ge(sem("e_qx"), b + 1)
                released(pe, sem("e_scaled"), b, per=J)
                for j in range(J):
                    for c in range(C):
                        ins = pe.matmul(bank(4 + u)[:, j, :], QX[u][:, c, cols(j)], QW[:, c, :], start=c == 0, stop=c == C - 1)
                ins.then_inc(sem("e_prod"), 1)

            pe.wait_ge(sem("qw"), 2)
            pipeline(pe, [(e_t, 0), (e_prod, 1)])

            pe.wait_ge(sem("we_sum"), E - 1)
            for m in range(C):
                for c in range(C):
                    ins = pe.matmul(bank(0)[:, m, :], WE[:, c, 0, cols(m)], WO2[:, c, :], start=c == 0, stop=c == C - 1)
            ins.then_inc(sem("fold"), 1)
            pe.wait_ge(sem("be_wide"), 1)
            for c in range(C):
                ins = pe.matmul(PS[:, 1, 0:D], BWIDE[:, c, :], WO2[:, c, :], start=c == 0, stop=c == C - 1)
            ins.then_inc(sem("fold"), 1)

            def f_in(b, u):
                pe.wait_ge(sem("f_x_lo"), b + 1)
                for q in range(4):
                    released(pe, sem("f_silu"), b, depth=1, per=8)
                    feature_major(pe, bank(q), W["w_in"], FXS, (2 * q, 2 * q + 1)).then_inc(sem("f_in"), 1)

            def f_dt(b, u):
                pe.wait_ge(sem("f_xi_lo"), b + 1)
                released(pe, sem("f_dt_read"), b, depth=1, per=4)
                feature_major(pe, bank(4), W["w_dt"], XIS, range(C), kc=DI // P).then_inc(sem("f_dt"), 1)
                released(pe, sem("f_decay"), b, depth=1)
                for k in range(DI // P):
                    ins = mm3(pe, PS[0:NS, 5, 0:S], at_(W["w_xp"], slice(None), k, slice(None)),
                              at_(XIS, slice(None), k, slice(None)), k == 0, k == DI // P - 1)
                ins.then_inc(sem("f_xp"), 1)

            def f_mean(b, u):
                pe.wait_ge(sem("f_sp"), b + 1)
                pe.wait_ge(sem("f_bx"), b + 1)
                for c in range(C):
                    ins = pe.matmul(PS[0:NS, 5, S:2 * S], MEANW[:, :], SP_[:, c, :], start=c == 0, stop=c == C - 1)
                ins.then_inc(sem("f_mean"), 1)

            def f_sum(b, u):
                pe.wait_ge(sem("f_states"), b + 1)
                released(pe, sem("f_added"), b, depth=1)
                pe.matmul(PS[:, 7, 0:S], ONES[0:NS, :], ST[0:NS, :], start=True, stop=True).then_inc(sem("f_sum"), 1)

            def f_out(b, u):
                pe.wait_ge(sem("f_y_lo"), b + 1)
                token_major(pe, bank(7), W["w_out"], YS, kc=DI // P).then_inc(sem("f_out"), 1)

            pe.wait_ge(sem("w_lo"), len(GROUPS))
            pe.wait_ge(sem("folded"), 3)
            pe.wait_ge(sem("e_added"), NB)
            pipeline(pe, [(transposes("f", "f_x_lo", 1), 0), (f_dt, 1), (f_in, 0), (f_mean, 1), (f_sum, 1), (f_out, 1)])

            attention(1)

            pe.sem_inc(sem("m_y"), 2)

            def m_t(b, u):
                pe.wait_ge(sem("m_xt"), b + 1)
                released(pe, sem("m_x_lo"), b)
                for c in range(C):
                    for j in range(J):
                        ins = pe.transpose(bank(6 + u)[:, c, cols(j)], XT[u][:, j, cols(c)], IDENT[:, :])
                ins.then_inc(sem("m_t"), 1)

            def m_logit(b, u):
                pe.wait_ge(sem("m_xf"), b + 1)
                released(pe, sem("m_logit_read"), b)
                for j in range(J):
                    for c in range(C):
                        ins = pe.matmul(PS[:, 4 + u, j * E:(j + 1) * E], XF[u][:, c, cols(j)], RW8[:, c, :],
                                        start=c == 0, stop=c == C - 1)
                ins.then_inc(sem("m_logit"), 1)

            pe.wait_ge(sem("router_loaded"), 16)
            pipeline(pe, [(m_t, 0), (m_logit, 1)])
            pe.wait_ge(sem("m_x_lo"), NB)
            pe.wait_ge(sem("m_logit_read"), NB)

            def m_out(e, ue, b, u):
                n = e * NB + b
                pe.wait_ge(sem("m_h_lo"), n + 1)
                pe.wait_ge(sem("m_acc"), (n + 1) * J)
                token_major(pe, bank(4 + u), MW[ue]["w2"], HS[u], kc=HID // P).then_inc(sem("m_y"), 1)

            def m_step(e, ue, b, u):
                n = e * NB + b
                if isinstance(b, int) and b == 0:
                    pe.wait_ge(sem("m_w_lo"), e + 1)
                x = (XFS[0][:, :, b, :], XFS[1][:, :, b, :])
                for m in range(HID // P):
                    pe.wait_ge(sem("m_h"), n * 4 + (m + 5))
                    for half, w in enumerate(("w1", "w3")):
                        ins = feature_major(pe, bank(m)[:, half:half + 1, :], MW[ue][w], x, (m,))
                    ins.then_inc(sem("m_hid"), 1)
                if not first_step(e, b):
                    e0, b0 = before(e, b)
                    m_out(e0, 1 - ue if isinstance(b, int) and b == 0 else ue, b0, 1 - u)

            over_experts(pe, m_step)
            m_out(NE - 1, 1, NB - 1, 1)

        @block.vector
        def _(v):
            def own_wait():
                v.sem_inc(sem("turns"), 1)

            def stats(tag, src):
                chain = Chain(v, norm_sem("stats", tag)[0], 5, norm_sem("stats", tag)[1])

                def step(b, u):
                    chain.begin(b)
                    own_wait()
                    for j in range(J):
                        chain.done(v.bn_stats(BN[tag][u][:, j, :], src[:, b, j, :]))
                    chain.wait()
                    own_wait()
                    for j in range(J):
                        chain.done(v.bn_aggr(AG[tag][u][:, j, :], BN[tag][u][:, j, :]))
                    chain.wait()
                    chain.done(v.tensor_copy(MEAN[tag][:, b, :], AG[tag][u][:, :, 0]))
                    v.tensor_scalar(VAR[tag][:, b, :], AG[tag][u][:, :, 1], EPS, None,
                                    ALU.add).then_inc(norm_sem("var", tag)[0], 1)
                    chain.end()
                return step

            def normalise(tag, dst, src, b, done):
                wait_norm(v, "stats", tag, (b + 1) * 5)
                wait_norm(v, "rstd", tag, b + 1)
                for j in range(J):
                    ins = v.tensor_scalar(dst[:, j, :], src[:, b, j, :], MEAN[tag][:, b, j:j + 1],
                                          RSTD[tag][:, b, j:j + 1], ALU.subtract, ALU.mult)
                    ins.then_inc(done, 1)

            v.wait_ge(sem("x_loaded"), 16)
            stats_n1 = stats("n1", XN)

            def first_norm(b, u):
                wait_norm(v, "stats", "n0", (b + 1) * 5)
                wait_norm(v, "rstd", "n0", b + 1)
                for j in range(J):
                    v.tensor_scalar(XN[:, b, j, :], X[:, b, j, :], MEAN["n0"][:, b, j:j + 1],
                                    RSTD["n0"][:, b, j:j + 1], ALU.subtract, ALU.mult).then_inc(sem("xn"), 1)
                v.wait_ge(sem("xn"), (b + 1) * 2)
                stats_n1(b, u)

            pipeline(v, [(stats("n0", X), 0), (first_norm, 1)])

            v.wait_ge(sem("const_loaded"), 80)
            v.wait_ge(sem("pool_const"), 8)
            v.wait_ge(sem("decay_exp"), 1)
            v.tensor_scalar(WD[:, :], WD[:, :], -1.0, None, ALU.mult).then_inc(sem("decay"), 1)
            v.wait_ge(sem("decay"), 1)

            def norm(stage, tag, src, base=0):
                def step(turn, u):
                    released(v, sem(f"{stage}_t"), turn)
                    b = turn - base
                    wait_norm(v, "stats", tag, (b + 1) * 5)
                    wait_norm(v, "rstd", tag, b + 1)
                    for j in range(J):
                        ins = v.tensor_scalar(XT[u][:, j, :], src[:, b, j, :], MEAN[tag][:, b, j:j + 1],
                                              RSTD[tag][:, b, j:j + 1], ALU.subtract, ALU.mult)
                    ins.then_inc(sem(f"{stage}_xt"), 1)
                return step

            def b_mix(b, u):
                h, shifted = HT[u][:, :, 1:S + 1], HT[u][:, :, 0:S]
                v.wait_ge(sem("b_ht"), (b + 1) * 2)
                v.tensor_tensor(DIFF, h, shifted, ALU.subtract).then_inc(sem("b_diff"), 1)
                v.wait_ge(sem("b_diff"), b + 1)
                for m, tm in enumerate(("tmk", "tmv", "tmr")):
                    released(v, sem("b_mix_hi"), b, depth=1, per=3)
                    v.scalar_tensor_tensor(MIX[m][:, 0, :], DIFF[:, 0, :], vec(tm, 0), shifted[:, 0, :], ALU.mult, ALU.add)
                    v.scalar_tensor_tensor(MIX[m][:, 1, :], DIFF[:, 1, :], vec(tm, 1), shifted[:, 1, :],
                                           ALU.mult, ALU.add).then_inc(sem("b_mixed"), 1)
                for m in range(3):
                    v.wait_ge(sem("b_mix_hi"), b * 3 + (m + 1))
                    v.tensor_tensor(MIXS[u][m][1], MIX[m], f(MIXS[u][m][0]), ALU.subtract).then_inc(sem("b_mix_lo"), 1)

            chain_w = Chain(v, sem("b_wkv"), 18)

            def b_wkv(b, u):
                chain_w.begin(b)
                k, uk, ez, val = KB[u], UK[u], EZ[u], bank(2 + u)
                before, after = PPX[:, :, 0:S], PPX[:, :, 1:S + 1]
                v.wait_ge(sem("b_k"), (b + 1) * 4)
                for c in range(C):
                    chain_w.done(v.tensor_tensor_scan(PPX[:, c, 1:S + 1], WD[:, c:c + 1].broadcast_to([P, S]), k[:, c, :],
                                                      LOWEST, ALU.add, ALU.max))
                chain_w.wait()
                released(v, sem("b_y_hi"), b, depth=1)
                chain_w.done(v.tensor_tensor(T1, before, uk, ALU.max))
                for c in range(C):
                    chain_w.done(v.scalar_tensor_tensor(T3[:, c, :], before[:, c, :], WD[:, c:c + 1], after[:, c, :],
                                                        ALU.add, ALU.subtract))
                chain_w.wait()
                v.tensor_tensor(k, k, after, ALU.subtract).then_inc(sem("b_e_state"), 1)
                chain_w.done(v.tensor_tensor(T2, before, T1, ALU.subtract))
                v.tensor_tensor(uk, uk, T1, ALU.subtract).then_inc(sem("b_e_out"), 1)
                v.wait_ge(sem("b_exp"), b * 4 + 2)
                v.wait_ge(sem("b_kvr"), b * 3 + 2)
                chain_w.wait()
                v.wait_ge(sem("b_e_out"), b + 1)
                chain_w.done(v.tensor_tensor(T1, k, val, ALU.mult))
                for c in range(C):
                    chain_w.done(v.tensor_tensor_scan(BB[:, c, 1:S + 1], T3[:, c, :], k[:, c, :], 0.0, ALU.mult, ALU.add))
                chain_w.wait()
                for c in range(C):
                    chain_w.done(v.tensor_tensor_scan(AA[:, c, 1:S + 1], T3[:, c, :], T1[:, c, :], 0.0, ALU.mult, ALU.add))
                chain_w.wait()
                v.wait_ge(sem("b_exp"), b * 4 + 4)
                chain_w.done(v.tensor_tensor(T3, T2, AA[:, :, 0:S], ALU.mult))
                chain_w.done(v.tensor_tensor(T1, uk, val, ALU.mult))
                chain_w.done(v.tensor_tensor(T2, T2, BB[:, :, 0:S], ALU.mult))
                chain_w.wait()
                chain_w.done(v.tensor_tensor(T3, T3, T1, ALU.add))
                chain_w.done(v.tensor_tensor(T2, T2, uk, ALU.add))
                chain_w.wait()
                chain_w.done(v.scalar_tensor_tensor(T2, ez, 1.0, T2, ALU.add, ALU.mult))
                chain_w.wait()
                chain_w.done(v.reciprocal(T2, T2))
                chain_w.wait()
                v.tensor_tensor(T3, T3, T2, ALU.mult).then_inc(sem("b_y"), 1)
                v.wait_ge(sem("b_y_hi"), b + 1)
                v.tensor_tensor(RW[u][1], T3, f(RW[u][0]), ALU.subtract).then_inc(sem("b_y_lo"), 1)
                chain_w.end()

            def b_add(b, u):
                v.wait_ge(sem("b_o"), b + 1)
                v.tensor_tensor(XN[:, b, :, :], XN[:, b, :, :], bank(7), ALU.add).then_inc(sem("b_done"), 1)
                v.wait_ge(sem("b_done"), b + 1)
                stats_n2(b, u)

            stats_n2 = stats("n2", XN)
            pipeline(v, [(norm("b", "n1", XN), 0), (b_wkv, 1), (b_mix, 0), (b_add, 1)])

            stats_n3 = stats("n3", X)

            def c_mix(b, u):
                h, shifted = HT[u][:, :, 1:S + 1], HT[u][:, :, 0:S]
                v.wait_ge(sem("c_ht"), (b + 1) * 2)
                v.tensor_tensor(DIFF, h, shifted, ALU.subtract).then_inc(sem("c_diff"), 1)
                v.wait_ge(sem("c_diff"), b + 1)
                for m, tm in enumerate(("ftmk", "ftmr")):
                    released(v, sem("c_mix_hi"), b, depth=1, per=2)
                    v.scalar_tensor_tensor(MIX[m][:, 0, :], DIFF[:, 0, :], vec(tm, 0), shifted[:, 0, :], ALU.mult, ALU.add)
                    v.scalar_tensor_tensor(MIX[m][:, 1, :], DIFF[:, 1, :], vec(tm, 1), shifted[:, 1, :],
                                           ALU.mult, ALU.add).then_inc(sem("c_mixed"), 1)
                for m in range(2):
                    v.wait_ge(sem("c_mix_hi"), b * 2 + (m + 1))
                    v.tensor_tensor(FMIXS[u][m][1], MIX[m], f(FMIXS[u][m][0]), ALU.subtract).then_inc(sem("c_mix_lo"), 1)

            def c_kk(b, u):
                for q in range(4):
                    v.wait_ge(sem("c_square"), b * 4 + (q + 1))
                    v.wait_ge(sem("c_kk_hi"), b * 4 + (q + 1))
                    v.tensor_tensor(KKS[1][:, q], KK[:, q], f(KKS[0][:, q]), ALU.subtract).then_inc(sem("c_kk"), 1)

            def c_add(b, u):
                v.wait_ge(sem("c_sig"), b + 1)
                v.wait_ge(sem("c_val"), b + 1)
                v.tensor_tensor(GATED, SIG[u], bank(4), ALU.mult).then_inc(sem("c_gated"), 1)
                v.wait_ge(sem("c_gated"), b + 1)
                v.wait_ge(sem("c_residual"), b + 1)
                v.tensor_tensor(X[:, b, :, :], X[:, b, :, :], GATED, ALU.add).then_inc(sem("c_done"), 1)
                v.wait_ge(sem("c_done"), b + 1)
                stats_n3(b, u)

            pipeline(v, [(norm("c", "n2", XN), 0), (c_add, 1), (c_mix, 0), (c_kk, 0)])

            def attention(k, tag, next_tag):
                s, base = "d_", NB * k
                stats_next = stats(next_tag, X)

                def x_lo(b, u):
                    v.wait_ge(sem(s + "x_hi"), b + 1)
                    v.tensor_tensor(XS[1], bank(6), f(XS[0]), ALU.subtract).then_inc(sem(s + "x_lo"), 1)

                def ctx_lo(b, u):
                    v.wait_ge(sem(s + "ctx_hi"), b + 1)
                    v.tensor_tensor(CS[1], CT[:, :, b - base, :], f(CS[0]), ALU.subtract).then_inc(sem(s + "ctx_lo"), 1)

                def q_lo(b, u):
                    v.wait_ge(sem(s + "q_hi"), (b + 1) * 2)
                    for c in range(C):
                        v.scalar_tensor_tensor(QS[u][1][:, c, :], bank(6)[:, c, :], vec(f"bq{k}", c), f(QS[u][0][:, c, :]),
                                               ALU.add, ALU.subtract).then_inc(sem(s + "q_lo"), 1)

                def kv_read(b, u):
                    v.wait_ge(sem(s + "k_hi"), (b + 1) * 2)
                    for c in range(C):
                        v.scalar_tensor_tensor(KS[1][:, c, :], KEY[:, c, :], vec(f"bk{k}", c), f(KS[0][:, c, :]),
                                               ALU.add, ALU.subtract).then_inc(sem(s + "k_lo"), 1)
                    v.tensor_tensor(VAL[u][0:KEYS, :, 0:DK], VALP[0:KEYS, :].rearrange("p (h n) -> p h n", n=DK),
                                    row(f"bv{k}", KEYS).rearrange("p (h n) -> p h n", n=DK), ALU.add).then_inc(sem(s + "v"), 1)

                SC = PS[:, 0:4, 0:4 * KP].rearrange("p a (h n) -> p a h n", n=KP)[:, :, :, 0:KEYS]

                def peak(j):
                    def step(b, u):
                        v.wait_ge(sem(s + "score"), b * J + (j + 1))
                        v.tensor_reduce(PEAK[j].rearrange("p (a h) -> p a h", h=4), SC, AX.X, ALU.max).then_inc(sem(s + "peak"), 1)
                    return step

                def centre(j):
                    def step(b, u):
                        v.wait_ge(sem(s + "peak"), b * J + (j + 1))
                        v.tensor_tensor(PROB[j].rearrange("p (a h) n -> p a h n", h=4), SC,
                                        PEAK[j].rearrange("p (a h) -> p a h", h=4).unsqueeze(3).broadcast_to([P, 4, 4, KEYS]),
                                        ALU.subtract).then_inc(sem(s + "centred"), 1)
                    return step

                def out(j):
                    def step(b, u):
                        v.wait_ge(sem(s + "pv"), b * J + (j + 1))
                        v.reciprocal(RDEN[j].unsqueeze(2), PV[:, :, DK:DK + 1]).then_inc(sem(s + "rden"), 1)
                        v.wait_ge(sem(s + "rden"), b * J + (j + 1))
                        v.tensor_tensor(OUTN.rearrange("p (h n) -> p h n", n=DK), PV[:, :, 0:DK],
                                        RDEN[j].unsqueeze(2).broadcast_to([P, H, DK]), ALU.mult).then_inc(sem(s + "o"), 1)
                    return step

                def o_lo(j):
                    def step(b, u):
                        v.wait_ge(sem(s + "o_hi"), b * J + (j + 1))
                        v.tensor_tensor(OS[1], bank(7, P)[:, 0:2, :], f(OS[0]), ALU.subtract).then_inc(sem(s + "o_lo"), 1)
                    return step

                def add(j):
                    def step(b, u):
                        v.wait_ge(sem(s + "proj"), b * J + (j + 1))
                        v.wait_ge(sem(s + "bias"), b + 1)
                        v.tensor_tensor(X[:, b - base, j, :], X[:, b - base, j, :], bank(7)[:, 1, :], ALU.add).then_inc(sem(s + "added"), 1)
                        if j:
                            v.wait_ge(sem(s + "added"), (b + 1) * J)
                            stats_next(b - base, u)
                    return step

                for u in range(2):
                    v.memset(VAL[u][0:KEYS, :, DK:DK + 1], 1.0).then_inc(sem(s + "ones"), 1)
                v.wait_ge(sem(s + "ones"), 2 * (k + 1))
                pipeline(v, [(out(0), 2), (norm("d", tag, X, base), 0), (peak(0), 1), (o_lo(0), 2), (centre(0), 1), (add(0), 2),
                             (ctx_lo, 0), (x_lo, 0), (q_lo, 0),
                             (out(1), 2), (peak(1), 1), (kv_read, 0), (o_lo(1), 2), (centre(1), 1), (add(1), 2)], base=base)

            def prepare_rhs():
                chain = Chain(v, sem("rhs"), 7)
                chain.begin(0)
                v.wait_ge(sem("rhs_loaded"), 16)
                chain.done(v.tensor_reduce(QMAX[:, 0, :], RHS_T, AX.X, ALU.max, apply_absolute_value=True))
                chain.wait()
                chain.done(v.tensor_scalar(QMAX[:, 1, :], QMAX[:, 0, :], 1e-12, 1.0 / 127.0, ALU.max, ALU.mult))
                chain.wait()
                chain.done(v.reciprocal(QMAX[:, 2, :], QMAX[:, 1, :]))
                chain.wait()
                for n in range(C):
                    chain.done(v.tensor_scalar(RHS_Q[:, n, :], RHS_T[:, n, :], QMAX[:, 2, n:n + 1], ROUND, ALU.mult, ALU.add))
                chain.wait()
                chain.done(v.tensor_scalar(RHS_Q, RHS_Q, -ROUND, -127.0, ALU.add, ALU.max))
                chain.wait()
                v.tensor_scalar(RHS_Q, RHS_Q, 127.0, None, ALU.min).then_inc(sem("rhs_q"), 1)
                chain.done(v.tensor_scalar(QDIAG[:, 0, :], IDENT[:, :], QMAX[:, 1, 0:1], None, ALU.mult))
                v.tensor_scalar(QDIAG[:, 1, :], IDENT[:, :], QMAX[:, 1, 1:2], None, ALU.mult).then_inc(sem("rhs_diag"), 1)
                chain.end()

            attention(0, "n3", "n4")
            prepare_rhs()
            stats_n5 = stats("n5", X)
            chain_e = Chain(v, sem("e_chain"), 8)

            def e_norm(b, u):
                chain_e.begin(b)
                wait_norm(v, "stats", "n4", (b + 1) * 5)
                wait_norm(v, "rstd", "n4", b + 1)
                for j in range(J):
                    chain_e.done(v.tensor_scalar(XT[u][:, j, :], X[:, b, j, :], MEAN["n4"][:, b, j:j + 1],
                                                 RSTD["n4"][:, b, j:j + 1], ALU.subtract, ALU.mult))
                chain_e.wait()
                chain_e.done(v.tensor_reduce(LR[u], XT[u], AX.X, ALU.max, apply_absolute_value=True))
                chain_e.wait()
                chain_e.done(v.tensor_scalar(LS[u], LR[u], 1e-12, 1.0 / 127.0, ALU.max, ALU.mult))
                chain_e.wait()
                chain_e.done(v.reciprocal(LR[u], LS[u]))
                chain_e.wait()
                released(v, sem("e_t"), b)
                for j in range(J):
                    chain_e.done(v.tensor_scalar(XQ[u][:, j, :], XT[u][:, j, :], LR[u][:, j:j + 1], ROUND, ALU.mult, ALU.add))
                chain_e.wait()
                chain_e.done(v.tensor_scalar(XQ[u], XQ[u], -ROUND, -127.0, ALU.add, ALU.max))
                chain_e.wait()
                v.tensor_scalar(XQ[u], XQ[u], 127.0, None, ALU.min).then_inc(sem("e_xt"), 1)
                chain_e.end()

            def e_add(b, u):
                v.wait_ge(sem("e_prod"), b + 1)
                for j in range(J):
                    v.scalar_tensor_tensor(QOUT[u][:, j, :], bank(4 + u)[:, j, :], LS[u][:, j:j + 1], QSCALE[:, :],
                                           ALU.mult, ALU.mult).then_inc(sem("e_scaled"), 1)
                v.wait_ge(sem("e_scaled"), (b + 1) * J)
                v.tensor_tensor(X[:, b, :, :], X[:, b, :, :], QOUT[u], ALU.add).then_inc(sem("e_added"), 1)
                v.wait_ge(sem("e_added"), b + 1)
                stats_n5(b, u)

            v.wait_ge(sem("qw"), 2)
            v.wait_ge(sem("rhs_diag"), 1)
            v.wait_ge(sem("rhs"), 7)
            pipeline(v, [(e_norm, 0), (e_add, 1)])

            v.wait_ge(sem("we_loaded"), 48)
            v.tensor_reduce(BSUM, BE, AX.X, ALU.add).then_inc(sem("be"), 1)
            v.wait_ge(sem("be"), 1)
            for c in range(C):
                ins = v.tensor_scalar(BWIDE[:, c, :], ONES[:, :], BSUM[:, c:c + 1], 1.0 / E, ALU.mult, ALU.mult)
            ins.then_inc(sem("be_wide"), 1)
            v.wait_ge(sem("folded"), 2)
            v.tensor_tensor(W["ao1"][1], FOLD, f(W["ao1"][0]), ALU.subtract).then_inc(sem("folded"), 1)
            v.wait_ge(sem("fold"), 2)
            v.tensor_tensor(row("bo1"), row("bo1"), PS[:, 1, 0:D], ALU.add).then_inc(sem("bo1"), 1)

            v.wait_ge(sem("a_exp"), 1)
            v.tensor_scalar(AD[0:NS, :], AD[0:NS, :], -1.0, None, ALU.mult).then_inc(sem("a"), 1)
            stats_n6 = stats("n6", X)

            def f_x_lo(b, u):
                v.wait_ge(sem("f_x_hi"), b + 1)
                v.tensor_tensor(FXS[1], bank(6), f(FXS[0]), ALU.subtract).then_inc(sem("f_x_lo"), 1)

            def f_softplus(b, u):
                v.wait_ge(sem("f_ln"), b + 1)
                v.scalar_tensor_tensor(SP_, DT, 0.0, DTA, ALU.max, ALU.add).then_inc(sem("f_sp"), 1)

            def f_scan(b, u):
                v.wait_ge(sem("f_decay"), b + 1)
                v.wait_ge(sem("f_bx"), b + 1)
                v.tensor_tensor_scan(ST[0:NS, :], AT[0:NS, :], BX[0:NS, :], 0.0, ALU.mult, ALU.add).then_inc(sem("f_states"), 1)

            def f_xi_lo(b, u):
                v.wait_ge(sem("f_xi_hi"), b + 1)
                v.tensor_tensor(XIS[1], XI[u], f(XIS[0]), ALU.subtract).then_inc(sem("f_xi_lo"), 1)

            def f_y(b, u):
                v.wait_ge(sem("f_sum"), b + 1)
                v.wait_ge(sem("f_gate"), b + 1)
                v.tensor_tensor(YF, GI[u], PS[:, 7:8, 0:S].broadcast_to([P, DI // P, S]), ALU.mult).then_inc(sem("f_y"), 1)
                v.wait_ge(sem("f_y_hi"), b + 1)
                v.tensor_tensor(YS[1], YF, f(YS[0]), ALU.subtract).then_inc(sem("f_y_lo"), 1)

            def f_add(b, u):
                v.wait_ge(sem("f_skipped"), b + 1)
                v.wait_ge(sem("f_out"), b + 1)
                v.tensor_tensor(X[:, b, :, :], X[:, b, :, :], bank(7), ALU.add).then_inc(sem("f_added"), 1)
                v.wait_ge(sem("f_added"), b + 1)
                stats_n6(b, u)

            pipeline(v, [(norm("f", "n5", X), 0), (f_x_lo, 0), (f_softplus, 1), (f_scan, 1), (f_y, 1), (f_xi_lo, 0),
                         (f_add, 1)])

            attention(1, "n6", "n7")

            v.sem_inc(sem("m_h"), 8)
            v.sem_inc(sem("m_acc"), 2 * J)

            def m_x_lo(b, u):
                v.wait_ge(sem("m_x_hi"), b + 1)
                v.tensor_tensor(XFS[1][:, :, b, :], bank(6 + u), f(XFS[0][:, :, b, :]), ALU.subtract).then_inc(sem("m_x_lo"), 1)

            def m_logits(b, u):
                v.wait_ge(sem("m_logit"), b + 1)
                v.tensor_tensor(LOGIT.rearrange("p (b j) e -> p b j e", j=J)[:, b, :, :],
                                PS[:, 4 + u, 0:J * E].rearrange("p (j e) -> p j e", e=E),
                                ROW[:, NROW - E:NROW].unsqueeze(1).broadcast_to([P, J, E]), ALU.add).then_inc(sem("m_logit_read"), 1)

            pipeline(v, [(norm("m", "n7", X), 0), (m_logits, 1), (m_x_lo, 0)])

            T = NB * J
            mine = LOGIT.unsqueeze(3).broadcast_to([P, T, E, E])
            other = LOGIT.unsqueeze(2).broadcast_to([P, T, E, E])
            chain_r = Chain(v, sem("m_rank"), 10)
            chain_r.begin(0)
            v.wait_ge(sem("m_logit_read"), NB)
            chain_r.done(v.tensor_tensor(ABOVE, other, mine, ALU.is_gt))
            chain_r.done(v.tensor_tensor(TIED, other, mine, ALU.is_equal))
            chain_r.done(v.tensor_reduce(TOP, LOGIT, AX.X, ALU.max))
            chain_r.wait()
            chain_r.done(v.tensor_tensor(TIED, TIED, LOWER[:, :, :].unsqueeze(1).broadcast_to([P, T, E, E]), ALU.mult))
            v.tensor_tensor(LOGIT, LOGIT, TOP.unsqueeze(2).broadcast_to([P, T, E]), ALU.subtract).then_inc(sem("m_centred"), 1)
            chain_r.wait()
            chain_r.done(v.tensor_tensor(TIED, TIED, ABOVE, ALU.add))
            chain_r.wait()
            chain_r.done(v.tensor_reduce(RANK, TIED, AX.X, ALU.add))
            chain_r.wait()
            chain_r.done(v.tensor_scalar(CHOSEN, RANK, 1.5, None, ALU.is_lt))
            v.wait_ge(sem("m_exp"), 1)
            chain_r.wait()
            chain_r.done(v.tensor_tensor(CHOSEN, CHOSEN, LOGIT_E, ALU.mult))
            chain_r.wait()
            chain_r.done(v.tensor_reduce(SHARE, CHOSEN, AX.X, ALU.add))
            chain_r.wait()
            chain_r.done(v.reciprocal(SHARE, SHARE))
            chain_r.wait()
            chain_r.end()
            v.memset(CW[:, E:NE, :, :], 1.0).then_inc(sem("m_cw"), 1)
            v.tensor_tensor(CW[:, 0:E, :, :].rearrange("p e b j -> p (b j) e"), CHOSEN,
                            SHARE.unsqueeze(2).broadcast_to([P, T, E]), ALU.mult).then_inc(sem("m_cw"), 1)
            v.wait_ge(sem("m_cw"), 2)

            def m_add(e, b, u):
                n = e * NB + b
                v.wait_ge(sem("m_y"), n + 3)
                for j in range(J):
                    v.scalar_tensor_tensor(X[:, b, j, :], bank(4 + u)[:, j, :], CW[:, e, b, j:j + 1], X[:, b, j, :],
                                           ALU.mult, ALU.add).then_inc(sem("m_acc"), 1)

            def m_step(e, ue, b, u):
                n = e * NB + b
                for m in range(HID // P):
                    v.wait_ge(sem("m_silu"), n * 4 + (m + 1))
                    v.tensor_tensor(HB[u][:, m, :], SILU[:, m, :], bank(m)[:, 1, :], ALU.mult).then_inc(sem("m_h"), 1)
                v.wait_ge(sem("m_h_hi"), n + 3)
                v.tensor_tensor(HS[u][1], HB[u], f(HS[u][0]), ALU.subtract).then_inc(sem("m_h_lo"), 1)
                if not first_step(e, b):
                    e0, b0 = before(e, b)
                    m_add(e0, b0, 1 - u)

            over_experts(v, m_step)
            m_add(NE - 1, NB - 1, 1)


def arrange(inputs):
    import numpy as np

    g = {k: np.asarray(v) for k, v in inputs.items()}

    def kn(w):
        k, n = w.shape
        return w.reshape(k // P, P, n).transpose(1, 0, 2).reshape(P, -1)

    def lanes(w):
        return w.reshape(-1, P).T

    def lanes64(w):
        return np.concatenate([w.reshape(1, NS), w.reshape(1, NS)], axis=1).reshape(P, 1)

    mats = {
        "wk": g["L0_attn_Wk"].T, "wv": g["L0_attn_Wv"].T, "wr": g["L0_attn_Wr"].T, "wo": g["L0_attn_Wo"].T,
        "wkey": g["L0_attn_Wkey"].T, "wval": g["L0_attn_Wval"].T, "wrec": g["L0_attn_Wrec"].T,
        "w_in": g["L1_attn_W_in"], "w_dt": g["L1_attn_W_dt"], "w_out": g["L1_attn_W_out"], "w_xp": g["L1_attn_W_xp"],
    }
    for n in range(2):
        for s in "qkv":
            mats[f"a{s}{n}"] = g[f"L{n}_xattn_W{s}"].T
    mats["ao0"] = g["L0_xattn_Wo"].T
    vecs = {
        "ln1_w": "L0_attn_ln1_w", "ln1_b": "L0_attn_ln1_b", "ln2_w": "L0_attn_ln2_w", "ln2_b": "L0_attn_ln2_b",
        "tmk": "L0_attn_att_tmk", "tmv": "L0_attn_att_tmv", "tmr": "L0_attn_att_tmr",
        "decay": "L0_attn_time_decay", "first": "L0_attn_time_first", "ftmk": "L0_attn_ffn_tmk",
        "ftmr": "L0_attn_ffn_tmr", "bq0": "L0_xattn_bq", "bk0": "L0_xattn_bk", "bq1": "L1_xattn_bq",
        "bk1": "L1_xattn_bk", "b_in": "L1_attn_b_in", "b_dt": "L1_attn_b_dt",
    }
    cols = [lanes(g[vecs[n]].reshape(-1)) if n in vecs else lanes64(g["L1_attn_b_xp" if n == "b_xp" else "L1_attn_A_log"])
            for n in VECS]
    rows = [g["L0_xattn_bv"], g["L0_xattn_bo"], g["L1_attn_b_out"], g["L1_attn_D"], g["L1_xattn_bv"], g["L1_xattn_bo"],
            g["L1_ffn_expert_bias"]]
    r = {
        "x": g["x"].reshape(NB, J, P, D).transpose(2, 0, 1, 3),
        "vec": np.concatenate(cols, axis=1),
        "row": np.concatenate(rows),
        "ident": np.eye(P, dtype=np.float32),
        "mask": np.repeat(np.eye(HC, dtype=np.float32), DK, axis=0),
        "lower": np.tril(np.ones((E, E), np.float32), -1),
    }
    w1 = np.concatenate([g["L1_ffn_w1"], g["L1_ffn_sw1"]])
    w3 = np.concatenate([g["L1_ffn_w3"], g["L1_ffn_sw3"]])
    w2 = np.concatenate([g["L1_ffn_w2"], g["L1_ffn_sw2"]])
    r["moe"] = np.stack([np.concatenate([kn(w1[e].T), kn(w3[e].T), kn(w2[e].T)], axis=1) for e in range(NE)])
    r["router"] = g["L1_ffn_router_w"].T.reshape(C, P, E).transpose(1, 0, 2)
    r["rhs_t"] = g["L0_ffn_rhs"].T.reshape(C, P, D).transpose(1, 0, 2)
    r["we"] = g["L1_xattn_We"].reshape(E, C, P, D).transpose(2, 1, 0, 3).reshape(P, NB, J, D)
    r["wo2"] = g["L1_xattn_Wo"].T.reshape(C, P, D).transpose(1, 0, 2)
    r["be"] = g["L1_xattn_be"].reshape(E, C, P).transpose(2, 1, 0)
    context = np.zeros((P, C, NB, KP), np.float32)
    context[..., :KEYS] = g["ctx_1024"].reshape(NB, KEYS, C, P).transpose(3, 2, 0, 1)
    r["ctx"] = context
    for n, (_, ws) in enumerate(GROUPS):
        r[f"g{n}"] = np.concatenate([kn(mats[name]) for name, _, _ in ws], axis=1)
    return {k: np.ascontiguousarray(v) for k, v in r.items()}


def kernel(**inputs):
    import numpy as np
    import concourse.bacc as bacc
    from concourse.bass_utils import run_bass_kernel_spmd

    nc = bacc.Bacc("TRN2", target_bir_lowering=False, num_devices=1)
    arrays = arrange(inputs)
    used = {}
    for name, v in arrays.items():
        used[name] = nc.dram_tensor(f"in_{name}", v.shape, mybir.dt.from_np(v.dtype), kind="ExternalInput").ap()
    out = nc.dram_tensor("out_x", (P, NB, J, D), F32, kind="ExternalOutput").ap()
    build(nc, used, out)
    r = run_bass_kernel_spmd(nc, [{f"in_{k}": v for k, v in arrays.items()}], core_ids=[0])
    y = np.asarray(r.results[0]["out_x"])
    return y.reshape(P, NB, J, D).transpose(1, 2, 0, 3).reshape(NB, S, D)
```

```python
from contextlib import ExitStack

import concourse.bass as bass
from concourse import mybir

F32 = mybir.dt.float32
FR = mybir.dt.float32r
BF = mybir.dt.bfloat16
U32 = mybir.dt.uint32
ACT = mybir.ActivationFunctionType
ALU = mybir.AluOpType
AX = mybir.AxisListType

P = 128
NB = 8
S = 256
D = 256
C = D // P
J = S // P
H = 16
DK = D // H
HC = H // C
KEYS = 77
KP = 78
F1 = 1024
DI = 512
NS = 64
E = 8
NE = 10
HID = 512
EPS = 1e-5
ROUND = 12582912.0
LOWEST = -1e38

VECS = {}
for _name, _cols in (
    ("ln1_w", 2), ("ln1_b", 2), ("ln2_w", 2), ("ln2_b", 2), ("tmk", 2), ("tmv", 2), ("tmr", 2),
    ("decay", 2), ("first", 2), ("ftmk", 2), ("ftmr", 2), ("bq0", 2), ("bk0", 2), ("bq1", 2), ("bk1", 2),
    ("b_in", 8), ("b_dt", 2), ("b_xp", 1), ("a_log", 1),
):
    VECS[_name] = (sum(n for _, n in VECS.values()), _cols)
NVEC = sum(n for _, n in VECS.values())

ROWS = ("bv0", "bo0", "b_out", "skip", "bv1", "bo1")
NROW = len(ROWS) * D + E

GROUPS = [
    (0, [("wk", C, D), ("wv", C, D), ("wr", C, D), ("wo", C, D)]),
    (4096, [("wkey", C, F1)]),
    (8192, [("wval", F1 // P, D)]),
    (12288, [("wrec", C, D)]),
    (13312, [("aq0", C, D), ("ak0", C, D), ("av0", C, D), ("ao0", C, D)]),
    (0, [("aq1", C, D), ("ak1", C, D), ("av1", C, D)]),
    (4096, [("w_in", C, 2 * DI)]),
    (8192, [("w_dt", DI // P, D), ("w_out", DI // P, D)]),
    (12288, [("w_xp", DI // P, NS)]),
]
GSIZE = [sum(c * n for _, c, n in ws) for _, ws in GROUPS]
EARLY = 5
UP = 2 * C * HID
DOWN = HID // P * D
MSIZE = UP + DOWN
T = NB * J
TOPK = 2
TILE = S
NT = NB * S * TOPK // TILE + E - 1
SHARED0 = 0
TILES0 = NB
SHARED1 = NB + NT
LAST = NT + 1
ACTS = 17408
FR_SIZE = 25600


def pipeline(eng, steps, start=2, n=NB, base=0):
    deepest = max(lag for _, lag in steps)
    assert start % 2 == 0 and start >= deepest
    for t in range(start):
        for step, lag in steps:
            if t >= lag:
                step(base + t - lag, (t - lag) % 2)
    if start < n:
        with eng.Fori(0, (n - start) // 2) as i:
            for u in range(2):
                for step, lag in steps:
                    step(i * 2 + (base + start + u - lag), (u - lag) % 2)
    for t in range(start + (n - start) // 2 * 2, n + deepest):
        for step, lag in steps:
            if t - lag < n:
                step(base + t - lag, (t - lag) % 2)


def released(eng, sem, b, depth=2, per=1, base=0):
    if isinstance(b, int) and b < depth:
        return
    eng.wait_ge(sem, (b - (depth - 1)) * per + base)


class Chain:

    def __init__(self, eng, sem, per, base=0):
        self.eng, self.sem, self.per, self.base = eng, sem, per, base

    def begin(self, b):
        self.b, self.n = b, 0

    def done(self, ins):
        ins.then_inc(self.sem, 1)
        self.n += 1

    def wait(self):
        self.eng.wait_ge(self.sem, self.b * self.per + (self.base + self.n))

    def end(self):
        assert self.n == self.per, (self.n, self.per)


def build(nc, a, out, rows_in, rows_out):
    ctx = ExitStack()
    with ctx:
        def sb(name, shape, dt=F32):
            return ctx.enter_context(nc.sbuf_tensor(name, shape, dt))

        sems = {}
        GOES_ON = {
            "c_diff": ("b_diff", NB), "c_ht": ("b_ht", NB * C), "c_mixed": ("b_mixed", NB * 3),
            "c_mix_hi": ("b_mix_hi", NB * 3), "c_mix_lo": ("b_mix_lo", NB * 3),
            "rhs_diag": ("rhs_q", 1), "rhs_b": ("rhs_t", 1), "a": ("decay", 2), "a_exp": ("decay_exp", 1),
            "m_slot": ("xn", NB * J), "m_first": ("b_diff", 2 * NB), "be": ("decay", 1),
            "m_w_hi": ("w_hi", len(GROUPS)), "m_w_lo": ("w_lo", len(GROUPS)),
            "m_up0": ("w_loaded0", (len(GROUPS) + 1) // 2 * 16), "m_up1": ("w_loaded1", len(GROUPS) // 2 * 16),
        }
        for kind in ("xt", "t"):
            for stage, n in (("c", 1), ("d0", 2), ("e", 3), ("f", 4), ("d1", 4), ("m", 6)):
                GOES_ON[f"{stage}_{kind}"] = (f"b_{kind}", n * NB)

        def earlier(name):
            return GOES_ON[name][1] if name in GOES_ON else 0

        def sem(name):
            name = GOES_ON[name][0] if name in GOES_ON else name
            if name not in sems:
                sems[name] = ctx.enter_context(nc.semaphore(name))
            return sems[name]

        PS = ctx.enter_context(nc.psum_tensor("PS", [P, 8, 512], F32))

        def bank(k, inner=256):
            return PS[:, k, :].rearrange("p (c n) -> p c n", n=inner)

        FRA = sb("FRA", [P, FR_SIZE], FR)
        X = sb("X", [P, NB, J, D])
        XN = sb("XN", [P, NB, J, D])
        RAW = sb("RAW", [P, 2, 2048])
        VEC = sb("VEC", [P, NVEC])
        ROW = sb("ROW", [P, NROW])
        IDENT = sb("IDENT", [P, P])
        MASK = sb("MASK", [P, HC])
        LOWER = sb("LOWER", [P, E, E])
        ONES = sb("ONES", [P, P])
        MEANW = sb("MEANW", [P, NS])
        HALF = sb("HALF", [P, J])
        WD = sb("WD", [P, C])
        AD = sb("AD", [P, 1])
        CT = sb("CT", [P, C, NB, KP])
        ARENA_SIZE = 10500
        ARENA = sb("ARENA", [P, ARENA_SIZE])

        def cut(t, off, dims):
            n = 1
            for d in dims:
                n *= d
            v = t[:, off:off + n]
            if len(dims) == 2:
                v = v.rearrange("p (a b) -> p a b", b=dims[1])
            if len(dims) == 3:
                v = v.rearrange("p (a b c) -> p a b c", b=dims[1], c=dims[2])
            return v

        def split(off, *dims):
            n = 1
            for d in dims:
                n *= d
            return cut(FRA, off, dims), cut(FRA, off + n, dims)

        def plan(t, limit):
            at = [0]

            def take(*dims):
                n = 1
                for d in dims:
                    n *= d
                v = cut(t, at[0], dims)
                at[0] += n
                assert at[0] <= limit, at[0]
                return v
            return take

        def plan_split(first, limit=FR_SIZE):
            at = [first]

            def take(*dims):
                v = split(at[0], *dims)
                n = 2
                for d in dims:
                    n *= d
                at[0] += n
                assert at[0] <= limit, at[0]
                return v
            return take

        def vec(name, c=0, rows=P):
            at = VECS[name][0] + c
            return VEC[0:rows, at:at + 1]

        def row(name, rows=P):
            at = ROWS.index(name) * D
            return ROW[0:rows, at:at + D]

        W = {}
        for (first, ws), size in zip(GROUPS, GSIZE):
            at = 0
            for name, c, n in ws:
                W[name] = (cut(FRA, first + at, (c, n)), cut(FRA, first + size + at, (c, n)))
                at += c * n

        def f(ap):
            return ap.bitcast(F32)

        NORMS = ("n0", "n1", "n2", "n3", "n4", "n5", "n6", "n7")
        BN2 = [[sb(f"BN{n}{u}", [P, J, 6]) for u in range(2)] for n in range(2)]
        AG2 = [[sb(f"AG{n}{u}", [P, J, 2]) for u in range(2)] for n in range(2)]
        BN = {t: BN2[n % 2] for n, t in enumerate(NORMS)}
        AG = {t: AG2[n % 2] for n, t in enumerate(NORMS)}
        MEAN = {t: sb(f"MEAN_{t}", [P, NB, J]) for t in NORMS}
        VAR = {t: sb(f"VAR_{t}", [P, NB, J]) for t in NORMS}
        RSTD = {t: sb(f"RSTD_{t}", [P, NB, J]) for t in NORMS}

        def norm_sem(kind, tag):
            n = NORMS.index(tag)
            return sem(f"{kind}{n % 2}"), n // 2 * NB * {"stats": 5, "var": 1, "rstd": 1}[kind]

        def wait_norm(eng, kind, tag, count):
            which, base = norm_sem(kind, tag)
            eng.wait_ge(which, count + base)

        take = plan(ARENA, ARENA_SIZE)
        XT = [take(J, D) for _ in range(2)]
        HT = [take(C, S + 1) for _ in range(2)]
        DIFF = take(C, S)
        MIX = [take(C, S) for _ in range(3)]
        KB = [take(C, S) for _ in range(2)]
        UK = [take(C, S) for _ in range(2)]
        EZ = [take(C, S) for _ in range(2)]
        T1, T2, T3 = take(C, S), take(C, S), take(C, S)
        PPX, AA, BB = take(C, S + 1), take(C, S + 1), take(C, S + 1)
        SCRATCH = T1.rearrange("p c s -> p (c s)")
        BN_ALL = SCRATCH[:, 0:T * 6].rearrange("p (t n) -> p t n", n=6)
        AG_ALL = SCRATCH[:, T * 6:T * 8].rearrange("p (t n) -> p t n", n=2)
        take = plan_split(ACTS)
        MIXS = [[take(C, S) for _ in range(3)] for _ in range(2)]
        RW = [take(C, S) for _ in range(2)]


        take = plan(ARENA, ARENA_SIZE)
        take(2, J, D), take(2, C, S + 1), take(C, S), take(2, C, S)
        SIG = [take(J, D) for _ in range(2)]
        GATED = take(J, D)
        RELU = take(4, 2, S)
        KK = take(4, 2, S)
        take = plan_split(ACTS)
        FMIXS = [[take(C, S) for _ in range(2)] for _ in range(2)]
        KKS = take(4, 2, S)

        take = plan(ARENA, ARENA_SIZE)
        take(2, J, D)
        PROB = [take(H, KEYS) for _ in range(J)]
        PT = take(H, P)
        VAL = [take(H, DK + 1) for _ in range(2)]
        OUTN = take(D)
        PEAK, RDEN = [take(H) for _ in range(J)], [take(H) for _ in range(J)]
        take = plan_split(ACTS)
        XS = take(C, S)
        QS = [take(C, S) for _ in range(2)]
        CS = take(C, KP)
        KS = take(C, KP)
        KBD = take(C, HC, KP)
        OS = take(C, P)

        QW = sb("QW", [P, C, D], BF)
        QSCALE = sb("QSCALE", [P, D])
        take = plan(ARENA, ARENA_SIZE)
        take(2, J, D)
        XQ = [take(J, D) for _ in range(2)]
        QOUT = [take(J, D) for _ in range(2)]
        LS, LR = [take(J) for _ in range(2)], [take(J) for _ in range(2)]
        take(6500 - 3080)
        RHS_T, RHS_Q, QDIAG = take(C, D), take(C, D), take(C, P)
        QMAX = take(3, C)
        QX = [sb(f"QX{u}", [P, C, S], BF) for u in range(2)]

        take = plan(ARENA, ARENA_SIZE)
        take(2, J, D)
        XI = [take(DI // P, S) for _ in range(2)]
        RES = take(DI // P, S)
        GI = [take(DI // P, S) for _ in range(2)]
        YF = take(DI // P, S)
        DT, DTA, SP_ = take(C, S), take(C, S), take(C, S)
        BX = [take(S) for _ in range(2)]
        AT, ST = take(S), take(S)
        SKIP = take(J, D)
        take = plan_split(ACTS)
        FXS = take(C, S)
        XIS = take(DI // P, S)
        YS = take(DI // P, S)

        take = plan(ARENA, ARENA_SIZE)
        XG = [take(J, D) for _ in range(2)]
        XF = [take(C, S) for _ in range(2)]
        YT = [x.rearrange("p c s -> p (c s)").rearrange("p (j d) -> p j d", d=D) for x in XF]
        SILU = take(HID // P, S)
        HB = [take(HID // P, S) for _ in range(2)]
        LOGIT, LOGIT_E, RANK = take(T, E), take(T, E), take(T, E)
        IS = [take(T, E) for _ in range(TOPK)]
        PICKED = [take(T, E) for _ in range(TOPK)]
        TAKEN, SUMS, POS = take(E, T), take(E, T), take(E, T)
        TOP, SHARE = take(T), take(T)
        CW, SLOT = take(TOPK, T), take(TOPK, T)
        NTILES, UPTO, FIRST = take(E), take(E), take(E)
        BELOW, EXPERT = take(NT, E), take(NT)
        SLOTU = take(TOPK * T).bitcast(U32)
        EXPERTU = take(NT).bitcast(U32)[0:1]
        RAW_FLAT = RAW[:, :, :].rearrange("p a n -> p (a n)")
        ABOVE, TIED = RAW_FLAT[:, 0:1024].rearrange("p (t e o) -> p t e o", e=E, o=E), \
            RAW_FLAT[:, 1024:2048].rearrange("p (t e o) -> p t e o", e=E, o=E)
        MRAW = [cut(ARENA, 7000, (MSIZE,)), RAW_FLAT[:, 0:MSIZE]]
        EARLIER = cut(ARENA, 7000 + MSIZE, (P,))
        KEEP = cut(ARENA, 7000 + MSIZE + P, (E * T,))
        NUMBER = cut(ARENA, 7000 + MSIZE + P + E * T, (NT,))
        RW8 = cut(ARENA, 7000 + MSIZE + P + E * T + NT, (C, E))
        BACK = [XN[:, :, :, :].rearrange("p b j d -> p (b j) d"), RAW_FLAT.rearrange("p (t d) -> p t d", d=D)]
        MW = []
        for at in (4096, 10240):
            hi, lo = FRA[:, at:at + MSIZE], FRA[:, at + MSIZE:at + 2 * MSIZE]
            MW.append({
                "up": (hi[:, 0:UP], lo[:, 0:UP]),
                "down": (hi[:, UP:MSIZE], lo[:, UP:MSIZE]),
                "w1": tuple(t[:, 0:C * HID].rearrange("p (c n) -> p c n", n=HID) for t in (hi, lo)),
                "w3": tuple(t[:, C * HID:UP].rearrange("p (c n) -> p c n", n=HID) for t in (hi, lo)),
                "w2": tuple(t[:, UP:MSIZE].rearrange("p (c n) -> p c n", n=D) for t in (hi, lo)),
            })
        XFS = tuple(FRA[:, 16384 + n * C * NB * S:16384 + (n + 1) * C * NB * S].rearrange("p (c b n) -> p c b n", c=C, b=NB)
                    for n in range(2))
        XGS = split(24576, C, S)
        HS = [split(2048 * u, HID // P, S) for u in range(2)]

        WE = XN[:, :, :, :].rearrange("p b j d -> p (b j d)").rearrange("p (c e d) -> p c e d", c=C, e=E)
        WO2 = RAW[:, 0, 0:C * D].rearrange("p (c n) -> p c n", n=D)
        BE = RAW[:, 0, 1024:1024 + C * E].rearrange("p (c e) -> p c e", e=E)
        BSUM = RAW[:, 0, 1100:1100 + C]
        BWIDE = RAW[:, 0, 1200:1200 + C * P].rearrange("p (c n) -> p c n", n=P)
        FOLD = RAW[:, 0, 1500:1500 + C * D].rearrange("p (c n) -> p c n", n=D)
        W["ao1"] = (cut(FRA, 3072, (C, D)), cut(FRA, 3584, (C, D)))

        block = ctx.enter_context(nc.Block())

        KEY = PS[:, 6, 0:C * KP].rearrange("p (c n) -> p c n", n=KP)
        VALP = PS[:, 6, 160:160 + D]
        PV = PS[:, 7, 0:H * (DK + 1)].rearrange("p (h n) -> p h n", n=DK + 1)

        def mm3(pe, out, lhs, rhs, first, last):
            pe.matmul(out, lhs[0], rhs[0], start=first, stop=False)
            pe.matmul(out, lhs[0], rhs[1], start=False, stop=False)
            return pe.matmul(out, lhs[1], rhs[0], start=False, stop=last)

        def at_(pair, *idx):
            return pair[0][idx], pair[1][idx]

        def cols(m):
            return slice(m * P, (m + 1) * P)

        def feature_major(pe, out, w, x, ms, kc=C):
            for i, m in enumerate(ms):
                for k in range(kc):
                    last = mm3(pe, out[:, i, :], at_(w, slice(None), k, cols(m)), at_(x, slice(None), k, slice(None)),
                               k == 0, k == kc - 1)
            return last

        def token_major(pe, out, w, x, kc=C, js=range(J)):
            for i, j in enumerate(js):
                for k in range(kc):
                    last = mm3(pe, out[:, i, :], at_(x, slice(None), k, cols(j)), at_(w, slice(None), k, slice(None)),
                               k == 0, k == kc - 1)
            return last

        @block.sync
        def _(sp):
            for half, name in enumerate(("x_loaded", "x_rest_loaded")):
                part = slice(half * NB // 2, (half + 1) * NB // 2)
                sp.dma_start(X[:, part, :, :], a["x"][:, part, :, :]).then_inc(sem(name), 16)
            sp.dma_start(VEC[:, :], a["vec"]).then_inc(sem("const_loaded"), 16)
            sp.dma_start(ROW[:, :], a["row"].partition_broadcast(P)).then_inc(sem("const_loaded"), 16)
            sp.dma_start(IDENT[:, :], a["ident"]).then_inc(sem("const_loaded"), 16)
            sp.dma_start(MASK[:, :], a["mask"]).then_inc(sem("const_loaded"), 16)
            sp.dma_start(LOWER[:, :, :], a["lower"].partition_broadcast(P)).then_inc(sem("const_loaded"), 16)
            sp.dma_start(CT[:, :, :, :], a["ctx"]).then_inc(sem("ctx_loaded"), 16)
            for g in range(EARLY):
                if g >= 2:
                    sp.wait_ge(sem("w_lo"), g - 1)
                sp.dma_start(RAW[:, g % 2, 0:GSIZE[g]], a[f"g{g}"]).then_inc(sem(f"w_loaded{g % 2}"), 16)
            sp.wait_ge(sem("pool_const"), 9)
            sp.dma_start(rows_in.rearrange("(n p) d -> p n d", p=P),
                         QSCALE[:, :].unsqueeze(1).broadcast_to([P, NT * TILE // P, D])).then_inc(sem("rows_zero"), 16)
            sp.wait_ge(sem("c_done"), NB)
            sp.dma_start(RHS_T, a["rhs_t"]).then_inc(sem("rhs_loaded"), 16)
            sp.dma_start(XN[:, :, :, :], a["we"]).then_inc(sem("we_loaded"), 16)
            for g in range(EARLY, len(GROUPS)):
                sp.wait_ge(sem("w_lo"), g - 1)
                sp.dma_start(RAW[:, g % 2, 0:GSIZE[g]], a[f"g{g}"]).then_inc(sem(f"w_loaded{g % 2}"), 16)
            sp.wait_ge(sem("w_lo"), len(GROUPS))
            sp.dma_start(WO2, a["wo2"]).then_inc(sem("we_loaded"), 16)
            sp.dma_start(BE, a["be"]).then_inc(sem("we_loaded"), 16)
            sp.wait_ge(sem("f_added"), NB)
            for name, where in (("router", RW8), ("earlier", EARLIER)):
                sp.dma_start(where, a[name]).then_inc(sem("router_loaded"), 16)
            for name, where in (("keep", KEEP), ("number", NUMBER)):
                sp.dma_start(where, a[name].partition_broadcast(P)).then_inc(sem("router_loaded"), 16)

            def raw(w, e, u, up_free, down_free):
                if up_free is not None:
                    sp.wait_ge(sem("m_w_lo"), up_free + earlier("m_w_lo"))
                sp.dma_start(MRAW[u][:, 0:UP], a["moe"][e, :, 0:UP].rearrange("a p n -> (a p) n")).then_inc(sem(f"m_up{u}"), 16)
                if down_free is not None:
                    sp.wait_ge(sem("m_w_lo"), down_free + earlier("m_w_lo"))
                sp.dma_start(MRAW[u][:, UP:MSIZE], a["moe"][e, :, UP:MSIZE].rearrange("a p n -> (a p) n")).then_inc(sem(f"m_down{u}"), 16)

            raw(0, slice(E, E + 1), 0, None, None)
            sp.wait_ge(sem("m_routed"), 1)
            raw(1, bass.ds(sp.value_load(EXPERTU[0:1, 0:1], min_val=0, max_val=E - 1), 1), 1, None, None)
            sp.wait_ge(sem("m_scattered"), TOPK * T * 16)

            def g_load(n, u):
                released(sp, sem("m_g_t"), n)
                sp.dma_start(XG[u], rows_in[bass.ds(n * TILE, TILE), :].rearrange("(j p) d -> p j d", p=P)).then_inc(sem(f"m_g_loaded{u}"), 16)

            def g_raw(n, u):
                if isinstance(n, int) and n == NT - 1:
                    e = slice(E + 1, E + 2)
                else:
                    e = bass.ds(sp.value_load(EXPERTU[0:1, bass.ds(n + 1, 1)], min_val=0, max_val=E - 1), 1)
                raw(n + 2, e, u, n * 2 + 1, n * 2 + 2)

            def g_store(n, u):
                sp.wait_ge(sem("m_acc"), n + (TILES0 + 3))
                sp.dma_start(rows_out[bass.ds(n * TILE, TILE), :].rearrange("(j p) d -> p j d", p=P), YT[u]).then_inc(sem(f"m_stored{u}"), 16)

            pipeline(sp, [(g_load, 0), (g_raw, 0), (g_store, 3)], start=4, n=NT)
            with sp.Fori(0, NB) as b:
                sp.wait_ge(sem("m_done"), b + 1)
                sp.dma_start(out[:, bass.ds(b, 1), :, :].rearrange("p a j d -> p (a j) d"),
                             X[:, bass.ds(b, 1), :, :].rearrange("p a j d -> p (a j) d")).then_inc(sem("out_stored"), 16)
            sp.wait_ge(sem("out_stored"), NB * 16)

        @block.gpsimd
        def _(pool):
            pool.memset(HALF[:, :], -0.5).then_inc(sem("pool_const"), 1)
            pool.memset(ONES[:, :], 1.0).then_inc(sem("pool_const"), 1)
            pool.memset(MEANW[:, :], 1.0 / D).then_inc(sem("pool_const"), 1)
            for t in (HT[0], HT[1], AA, BB):
                pool.memset(t[:, :, 0:1], 0.0).then_inc(sem("pool_const"), 1)
            pool.memset(PPX[:, :, 0:1], LOWEST).then_inc(sem("pool_const"), 1)
            pool.memset(QSCALE[:, :], 0.0).then_inc(sem("pool_const"), 1)
            pool.wait_ge(sem("pool_const"), 9)

            def rstd(tag, base=0):
                def step(turn, u):
                    b = turn - base
                    wait_norm(pool, "var", tag, b + 1)
                    pool.tensor_tensor(RSTD[tag][:, b, :], VAR[tag][:, b, :], HALF[:, :],
                                       ALU.pow).then_inc(norm_sem("rstd", tag)[0], 1)
                return step

            def weights_lo(g):
                first, size = GROUPS[g][0], GSIZE[g]
                pool.wait_ge(sem("w_hi"), g + 1)
                pool.tensor_tensor(FRA[:, first + size:first + 2 * size], RAW[:, g % 2, 0:size],
                                   f(FRA[:, first:first + size]), ALU.subtract).then_inc(sem("w_lo"), 1)

            def rstd_all(tag):
                wait_norm(pool, "var", tag, NB)
                pool.tensor_tensor(RSTD[tag][:, :, :], VAR[tag][:, :, :], HALF[:, :].unsqueeze(1).broadcast_to([P, NB, J]),
                                   ALU.pow).then_inc(norm_sem("rstd", tag)[0], NB)

            rstd_all("n0")
            weights_lo(0)
            rstd_all("n1")

            def b_mix_lo(b, u):
                for m in range(3):
                    pool.wait_ge(sem("b_mix_hi"), b * 3 + (m + 1))
                    pool.tensor_tensor(MIXS[u][m][1], MIX[m], f(MIXS[u][m][0]), ALU.subtract).then_inc(sem("b_mix_lo"), 1)

            def b_den(b, u):
                pool.wait_ge(sem("b_num"), b + 1)
                pool.tensor_tensor(T2, T2, BB[:, :, 0:S], ALU.mult).then_inc(sem("b_den"), 1)
                pool.wait_ge(sem("b_den"), b * 3 + 1)
                pool.tensor_tensor(T2, T2, UK[u], ALU.add).then_inc(sem("b_den"), 1)
                pool.wait_ge(sem("b_den"), b * 3 + 2)
                pool.tensor_tensor(T2, T2, EZ[u], ALU.mult).then_inc(sem("b_den"), 1)

            def weights_later(b, u):
                if isinstance(b, int):
                    weights_lo(b + 1 if b < 2 else b + 5 - NB)

            pipeline(pool, [(b_mix_lo, 0), (b_den, 1), (rstd("n2"), 2), (weights_later, 0), (weights_later, 2)])

            def c_residual(b, u):
                pool.wait_ge(sem("b_done"), b + 1)
                pool.tensor_tensor(X[:, b, :, :], X[:, b, :, :], XN[:, b, :, :], ALU.add).then_inc(sem("c_residual"), 1)

            def c_square(b, u):
                for q in range(4):
                    pool.wait_ge(sem("c_relu"), b * 4 + (q + 1))
                    released(pool, sem("c_kk"), b, depth=1, per=4)
                    pool.tensor_tensor(KK[:, q], RELU[:, q], RELU[:, q], ALU.mult).then_inc(sem("c_square"), 1)

            pipeline(pool, [(c_square, 2), (c_residual, 0), (rstd("n3"), 3)], start=4)

            def up_lo(w, u):
                pool.wait_ge(sem("m_w_hi"), w * 2 + 1 + earlier("m_w_hi"))
                pool.tensor_tensor(MW[u]["up"][1], MRAW[u][:, 0:UP], f(MW[u]["up"][0]), ALU.subtract).then_inc(sem("m_w_lo"), 1)

            def down_lo(w, u):
                pool.wait_ge(sem("m_w_hi"), w * 2 + 2 + earlier("m_w_hi"))
                pool.tensor_tensor(MW[u]["down"][1], MRAW[u][:, UP:MSIZE], f(MW[u]["down"][0]),
                                   ALU.subtract).then_inc(sem("m_w_lo"), 1)

            def attention(k, tag):
                s, base = "d_", NB * k

                def bias(b, u):
                    pool.wait_ge(sem(f"d{k}_xt"), b + 1 + earlier(f"d{k}_xt"))
                    pool.tensor_tensor(X[:, b - base, :, :], X[:, b - base, :, :],
                                       row(f"bo{k}").unsqueeze(1).broadcast_to([P, J, D]), ALU.add).then_inc(sem(s + "bias"), 1)

                def spread(b, u):
                    pool.wait_ge(sem(s + "k_lo"), (b + 1) * 2)
                    released(pool, sem(s + "score"), b, depth=1, per=J)
                    for part in range(2):
                        for c in range(C):
                            ins = pool.tensor_tensor(
                                KBD[part][:, c], f(KS[part][:, c:c + 1, :]).broadcast_to([P, HC, KP]),
                                MASK[:, :].unsqueeze(2).broadcast_to([P, HC, KP]), ALU.mult)
                            ins.then_inc(sem(s + "spread"), 1)

                def weights_later(b, u):
                    if k == 0 and isinstance(b, int) and b >= NB - 2:
                        for g in range(EARLY + 2 * (b - NB + 2), EARLY + 2 * (b - NB + 3)):
                            weights_lo(g)
                    if k == 1 and isinstance(b, int) and b == base + NB - 2:
                        up_lo(0, 0)
                        down_lo(0, 0)

                pipeline(pool, [(bias, 0), (spread, 0), (weights_later, 2), (rstd(tag, base), 2)], base=base)

            pool.wait_ge(sem("const_loaded"), 80)
            attention(0, "n4")

            pool.wait_ge(sem("we_loaded"), 48)
            for n, e in enumerate(range(1, E)):
                if n:
                    pool.wait_ge(sem("we_sum"), n)
                pool.tensor_tensor(WE[:, :, 0, :], WE[:, :, 0, :], WE[:, :, e, :], ALU.add).then_inc(sem("we_sum"), 1)

            pipeline(pool, [(rstd("n5"), 0)])

            def f_gate(b, u):
                pool.wait_ge(sem("f_silu"), (b + 1) * 8)
                released(pool, sem("f_y"), b)
                pool.tensor_tensor(GI[u], XI[u], RES, ALU.mult).then_inc(sem("f_gate"), 1)

            def f_skip(b, u):
                pool.wait_ge(sem("f_xt"), b + 1 + earlier("f_xt"))
                released(pool, sem("f_skipped"), b, depth=1)
                for j in range(J):
                    pool.tensor_tensor(SKIP[:, j, :], XT[u][:, j, :], row("skip"), ALU.mult).then_inc(sem("f_skip"), 1)
                pool.wait_ge(sem("f_skip"), b * 4 + 2)
                for j in range(J):
                    pool.tensor_tensor(SKIP[:, j, :], SKIP[:, j, :], row("b_out"), ALU.add).then_inc(sem("f_skip"), 1)
                pool.wait_ge(sem("f_skip"), b * 4 + 4)
                pool.tensor_tensor(X[:, b, :, :], X[:, b, :, :], SKIP, ALU.add).then_inc(sem("f_skipped"), 1)

            pipeline(pool, [(f_skip, 0), (f_gate, 0), (rstd("n6"), 3)], start=4)

            attention(1, "n7")

            def m_keep(b, u):
                pool.wait_ge(sem("m_xt"), b + 1 + earlier("m_xt"))
                pool.tensor_copy(XN[:, b, :, :], XT[u]).then_inc(sem("m_kept"), 1)

            pipeline(pool, [(m_keep, 0)])

            def g_weights(n, u):
                down_lo(n + 1, 1 - u)
                up_lo(n + 2, u)

            pool.wait_ge(sem("m_slots"), 1)
            pool.wait_ge(sem("rows_zero"), 16)
            pool.wait_ge(sem("m_kept"), NB)
            for t in range(T):
                for k in range(TOPK):
                    pool.indirect_dma_start(rows_in, bass.IndirectOffsetOnAxis(SLOTU[:, k * T + t:k * T + t + 1], 0),
                                            XN[:, t // J, t % J, :], None, bounds_check=NT * TILE - 1,
                                            oob_is_err=False).then_inc(sem("m_scattered"), 16)
            up_lo(1, 1)
            pipeline(pool, [(g_weights, 0)], n=NT)
            down_lo(LAST, LAST % 2)
            pool.wait_ge(sem("m_scattered"), TOPK * T * 16)
            for u in range(2):
                pool.wait_ge(sem(f"m_stored{u}"), (NT + 1 - u) // 2 * 16)
            for b in range(NB):
                if b >= 2:
                    pool.wait_ge(sem(f"m_back{b % 2}"), b // 2 * J * TOPK * 16)
                for t in range(b * J, (b + 1) * J):
                    for k in range(TOPK):
                        pool.indirect_dma_start(BACK[k][:, t, :], None, rows_out,
                                                bass.IndirectOffsetOnAxis(SLOTU[:, k * T + t:k * T + t + 1], 0),
                                                bounds_check=NT * TILE - 1,
                                                oob_is_err=False).then_inc(sem(f"m_back{b % 2}"), 16)

        @block.scalar
        def _(act):
            act.wait_ge(sem("const_loaded"), 80)
            act.activation(WD[:, :], VEC[:, VECS["decay"][0]:VECS["decay"][0] + C], ACT.Exp).then_inc(sem("decay_exp"), 1)

            def weights_hi(g):
                first, size = GROUPS[g][0], GSIZE[g]
                act.wait_ge(sem(f"w_loaded{g % 2}"), 16 * (g // 2 + 1))
                act.activation(FRA[:, first:first + size], RAW[:, g % 2, 0:size], ACT.Copy).then_inc(sem("w_hi"), 1)

            weights_hi(0)
            act.wait_ge(sem("pool_const"), 9)

            def h_t(b, u):
                act.wait_ge(sem("b_t"), b + 1)
                released(act, sem("b_mixed"), b, per=3)
                for c in range(C):
                    ins = act.activation(HT[u][:, c, 1:S + 1], bank(6)[:, c, :], ACT.Identity,
                                         bias=vec("ln1_b", c), scale=vec("ln1_w", c))
                    ins.then_inc(sem("b_ht"), 1)

            def mix_hi(b, u):
                for m in range(3):
                    act.wait_ge(sem("b_mixed"), b * 3 + (m + 1))
                    act.activation(MIXS[u][m][0], MIX[m], ACT.Copy).then_inc(sem("b_mix_hi"), 1)

            def kvr(b, u):
                act.wait_ge(sem("b_kvr"), b * 3 + 1)
                act.activation(KB[u], bank(u), ACT.Copy).then_inc(sem("b_k"), 1)
                for c in range(C):
                    act.activation(UK[u][:, c, :], bank(u)[:, c, :], ACT.Identity,
                                   bias=vec("first", c)).then_inc(sem("b_k"), 1)
                act.wait_ge(sem("b_kvr"), b * 3 + 3)
                act.activation(EZ[u], bank(4 + u), ACT.Exp, scale=-1.0).then_inc(sem("b_k"), 1)
                act.wait_ge(sem("b_k"), b * 5 + 4)
                act.activation(EZ[u], EZ[u], ACT.Identity, bias=1.0).then_inc(sem("b_k"), 1)

            def wkv_exp(b, u):
                act.wait_ge(sem("b_e_state"), b + 1)
                act.activation(T3, T3, ACT.Exp).then_inc(sem("b_exp"), 1)
                act.activation(KB[u], KB[u], ACT.Exp).then_inc(sem("b_exp"), 1)
                act.wait_ge(sem("b_e_out"), b + 1)
                act.activation(T2, T2, ACT.Exp).then_inc(sem("b_exp"), 1)
                act.activation(UK[u], UK[u], ACT.Exp).then_inc(sem("b_exp"), 1)

            def y_hi(b, u):
                act.wait_ge(sem("b_y"), b + 1)
                act.activation(RW[u][0], T3, ACT.Copy).then_inc(sem("b_y_hi"), 1)

            def weights_later(b, u):
                if isinstance(b, int):
                    weights_hi(b + 1 if b < 2 else b + 5 - NB)

            pipeline(act, [(h_t, 0), (wkv_exp, 1), (mix_hi, 0), (y_hi, 1), (kvr, 0), (weights_later, 0), (weights_later, 2)])

            def c_h(b, u):
                act.wait_ge(sem("c_t"), b + 1 + earlier("c_t"))
                released(act, sem("c_mixed"), b, per=2, base=earlier("c_mixed"))
                for c in range(C):
                    act.activation(HT[u][:, c, 1:S + 1], bank(6)[:, c, :], ACT.Identity,
                                   bias=vec("ln2_b", c), scale=vec("ln2_w", c)).then_inc(sem("c_ht"), 1)

            def c_mix_hi(b, u):
                for m in range(2):
                    act.wait_ge(sem("c_mixed"), b * 2 + (m + 1) + earlier("c_mixed"))
                    act.activation(FMIXS[u][m][0], MIX[m], ACT.Copy).then_inc(sem("c_mix_hi"), 1)

            def c_gate(b, u):
                act.wait_ge(sem("c_rec"), b + 1)
                released(act, sem("c_gated"), b)
                act.activation(SIG[u], bank(5), ACT.Sigmoid).then_inc(sem("c_sig"), 1)

            def c_relu(b, u):
                for q in range(4):
                    act.wait_ge(sem("c_key"), b * 4 + (q + 1))
                    if not (isinstance(b, int) and b == 0):
                        act.wait_ge(sem("c_square"), b * 4 + (q - 3))
                        act.wait_ge(sem("c_kk_hi"), b * 4 + (q - 3))
                    act.activation(RELU[:, q], bank(q), ACT.Relu).then_inc(sem("c_relu"), 1)

            def c_kk_hi(b, u):
                for q in range(4):
                    act.wait_ge(sem("c_relu"), b * 4 + (q + 1))
                    released(act, sem("c_val"), b, depth=1)
                    act.activation(KKS[0][:, q], RELU[:, q], ACT.Square).then_inc(sem("c_kk_hi"), 1)

            pipeline(act, [(c_kk_hi, 2), (c_relu, 1), (c_gate, 1), (c_h, 0), (c_mix_hi, 0)], start=4)

            def up_hi(w, u):
                act.wait_ge(sem(f"m_up{u}"), (w - u) * 8 + 16 + earlier(f"m_up{u}"))
                if not (isinstance(w, int) and w < 2):
                    act.wait_ge(sem("m_hid"), (w + (NB - 2)) * 4)
                act.activation(MW[u]["up"][0], MRAW[u][:, 0:UP], ACT.Copy).then_inc(sem("m_w_hi"), 1)

            def down_hi(w, u):
                act.wait_ge(sem(f"m_down{u}"), (w - u) * 8 + 16)
                if not (isinstance(w, int) and w < 2):
                    act.wait_ge(sem("m_y"), w + NB)
                act.activation(MW[u]["down"][0], MRAW[u][:, UP:MSIZE], ACT.Copy).then_inc(sem("m_w_hi"), 1)

            def attention(k):
                s, base = "d_", NB * k

                def x_hi(b, u):
                    act.wait_ge(sem(f"d{k}_t"), b + 1 + earlier(f"d{k}_t"))
                    released(act, sem(s + "q"), b, depth=1)
                    act.activation(XS[0], bank(6), ACT.Copy).then_inc(sem(s + "x_hi"), 1)

                def ctx_hi(b, u):
                    released(act, sem(s + "kv"), b, depth=1)
                    act.activation(CS[0], CT[:, :, b - base, :], ACT.Copy).then_inc(sem(s + "ctx_hi"), 1)

                def q_hi(b, u):
                    act.wait_ge(sem(s + "q"), b + 1)
                    for c in range(C):
                        act.activation(QS[u][0][:, c, :], bank(6)[:, c, :], ACT.Identity,
                                       bias=vec(f"bq{k}", c)).then_inc(sem(s + "q_hi"), 1)

                def k_hi(b, u):
                    act.wait_ge(sem(s + "kv"), b + 1)
                    released(act, sem(s + "spread"), b, depth=1, per=4)
                    for c in range(C):
                        act.activation(KS[0][:, c, :], KEY[:, c, :], ACT.Identity,
                                       bias=vec(f"bk{k}", c)).then_inc(sem(s + "k_hi"), 1)

                def exps(j):
                    def step(b, u):
                        act.wait_ge(sem(s + "centred"), b * J + (j + 1))
                        act.activation(PROB[j], PROB[j], ACT.Exp, scale=DK ** -0.5).then_inc(sem(s + "exp"), 1)
                    return step

                def pt(j, half):
                    def step(b, u):
                        for r in (2 * half, 2 * half + 1):
                            act.wait_ge(sem(s + "pt"), (b * J + j) * 4 + (r + 1))
                            act.activation(PT[0:KEYS, 4 * r:4 * r + 4, :], bank(4 + r % 2, P)[0:KEYS],
                                           ACT.Copy).then_inc(sem(s + "pt_read"), 1)
                    return step

                def o_hi(j):
                    def step(b, u):
                        act.wait_ge(sem(s + "ot"), b * J + (j + 1))
                        act.activation(OS[0], bank(7, P)[:, 0:2, :], ACT.Copy).then_inc(sem(s + "o_hi"), 1)
                    return step

                def weights_later(b, u):
                    if k == 0 and isinstance(b, int) and b >= NB - 2:
                        for g in range(EARLY + 2 * (b - NB + 2), EARLY + 2 * (b - NB + 3)):
                            weights_hi(g)
                    if k == 1 and isinstance(b, int) and b == base + NB - 2:
                        up_hi(0, 0)
                        down_hi(0, 0)

                pipeline(act, [(o_hi(0), 2), (pt(1, 0), 2), (x_hi, 0), (pt(1, 1), 2), (exps(0), 1), (ctx_hi, 0), (q_hi, 0),
                               (k_hi, 0), (o_hi(1), 2), (pt(0, 0), 1), (pt(0, 1), 1), (exps(1), 1), (weights_later, 2)],
                         base=base)

            act.wait_ge(sem("ctx_loaded"), 16)
            attention(0)

            act.wait_ge(sem("rhs_t"), 1)
            act.activation(QW[:, :, :], bank(4), ACT.Copy).then_inc(sem("qw"), 1)
            act.wait_ge(sem("rhs_b"), 1 + earlier("rhs_b"))
            act.wait_ge(sem("rows_zero"), 16)
            act.activation(QSCALE[:, :], PS[:, 5, 0:D], ACT.Copy).then_inc(sem("qw"), 1)

            def e_q(b, u):
                act.wait_ge(sem("e_t"), b + 1 + earlier("e_t"))
                released(act, sem("e_prod"), b)
                act.activation(QX[u][:, :, :], bank(6 + u), ACT.Copy).then_inc(sem("e_qx"), 1)

            pipeline(act, [(e_q, 0)])

            act.wait_ge(sem("fold"), 1)
            act.activation(FOLD, bank(0), ACT.Copy, scale=1.0 / E).then_inc(sem("folded"), 1)
            act.wait_ge(sem("folded"), 1)
            act.activation(W["ao1"][0], FOLD, ACT.Copy).then_inc(sem("folded"), 1)

            act.wait_ge(sem("const_loaded"), 80)
            act.activation(AD[0:NS, :], vec("a_log", rows=NS), ACT.Exp).then_inc(sem("a_exp"), 1)

            def f_x_hi(b, u):
                act.wait_ge(sem("f_t"), b + 1 + earlier("f_t"))
                released(act, sem("f_in"), b, depth=1, per=4)
                act.activation(FXS[0], bank(6), ACT.Copy).then_inc(sem("f_x_hi"), 1)

            def f_dt(b, u):
                act.wait_ge(sem("f_dt"), b + 1)
                released(act, sem("f_sp"), b, depth=1)
                for c in range(C):
                    act.activation(DT[:, c, :], bank(4)[:, c, :], ACT.Identity, bias=vec("b_dt", c)).then_inc(sem("f_dt_read"), 1)
                    act.activation(DTA[:, c, :], bank(4)[:, c, :], ACT.Abs, bias=vec("b_dt", c)).then_inc(sem("f_dt_read"), 1)
                act.wait_ge(sem("f_dt_read"), (b + 1) * 4)
                act.activation(DTA, DTA, ACT.Exp, scale=-1.0).then_inc(sem("f_exp"), 1)
                act.wait_ge(sem("f_xp"), b + 1)
                act.activation(BX[u][0:NS, :], PS[0:NS, 5, 0:S], ACT.Identity, bias=vec("b_xp", rows=NS)).then_inc(sem("f_bx"), 1)
                act.wait_ge(sem("f_exp"), b + 1)
                act.activation(DTA, DTA, ACT.Ln, bias=1.0).then_inc(sem("f_ln"), 1)

            def f_decay(b, u):
                act.wait_ge(sem("f_mean"), b + 1)
                act.activation(AT[0:NS, :], PS[0:NS, 5, S:2 * S], ACT.Exp, scale=AD[0:NS, :]).then_inc(sem("f_decay"), 1)

            def silu(half):
                def step(b, u):
                    for q in (2 * half, 2 * half + 1):
                        act.wait_ge(sem("f_in"), b * 4 + (q + 1))
                        if q == 2:
                            released(act, sem("f_gate"), b, depth=1)
                        for c in range(C):
                            m = 2 * q + c
                            dst = XI[u][:, m, :] if m < 4 else RES[:, m - 4, :]
                            act.activation(dst, bank(q)[:, c, :], ACT.Silu, bias=vec("b_in", m)).then_inc(sem("f_silu"), 1)
                return step

            def f_xi_hi(b, u):
                act.wait_ge(sem("f_silu"), b * 8 + 4)
                released(act, sem("f_xp"), b, depth=1)
                act.activation(XIS[0], XI[u], ACT.Copy).then_inc(sem("f_xi_hi"), 1)

            def f_y_hi(b, u):
                act.wait_ge(sem("f_y"), b + 1)
                released(act, sem("f_out"), b, depth=1)
                act.activation(YS[0], YF, ACT.Copy).then_inc(sem("f_y_hi"), 1)

            act.wait_ge(sem("a"), 1 + earlier("a"))
            pipeline(act, [(f_decay, 2), (f_x_hi, 0), (f_dt, 1), (silu(0), 0), (f_y_hi, 2), (f_xi_hi, 0), (silu(1), 0)],
                     start=4)

            act.wait_ge(sem("f_out"), NB)
            attention(1)

            act.sem_inc(sem("m_h_hi"), 2)

            def m_x_hi(b, u):
                act.wait_ge(sem("m_t"), b + 1 + earlier("m_t"))
                released(act, sem("m_logit"), b)
                act.activation(XF[u], bank(6 + u), ACT.Copy).then_inc(sem("m_xf"), 1)
                act.activation(XFS[0][:, :, b, :], bank(6 + u), ACT.Copy).then_inc(sem("m_x_hi"), 1)

            pipeline(act, [(m_x_hi, 0)])
            act.wait_ge(sem("m_centred"), 1)
            act.activation(LOGIT_E, LOGIT, ACT.Exp).then_inc(sem("m_exp"), 1)

            def silu(first):
                def step(b, u):
                    n = b + first
                    for m in range(HID // P):
                        act.wait_ge(sem("m_hid"), n * 4 + (m + 1))
                        act.activation(SILU[:, m, :], bank(m)[:, 0, :], ACT.Silu).then_inc(sem("m_silu"), 1)
                return step

            def h_hi(first):
                def step(b, u):
                    n, u = b + first, (u + first) % 2
                    act.wait_ge(sem("m_h"), n * 4 + 12)
                    act.wait_ge(sem("m_y"), n + 1)
                    act.activation(HS[u][0], HB[u], ACT.Copy).then_inc(sem("m_h_hi"), 1)
                return step

            def g_weights(n, u):
                down_hi(n + 1, 1 - u)
                up_hi(n + 2, u)

            def g_x_hi(n, u):
                act.wait_ge(sem("m_g_t"), n + 1)
                if not (isinstance(n, int) and n == 0):
                    act.wait_ge(sem("m_hid"), n * 4 + TILES0 * 4)
                act.activation(XGS[0], bank(6), ACT.Copy).then_inc(sem("m_g_hi"), 1)

            pipeline(act, [(silu(SHARED0), 0), (h_hi(SHARED0), 0)])
            up_hi(1, 1)
            pipeline(act, [(g_weights, 1), (silu(TILES0), 1), (g_x_hi, 0), (h_hi(TILES0), 1)], n=NT)
            down_hi(LAST, LAST % 2)
            pipeline(act, [(silu(SHARED1), 0), (h_hi(SHARED1), 0)])

        @block.tensor
        def _(pe):
            def transposes(tag, read, per, k=6):
                def step(b, u):
                    pe.wait_ge(sem(f"{tag}_xt"), b + 1 + earlier(f"{tag}_xt"))
                    released(pe, sem(read), b, depth=1, per=per, base=earlier(read))
                    for c in range(C):
                        for j in range(J):
                            ins = pe.transpose(bank(k)[:, c, cols(j)], XT[u][:, j, cols(c)], IDENT[:, :])
                    ins.then_inc(sem(f"{tag}_t"), 1)
                return step

            def b_project(b, u):
                released(pe, sem("b_y"), b)
                for m, name in enumerate(("wk", "wv", "wr")):
                    pe.wait_ge(sem("b_mix_lo"), b * 3 + (m + 1))
                    feature_major(pe, bank(2 * m + u), W[name], MIXS[u][m], range(C)).then_inc(sem("b_kvr"), 1)

            def b_out(b, u):
                pe.wait_ge(sem("b_y_lo"), b + 1)
                released(pe, sem("b_done"), b, depth=1)
                token_major(pe, bank(7), W["wo"], RW[u]).then_inc(sem("b_o"), 1)

            pe.wait_ge(sem("const_loaded"), 80)
            pe.wait_ge(sem("w_lo"), 1)
            pipeline(pe, [(transposes("b", "b_ht", 2), 0), (b_project, 0), (b_out, 1)])

            def c_values(b, u):
                pe.wait_ge(sem("c_kk"), (b + 1) * 4)
                released(pe, sem("c_gated"), b, depth=1)
                token_major(pe, bank(4), W["wval"], (KKS[0].rearrange("p q m n -> p (q m) n"),
                                                     KKS[1].rearrange("p q m n -> p (q m) n")),
                            kc=F1 // P).then_inc(sem("c_val"), 1)

            def c_keys(b, u):
                pe.wait_ge(sem("c_mix_lo"), b * 2 + 1 + earlier("c_mix_lo"))
                for q in range(4):
                    released(pe, sem("c_relu"), b, depth=1, per=4)
                    feature_major(pe, bank(q), W["wkey"], FMIXS[u][0], (2 * q, 2 * q + 1)).then_inc(sem("c_key"), 1)
                pe.wait_ge(sem("c_mix_lo"), b * 2 + 2 + earlier("c_mix_lo"))
                released(pe, sem("c_sig"), b, depth=1)
                token_major(pe, bank(5), W["wrec"], FMIXS[u][1]).then_inc(sem("c_rec"), 1)

            pe.wait_ge(sem("w_lo"), 4)
            pe.wait_ge(sem("b_done"), NB)
            pipeline(pe, [(c_keys, 1), (transposes("c", "c_ht", 2), 0), (c_values, 2)], start=4)

            def attention(k):
                s, base = "d_", NB * k
                wq, wk, wv, wo = (W[f"a{m}{k}"] for m in "qkvo")

                def t(b, u):
                    pe.wait_ge(sem(f"d{k}_xt"), b + 1 + earlier(f"d{k}_xt"))
                    released(pe, sem(s + "v"), b, depth=1)
                    for c in range(C):
                        for j in range(J):
                            ins = pe.transpose(bank(6)[:, c, cols(j)], XT[u][:, j, cols(c)], IDENT[:, :])
                    ins.then_inc(sem(f"d{k}_t"), 1)

                def q(b, u):
                    pe.wait_ge(sem(s + "x_lo"), b + 1)
                    feature_major(pe, bank(6), wq, XS, range(C)).then_inc(sem(s + "q"), 1)

                def kv(b, u):
                    pe.wait_ge(sem(s + "ctx_lo"), b + 1)
                    pe.wait_ge(sem(s + "q_lo"), (b + 1) * 2)
                    feature_major(pe, KEY, wk, CS, range(C))
                    for c in range(C):
                        ins = mm3(pe, VALP[0:KP, :], at_(CS, slice(None), c, slice(None)), at_(wv, slice(None), c, slice(None)),
                                  c == 0, c == C - 1)
                    ins.then_inc(sem(s + "kv"), 1)

                def scores(j):
                    def step(b, u):
                        pe.wait_ge(sem(s + "q_lo"), (b + 1) * 2)
                        pe.wait_ge(sem(s + "spread"), (b + 1) * 4)
                        if j:
                            pe.wait_ge(sem(s + "centred"), b * J + j)
                        else:
                            released(pe, sem(s + "centred"), b, depth=1, per=J)
                        for c in range(C):
                            for g in range(2):
                                heads = (slice(None), c, slice(4 * g, 4 * g + 4), slice(None))
                                ins = mm3(pe, PS[:, 2 * c + g, 0:4 * KP].rearrange("p (h n) -> p h n", n=KP),
                                          at_(QS[u], slice(None), c, cols(j)), at_(KBD, *heads), True, True)
                        ins.then_inc(sem(s + "score"), 1)
                    return step

                def pt(j, half):
                    def step(b, u):
                        pe.wait_ge(sem(s + "exp"), b * J + (j + 1))
                        if half == 0 and not (isinstance(b, int) and b == 0):
                            pe.wait_ge(sem(s + "added"), b * J + (j - 1))
                        for r in (2 * half, 2 * half + 1):
                            if not (isinstance(b, int) and b == 0 and j == 0 and r < 2):
                                pe.wait_ge(sem(s + "pt_read"), b * J * 4 + (j * 4 + r - 1))
                            for h in range(4):
                                ins = pe.transpose(PS[0:KEYS, 4 + r % 2, cols(h)], PROB[j][:, 4 * r + h, :], IDENT[:, :])
                            ins.then_inc(sem(s + "pt"), 1)
                    return step

                def weigh(j):
                    def step(b, u):
                        pe.wait_ge(sem(s + "pt_read"), (b * J + j) * 4 + 4)
                        pe.wait_ge(sem(s + "v"), b + 1)
                        for h in range(H):
                            ins = pe.matmul(PV[:, h, :], PT[0:KEYS, h, :], VAL[u][0:KEYS, h, :], start=True, stop=True)
                        ins.then_inc(sem(s + "pv"), 1)
                    return step

                def ot(j):
                    def step(b, u):
                        pe.wait_ge(sem(s + "o"), b * J + (j + 1))
                        for c in range(C):
                            ins = pe.transpose(bank(7, P)[:, c, :], OUTN[:, cols(c)], IDENT[:, :])
                        ins.then_inc(sem(s + "ot"), 1)
                    return step

                def project(j):
                    def step(b, u):
                        last = j == J - 1 and isinstance(b, int) and b == base + NB - 1
                        pe.wait_ge(sem(s + "o_lo"), b * J + (j + 1))
                        pe.wait_ge(sem(s + "pt_read"), (b * J + j) * 4 + (4 if last else 7))
                        for c in range(C):
                            ins = mm3(pe, bank(4)[:, 0, :], at_(OS, slice(None), c, slice(None)),
                                      at_(wo, slice(None), c, slice(None)), c == 0, c == C - 1)
                        ins.then_inc(sem(s + "proj"), 1)
                    return step

                pipeline(pe, [(scores(0), 1), (ot(0), 2), (pt(1, 0), 2), (t, 0), (pt(1, 1), 2), (project(0), 2),
                              (weigh(1), 2), (q, 0),
                              (scores(1), 1), (kv, 0), (ot(1), 2), (pt(0, 0), 1), (pt(0, 1), 1), (project(1), 2),
                              (weigh(0), 1)], base=base)

            pe.wait_ge(sem("w_lo"), EARLY)
            attention(0)

            pe.wait_ge(sem("rhs_q"), 1)
            pe.wait_ge(sem("d_added"), NB * J)
            for c in range(C):
                for n in range(C):
                    ins = pe.transpose(bank(4)[:, c, cols(n)], RHS_Q[:, n, cols(c)], IDENT[:, :])
            ins.then_inc(sem("rhs_t"), 1)
            pe.wait_ge(sem("rhs_diag"), 1 + earlier("rhs_diag"))
            for n in range(C):
                ins = pe.matmul(PS[:, 5, cols(n)], ONES[:, :], QDIAG[:, n, :], start=True, stop=True)
            ins.then_inc(sem("rhs_b"), 1)

            def e_t(b, u):
                pe.wait_ge(sem("e_xt"), b + 1 + earlier("e_xt"))
                released(pe, sem("e_qx"), b)
                for c in range(C):
                    for j in range(J):
                        ins = pe.transpose(bank(6 + u)[:, c, cols(j)], XQ[u][:, j, cols(c)], IDENT[:, :])
                ins.then_inc(sem("e_t"), 1)

            def e_prod(b, u):
                pe.wait_ge(sem("e_qx"), b + 1)
                released(pe, sem("e_scaled"), b, per=J)
                for j in range(J):
                    for c in range(C):
                        ins = pe.matmul(bank(4 + u)[:, j, :], QX[u][:, c, cols(j)], QW[:, c, :], start=c == 0, stop=c == C - 1)
                ins.then_inc(sem("e_prod"), 1)

            pe.wait_ge(sem("qw"), 2)
            pipeline(pe, [(e_prod, 1), (e_t, 0)])

            pe.wait_ge(sem("we_sum"), E - 1)
            for m in range(C):
                for c in range(C):
                    ins = pe.matmul(bank(0)[:, m, :], WE[:, c, 0, cols(m)], WO2[:, c, :], start=c == 0, stop=c == C - 1)
            ins.then_inc(sem("fold"), 1)
            pe.wait_ge(sem("be_wide"), 1)
            for c in range(C):
                ins = pe.matmul(PS[:, 1, 0:D], BWIDE[:, c, :], WO2[:, c, :], start=c == 0, stop=c == C - 1)
            ins.then_inc(sem("fold"), 1)

            def f_in(b, u):
                pe.wait_ge(sem("f_x_lo"), b + 1)
                for q in range(4):
                    released(pe, sem("f_silu"), b, depth=1, per=8)
                    feature_major(pe, bank(q), W["w_in"], FXS, (2 * q, 2 * q + 1)).then_inc(sem("f_in"), 1)

            def f_dt(b, u):
                pe.wait_ge(sem("f_xi_lo"), b + 1)
                released(pe, sem("f_dt_read"), b, depth=1, per=4)
                feature_major(pe, bank(4), W["w_dt"], XIS, range(C), kc=DI // P).then_inc(sem("f_dt"), 1)
                released(pe, sem("f_decay"), b, depth=1)
                for k in range(DI // P):
                    ins = mm3(pe, PS[0:NS, 5, 0:S], at_(W["w_xp"], slice(None), k, slice(None)),
                              at_(XIS, slice(None), k, slice(None)), k == 0, k == DI // P - 1)
                ins.then_inc(sem("f_xp"), 1)

            def f_mean(b, u):
                pe.wait_ge(sem("f_sp"), b + 1)
                pe.wait_ge(sem("f_bx"), b + 1)
                for c in range(C):
                    ins = pe.matmul(PS[0:NS, 5, S:2 * S], MEANW[:, :], SP_[:, c, :], start=c == 0, stop=c == C - 1)
                ins.then_inc(sem("f_mean"), 1)

            def f_sum(b, u):
                pe.wait_ge(sem("f_states"), b + 1)
                released(pe, sem("f_added"), b, depth=1)
                pe.matmul(PS[:, 7, 0:S], ONES[0:NS, :], ST[0:NS, :], start=True, stop=True).then_inc(sem("f_sum"), 1)

            def f_out(b, u):
                pe.wait_ge(sem("f_y_lo"), b + 1)
                token_major(pe, bank(7), W["w_out"], YS, kc=DI // P).then_inc(sem("f_out"), 1)

            pe.wait_ge(sem("w_lo"), len(GROUPS))
            pe.wait_ge(sem("e_added"), NB)
            pipeline(pe, [(f_mean, 2), (transposes("f", "f_x_lo", 1), 0), (f_dt, 1), (f_out, 3), (f_sum, 2), (f_in, 0)],
                     start=4)

            pe.wait_ge(sem("folded"), 3)
            attention(1)

            pe.sem_inc(sem("m_y"), 2)

            def m_t(b, u):
                pe.wait_ge(sem("m_xt"), b + 1 + earlier("m_xt"))
                released(pe, sem("m_x_lo"), b)
                for c in range(C):
                    for j in range(J):
                        ins = pe.transpose(bank(6 + u)[:, c, cols(j)], XT[u][:, j, cols(c)], IDENT[:, :])
                ins.then_inc(sem("m_t"), 1)

            def m_logit(b, u):
                pe.wait_ge(sem("m_xf"), b + 1)
                released(pe, sem("m_logit_read"), b)
                for j in range(J):
                    for c in range(C):
                        ins = pe.matmul(PS[:, 4 + u, j * E:(j + 1) * E], XF[u][:, c, cols(j)], RW8[:, c, :],
                                        start=c == 0, stop=c == C - 1)
                ins.then_inc(sem("m_logit"), 1)

            pe.wait_ge(sem("router_loaded"), 64)
            pipeline(pe, [(m_t, 0), (m_logit, 1)])
            pe.wait_ge(sem("m_x_lo"), NB)
            pe.wait_ge(sem("m_logit_read"), NB)
            pe.wait_ge(sem("m_taken"), 1)
            taken = TAKEN.rearrange("p e t -> p (e t)")
            pe.matmul(PS[:, 6, 0:E * T], EARLIER, taken, start=True, stop=True)
            pe.matmul(PS[:, 7, 0:E * T], ONES[:, :], taken, start=True, stop=True).then_inc(sem("m_counted"), 1)

            def g_t(n, u):
                pe.wait_ge(sem(f"m_g_loaded{u}"), (n - u) * 8 + 16)
                if isinstance(n, int) and n == 0:
                    pe.wait_ge(sem("m_routed"), 1)
                else:
                    pe.wait_ge(sem("m_g_lo"), n)
                for c in range(C):
                    for j in range(J):
                        ins = pe.transpose(bank(6)[:, c, cols(j)], XG[u][:, j, cols(c)], IDENT[:, :])
                ins.then_inc(sem("m_g_t"), 1)

            def hidden(n, u, uw, x):
                for m in range(HID // P):
                    pe.wait_ge(sem("m_h"), n * 4 + (m + 5))
                    for half, w in enumerate(("w1", "w3")):
                        ins = feature_major(pe, bank(m)[:, half:half + 1, :], MW[uw][w], x, (m,))
                    ins.then_inc(sem("m_hid"), 1)

            def output(n, u, uw):
                pe.wait_ge(sem("m_h_lo"), n + 1)
                pe.wait_ge(sem("m_acc"), n + 1)
                token_major(pe, bank(4 + u), MW[uw]["w2"], HS[u], kc=HID // P).then_inc(sem("m_y"), 1)

            def shared(first, w):
                def hid(b, u):
                    hidden(b + first, (u + first) % 2, w % 2, (XFS[0][:, :, b, :], XFS[1][:, :, b, :]))

                def down(b, u):
                    output(b + first, (u + first) % 2, w % 2)
                pe.wait_ge(sem("m_w_lo"), w * 2 + 2 + earlier("m_w_lo"))
                pipeline(pe, [(hid, 0), (down, 1)])

            def g_hidden(n, u):
                pe.wait_ge(sem("m_g_lo"), n + 1)
                pe.wait_ge(sem("m_w_lo"), n * 2 + 3 + earlier("m_w_lo"))
                hidden(n + TILES0, u, 1 - u, XGS)

            def g_output(n, u):
                pe.wait_ge(sem("m_w_lo"), n * 2 + 4 + earlier("m_w_lo"))
                output(n + TILES0, u, 1 - u)

            shared(SHARED0, 0)
            pipeline(pe, [(g_t, 0), (g_hidden, 1), (g_output, 2)], n=NT)
            shared(SHARED1, LAST)

        @block.vector
        def _(v):
            def own_wait():
                v.sem_inc(sem("turns"), 1)

            def stats(tag, src):
                chain = Chain(v, norm_sem("stats", tag)[0], 5, norm_sem("stats", tag)[1])

                def step(b, u):
                    chain.begin(b)
                    own_wait()
                    for j in range(J):
                        chain.done(v.bn_stats(BN[tag][u][:, j, :], src[:, b, j, :]))
                    chain.wait()
                    own_wait()
                    for j in range(J):
                        chain.done(v.bn_aggr(AG[tag][u][:, j, :], BN[tag][u][:, j, :]))
                    chain.wait()
                    chain.done(v.tensor_copy(MEAN[tag][:, b, :], AG[tag][u][:, :, 0]))
                    v.tensor_scalar(VAR[tag][:, b, :], AG[tag][u][:, :, 1], EPS, None,
                                    ALU.add).then_inc(norm_sem("var", tag)[0], 1)
                    chain.end()
                return step

            def stats_all(tag, src):
                which, count = norm_sem("stats", tag)
                for t in range(T):
                    if tag == "n0" and t in (0, T // 2):
                        v.wait_ge(sem("x_rest_loaded" if t else "x_loaded"), 16)
                    v.bn_stats(BN_ALL[:, t, :], src[:, t // J, t % J, :]).then_inc(which, 1)
                v.wait_ge(which, count + T)
                for t in range(T):
                    v.bn_aggr(AG_ALL[:, t, :], BN_ALL[:, t, :]).then_inc(which, 1)
                v.wait_ge(which, count + 2 * T)
                v.tensor_copy(MEAN[tag][:, :, :].rearrange("p b j -> p (b j)"), AG_ALL[:, :, 0]).then_inc(which, NB * 5 - 2 * T)
                v.tensor_scalar(VAR[tag][:, :, :].rearrange("p b j -> p (b j)"), AG_ALL[:, :, 1], EPS, None,
                                ALU.add).then_inc(norm_sem("var", tag)[0], NB)

            stats_all("n0", X)
            wait_norm(v, "stats", "n0", NB * 5)
            wait_norm(v, "rstd", "n0", NB)
            with v.Fori(0, NB) as b:
                for j in range(J):
                    v.tensor_scalar(XN[:, b, j, :], X[:, b, j, :], MEAN["n0"][:, b, j:j + 1],
                                    RSTD["n0"][:, b, j:j + 1], ALU.subtract, ALU.mult).then_inc(sem("xn"), 1)
            v.wait_ge(sem("xn"), T)
            stats_all("n1", XN)

            v.wait_ge(sem("const_loaded"), 80)
            v.wait_ge(sem("pool_const"), 9)
            v.wait_ge(sem("decay_exp"), 1)
            v.tensor_scalar(WD[:, :], WD[:, :], -1.0, None, ALU.mult).then_inc(sem("decay"), 1)
            v.wait_ge(sem("decay"), 1)

            def norm(stage, tag, src, base=0):
                def step(turn, u):
                    released(v, sem(f"{stage}_t"), turn, base=earlier(f"{stage}_t"))
                    b = turn - base
                    wait_norm(v, "stats", tag, (b + 1) * 5)
                    wait_norm(v, "rstd", tag, b + 1)
                    for j in range(J):
                        ins = v.tensor_scalar(XT[u][:, j, :], src[:, b, j, :], MEAN[tag][:, b, j:j + 1],
                                              RSTD[tag][:, b, j:j + 1], ALU.subtract, ALU.mult)
                    ins.then_inc(sem(f"{stage}_xt"), 1)
                return step

            def b_mix(b, u):
                h, shifted = HT[u][:, :, 1:S + 1], HT[u][:, :, 0:S]
                v.wait_ge(sem("b_ht"), (b + 1) * 2)
                v.tensor_tensor(DIFF, h, shifted, ALU.subtract).then_inc(sem("b_diff"), 1)
                v.wait_ge(sem("b_diff"), b + 1)
                for m, tm in enumerate(("tmk", "tmv", "tmr")):
                    released(v, sem("b_mix_lo"), b, depth=1, per=3)
                    v.scalar_tensor_tensor(MIX[m][:, 0, :], DIFF[:, 0, :], vec(tm, 0), shifted[:, 0, :], ALU.mult, ALU.add)
                    v.scalar_tensor_tensor(MIX[m][:, 1, :], DIFF[:, 1, :], vec(tm, 1), shifted[:, 1, :],
                                           ALU.mult, ALU.add).then_inc(sem("b_mixed"), 1)

            chain_w = Chain(v, sem("b_wkv"), 14)

            def wkv_max(b, u):
                chain_w.begin(b)
                k, uk = KB[u], UK[u]
                before, after = PPX[:, :, 0:S], PPX[:, :, 1:S + 1]
                v.wait_ge(sem("b_k"), (b + 1) * 5)
                for c in range(C):
                    chain_w.done(v.tensor_tensor_scan(PPX[:, c, 1:S + 1], WD[:, c:c + 1].broadcast_to([P, S]), k[:, c, :],
                                                      LOWEST, ALU.add, ALU.max))
                chain_w.wait()
                released(v, sem("b_y_lo"), b, depth=1)
                chain_w.done(v.tensor_tensor(T1, before, uk, ALU.max))
                for c in range(C):
                    chain_w.done(v.scalar_tensor_tensor(T3[:, c, :], before[:, c, :], WD[:, c:c + 1], after[:, c, :],
                                                        ALU.add, ALU.subtract))
                chain_w.wait()
                v.tensor_tensor(k, k, after, ALU.subtract).then_inc(sem("b_e_state"), 1)
                chain_w.done(v.tensor_tensor(T2, before, T1, ALU.subtract))
                v.tensor_tensor(uk, uk, T1, ALU.subtract).then_inc(sem("b_e_out"), 1)

            def wkv_state(b, u):
                k, uk, val = KB[u], UK[u], bank(2 + u)
                v.wait_ge(sem("b_exp"), b * 4 + 2)
                v.wait_ge(sem("b_kvr"), b * 3 + 2)
                chain_w.wait()
                v.wait_ge(sem("b_e_out"), b + 1)
                chain_w.done(v.tensor_tensor(T1, k, val, ALU.mult))
                for c in range(C):
                    chain_w.done(v.tensor_tensor_scan(BB[:, c, 1:S + 1], T3[:, c, :], k[:, c, :], 0.0, ALU.mult, ALU.add))
                chain_w.wait()
                for c in range(C):
                    chain_w.done(v.tensor_tensor_scan(AA[:, c, 1:S + 1], T3[:, c, :], T1[:, c, :], 0.0, ALU.mult, ALU.add))
                chain_w.wait()
                v.wait_ge(sem("b_exp"), b * 4 + 4)
                v.tensor_tensor(T3, T2, AA[:, :, 0:S], ALU.mult).then_inc(sem("b_num"), 1)
                chain_w.done(v.tensor_tensor(T1, uk, val, ALU.mult))
                chain_w.wait()
                v.wait_ge(sem("b_num"), b + 1)
                chain_w.done(v.tensor_tensor(T3, T3, T1, ALU.add))

            def wkv_y(b, u):
                v.wait_ge(sem("b_den"), (b + 1) * 3)
                chain_w.done(v.reciprocal(T2, T2))
                chain_w.wait()
                v.tensor_tensor(T3, T3, T2, ALU.mult).then_inc(sem("b_y"), 1)
                chain_w.end()

            def y_lo(b, u):
                v.wait_ge(sem("b_y_hi"), b + 1)
                v.tensor_tensor(RW[u][1], T3, f(RW[u][0]), ALU.subtract).then_inc(sem("b_y_lo"), 1)

            def b_add(b, u):
                v.wait_ge(sem("b_o"), b + 1)
                v.tensor_tensor(XN[:, b, :, :], XN[:, b, :, :], bank(7), ALU.add).then_inc(sem("b_done"), 1)
                v.wait_ge(sem("b_done"), b + 1)
                stats_n2(b, u)

            stats_n2 = stats("n2", XN)
            pipeline(v, [(norm("b", "n1", XN), 0), (y_lo, 2), (wkv_max, 1), (b_mix, 0), (wkv_state, 1), (b_add, 2), (wkv_y, 1)])

            stats_n3 = stats("n3", X)

            def c_mix(b, u):
                h, shifted = HT[u][:, :, 1:S + 1], HT[u][:, :, 0:S]
                v.wait_ge(sem("c_ht"), (b + 1) * 2 + earlier("c_ht"))
                v.tensor_tensor(DIFF, h, shifted, ALU.subtract).then_inc(sem("c_diff"), 1)
                v.wait_ge(sem("c_diff"), b + 1 + earlier("c_diff"))
                for m, tm in enumerate(("ftmk", "ftmr")):
                    released(v, sem("c_mix_hi"), b, depth=1, per=2, base=earlier("c_mix_hi"))
                    v.scalar_tensor_tensor(MIX[m][:, 0, :], DIFF[:, 0, :], vec(tm, 0), shifted[:, 0, :], ALU.mult, ALU.add)
                    v.scalar_tensor_tensor(MIX[m][:, 1, :], DIFF[:, 1, :], vec(tm, 1), shifted[:, 1, :],
                                           ALU.mult, ALU.add).then_inc(sem("c_mixed"), 1)
                for m in range(2):
                    v.wait_ge(sem("c_mix_hi"), b * 2 + (m + 1) + earlier("c_mix_hi"))
                    v.tensor_tensor(FMIXS[u][m][1], MIX[m], f(FMIXS[u][m][0]), ALU.subtract).then_inc(sem("c_mix_lo"), 1)

            def c_kk(b, u):
                for q in range(4):
                    v.wait_ge(sem("c_square"), b * 4 + (q + 1))
                    v.wait_ge(sem("c_kk_hi"), b * 4 + (q + 1))
                    v.tensor_tensor(KKS[1][:, q], KK[:, q], f(KKS[0][:, q]), ALU.subtract).then_inc(sem("c_kk"), 1)

            def c_add(b, u):
                v.wait_ge(sem("c_sig"), b + 1)
                v.wait_ge(sem("c_val"), b + 1)
                v.tensor_tensor(GATED, SIG[u], bank(4), ALU.mult).then_inc(sem("c_gated"), 1)
                v.wait_ge(sem("c_gated"), b + 1)
                v.wait_ge(sem("c_residual"), b + 1)
                v.tensor_tensor(X[:, b, :, :], X[:, b, :, :], GATED, ALU.add).then_inc(sem("c_done"), 1)
                v.wait_ge(sem("c_done"), b + 1)
                stats_n3(b, u)

            pipeline(v, [(norm("c", "n2", XN), 0), (c_add, 3), (c_kk, 2), (c_mix, 0)], start=4)

            def attention(k, tag, next_tag):
                s, base = "d_", NB * k
                stats_next = stats(next_tag, X)

                def x_lo(b, u):
                    v.wait_ge(sem(s + "x_hi"), b + 1)
                    v.tensor_tensor(XS[1], bank(6), f(XS[0]), ALU.subtract).then_inc(sem(s + "x_lo"), 1)

                def ctx_lo(b, u):
                    v.wait_ge(sem(s + "ctx_hi"), b + 1)
                    v.tensor_tensor(CS[1], CT[:, :, b - base, :], f(CS[0]), ALU.subtract).then_inc(sem(s + "ctx_lo"), 1)

                def q_lo(b, u):
                    v.wait_ge(sem(s + "q_hi"), (b + 1) * 2)
                    for c in range(C):
                        v.scalar_tensor_tensor(QS[u][1][:, c, :], bank(6)[:, c, :], vec(f"bq{k}", c), f(QS[u][0][:, c, :]),
                                               ALU.add, ALU.subtract).then_inc(sem(s + "q_lo"), 1)

                def kv_read(b, u):
                    v.wait_ge(sem(s + "k_hi"), (b + 1) * 2)
                    for c in range(C):
                        v.scalar_tensor_tensor(KS[1][:, c, :], KEY[:, c, :], vec(f"bk{k}", c), f(KS[0][:, c, :]),
                                               ALU.add, ALU.subtract).then_inc(sem(s + "k_lo"), 1)
                    v.tensor_tensor(VAL[u][0:KEYS, :, 0:DK], VALP[0:KEYS, :].rearrange("p (h n) -> p h n", n=DK),
                                    row(f"bv{k}", KEYS).rearrange("p (h n) -> p h n", n=DK), ALU.add).then_inc(sem(s + "v"), 1)

                SC = PS[:, 0:4, 0:4 * KP].rearrange("p a (h n) -> p a h n", n=KP)[:, :, :, 0:KEYS]

                def peak(j):
                    def step(b, u):
                        v.wait_ge(sem(s + "score"), b * J + (j + 1))
                        v.tensor_reduce(PEAK[j].rearrange("p (a h) -> p a h", h=4), SC, AX.X, ALU.max).then_inc(sem(s + "peak"), 1)
                    return step

                def centre(j):
                    def step(b, u):
                        v.wait_ge(sem(s + "peak"), b * J + (j + 1))
                        v.tensor_tensor(PROB[j].rearrange("p (a h) n -> p a h n", h=4), SC,
                                        PEAK[j].rearrange("p (a h) -> p a h", h=4).unsqueeze(3).broadcast_to([P, 4, 4, KEYS]),
                                        ALU.subtract).then_inc(sem(s + "centred"), 1)
                    return step

                def out(j):
                    def step(b, u):
                        v.wait_ge(sem(s + "pv"), b * J + (j + 1))
                        v.reciprocal(RDEN[j].unsqueeze(2), PV[:, :, DK:DK + 1]).then_inc(sem(s + "rden"), 1)
                        v.wait_ge(sem(s + "rden"), b * J + (j + 1))
                        v.tensor_tensor(OUTN.rearrange("p (h n) -> p h n", n=DK), PV[:, :, 0:DK],
                                        RDEN[j].unsqueeze(2).broadcast_to([P, H, DK]), ALU.mult).then_inc(sem(s + "o"), 1)
                    return step

                def o_lo(j):
                    def step(b, u):
                        v.wait_ge(sem(s + "o_hi"), b * J + (j + 1))
                        v.tensor_tensor(OS[1], bank(7, P)[:, 0:2, :], f(OS[0]), ALU.subtract).then_inc(sem(s + "o_lo"), 1)
                    return step

                def add(j):
                    def step(b, u):
                        v.wait_ge(sem(s + "proj"), b * J + (j + 1))
                        v.wait_ge(sem(s + "bias"), b + 1)
                        v.tensor_tensor(X[:, b - base, j, :], X[:, b - base, j, :], bank(4)[:, 0, :], ALU.add).then_inc(sem(s + "added"), 1)
                        if j:
                            v.wait_ge(sem(s + "added"), (b + 1) * J)
                            stats_next(b - base, u)
                    return step

                for u in range(2):
                    v.memset(VAL[u][0:KEYS, :, DK:DK + 1], 1.0).then_inc(sem(s + "ones"), 1)
                v.wait_ge(sem(s + "ones"), 2 * (k + 1))
                def rhs(b, u):
                    if k == 0 and isinstance(b, int) and b == NB - 2:
                        prepare_rhs()

                pipeline(v, [(out(0), 2), (norm(f"d{k}", tag, X, base), 0), (peak(0), 1), (o_lo(0), 2), (centre(0), 1),
                             (x_lo, 0), (add(0), 2), (ctx_lo, 0), (q_lo, 0),
                             (out(1), 2), (peak(1), 1), (o_lo(1), 2), (kv_read, 0), (centre(1), 1), (add(1), 2), (rhs, 2)],
                         base=base)

            def prepare_rhs():
                chain = Chain(v, sem("rhs"), 7)
                chain.begin(0)
                v.wait_ge(sem("rhs_loaded"), 16)
                chain.done(v.tensor_reduce(QMAX[:, 0, :], RHS_T, AX.X, ALU.max, apply_absolute_value=True))
                chain.wait()
                chain.done(v.tensor_scalar(QMAX[:, 1, :], QMAX[:, 0, :], 1e-12, 1.0 / 127.0, ALU.max, ALU.mult))
                chain.wait()
                chain.done(v.reciprocal(QMAX[:, 2, :], QMAX[:, 1, :]))
                chain.wait()
                for n in range(C):
                    chain.done(v.tensor_scalar(RHS_Q[:, n, :], RHS_T[:, n, :], QMAX[:, 2, n:n + 1], ROUND, ALU.mult, ALU.add))
                chain.wait()
                chain.done(v.tensor_scalar(RHS_Q, RHS_Q, -ROUND, -127.0, ALU.add, ALU.max))
                chain.wait()
                v.tensor_scalar(RHS_Q, RHS_Q, 127.0, None, ALU.min).then_inc(sem("rhs_q"), 1)
                chain.done(v.tensor_scalar(QDIAG[:, 0, :], IDENT[:, :], QMAX[:, 1, 0:1], None, ALU.mult))
                v.tensor_scalar(QDIAG[:, 1, :], IDENT[:, :], QMAX[:, 1, 1:2], None, ALU.mult).then_inc(sem("rhs_diag"), 1)
                chain.end()

            attention(0, "n3", "n4")
            stats_n5 = stats("n5", X)
            chain_e = Chain(v, sem("e_chain"), 8)

            def e_norm(b, u):
                chain_e.begin(b)
                wait_norm(v, "stats", "n4", (b + 1) * 5)
                wait_norm(v, "rstd", "n4", b + 1)
                for j in range(J):
                    chain_e.done(v.tensor_scalar(XT[u][:, j, :], X[:, b, j, :], MEAN["n4"][:, b, j:j + 1],
                                                 RSTD["n4"][:, b, j:j + 1], ALU.subtract, ALU.mult))

            def e_top(b, u):
                chain_e.wait()
                chain_e.done(v.tensor_reduce(LR[u], XT[u], AX.X, ALU.max, apply_absolute_value=True))

            def e_scale(b, u):
                chain_e.wait()
                chain_e.done(v.tensor_scalar(LS[u], LR[u], 1e-12, 1.0 / 127.0, ALU.max, ALU.mult))
                chain_e.wait()
                chain_e.done(v.reciprocal(LR[u], LS[u]))
                chain_e.wait()

            def e_round(b, u):
                released(v, sem("e_t"), b, base=earlier("e_t"))
                for j in range(J):
                    chain_e.done(v.tensor_scalar(XQ[u][:, j, :], XT[u][:, j, :], LR[u][:, j:j + 1], ROUND, ALU.mult, ALU.add))
                chain_e.wait()
                chain_e.done(v.tensor_scalar(XQ[u], XQ[u], -ROUND, -127.0, ALU.add, ALU.max))
                chain_e.wait()
                v.tensor_scalar(XQ[u], XQ[u], 127.0, None, ALU.min).then_inc(sem("e_xt"), 1)
                chain_e.end()

            def e_out(b, u):
                v.wait_ge(sem("e_prod"), b + 1)
                for j in range(J):
                    v.scalar_tensor_tensor(QOUT[u][:, j, :], bank(4 + u)[:, j, :], LS[u][:, j:j + 1], QSCALE[:, :],
                                           ALU.mult, ALU.mult).then_inc(sem("e_scaled"), 1)

            def e_add(b, u):
                v.wait_ge(sem("e_scaled"), (b + 1) * J)
                v.tensor_tensor(X[:, b, :, :], X[:, b, :, :], QOUT[u], ALU.add).then_inc(sem("e_added"), 1)

            def e_stats(b, u):
                v.wait_ge(sem("e_added"), b + 1)
                stats_n5(b, u)

            v.wait_ge(sem("qw"), 2)
            v.wait_ge(sem("rhs_diag"), 1 + earlier("rhs_diag"))
            v.wait_ge(sem("rhs"), 7)
            pipeline(v, [(e_norm, 0), (e_out, 1), (e_top, 0), (e_add, 1), (e_scale, 0), (e_round, 0), (e_stats, 1)])

            v.wait_ge(sem("we_loaded"), 48)
            v.tensor_reduce(BSUM, BE, AX.X, ALU.add).then_inc(sem("be"), 1)
            v.wait_ge(sem("be"), 1 + earlier("be"))
            for c in range(C):
                ins = v.tensor_scalar(BWIDE[:, c, :], ONES[:, :], BSUM[:, c:c + 1], 1.0 / E, ALU.mult, ALU.mult)
            ins.then_inc(sem("be_wide"), 1)
            v.wait_ge(sem("folded"), 2)
            v.tensor_tensor(W["ao1"][1], FOLD, f(W["ao1"][0]), ALU.subtract).then_inc(sem("folded"), 1)
            v.wait_ge(sem("fold"), 2)
            v.tensor_tensor(row("bo1"), row("bo1"), PS[:, 1, 0:D], ALU.add).then_inc(sem("bo1"), 1)

            v.wait_ge(sem("a_exp"), 1 + earlier("a_exp"))
            v.tensor_scalar(AD[0:NS, :], AD[0:NS, :], -1.0, None, ALU.mult).then_inc(sem("a"), 1)
            stats_n6 = stats("n6", X)

            def f_x_lo(b, u):
                v.wait_ge(sem("f_x_hi"), b + 1)
                v.tensor_tensor(FXS[1], bank(6), f(FXS[0]), ALU.subtract).then_inc(sem("f_x_lo"), 1)

            def f_softplus(b, u):
                v.wait_ge(sem("f_ln"), b + 1)
                v.scalar_tensor_tensor(SP_, DT, 0.0, DTA, ALU.max, ALU.add).then_inc(sem("f_sp"), 1)

            def f_scan(b, u):
                v.wait_ge(sem("f_decay"), b + 1)
                v.wait_ge(sem("f_bx"), b + 1)
                v.tensor_tensor_scan(ST[0:NS, :], AT[0:NS, :], BX[u][0:NS, :], 0.0, ALU.mult, ALU.add).then_inc(sem("f_states"), 1)

            def f_xi_lo(b, u):
                v.wait_ge(sem("f_xi_hi"), b + 1)
                v.tensor_tensor(XIS[1], XI[u], f(XIS[0]), ALU.subtract).then_inc(sem("f_xi_lo"), 1)

            def f_y(b, u):
                v.wait_ge(sem("f_sum"), b + 1)
                v.wait_ge(sem("f_gate"), b + 1)
                v.tensor_tensor(YF, GI[u], PS[:, 7:8, 0:S].broadcast_to([P, DI // P, S]), ALU.mult).then_inc(sem("f_y"), 1)

            def f_y_lo(b, u):
                v.wait_ge(sem("f_y_hi"), b + 1)
                v.tensor_tensor(YS[1], YF, f(YS[0]), ALU.subtract).then_inc(sem("f_y_lo"), 1)

            def f_add(b, u):
                v.wait_ge(sem("f_skipped"), b + 1)
                v.wait_ge(sem("f_out"), b + 1)
                v.tensor_tensor(X[:, b, :, :], X[:, b, :, :], bank(7), ALU.add).then_inc(sem("f_added"), 1)
                v.wait_ge(sem("f_added"), b + 1)
                stats_n6(b, u)

            def f_free(b, u):
                released(v, sem("f_skipped"), b)

            pipeline(v, [(f_free, 0), (norm("f", "n5", X), 0), (f_xi_lo, 1), (f_y_lo, 3), (f_scan, 2), (f_x_lo, 0), (f_add, 3), (f_y, 2),
                         (f_softplus, 1)], start=4)

            attention(1, "n6", "n7")

            v.sem_inc(sem("m_h"), 8)
            v.sem_inc(sem("m_acc"), 2)

            def m_norm(b, u):
                released(v, sem("m_t"), b, base=earlier("m_t"))
                released(v, sem("m_kept"), b)
                wait_norm(v, "stats", "n7", (b + 1) * 5)
                wait_norm(v, "rstd", "n7", b + 1)
                for j in range(J):
                    ins = v.tensor_scalar(XT[u][:, j, :], X[:, b, j, :], MEAN["n7"][:, b, j:j + 1],
                                          RSTD["n7"][:, b, j:j + 1], ALU.subtract, ALU.mult)
                ins.then_inc(sem("m_xt"), 1)

            def m_x_lo(b, u):
                v.wait_ge(sem("m_x_hi"), b + 1)
                v.tensor_tensor(XFS[1][:, :, b, :], bank(6 + u), f(XFS[0][:, :, b, :]), ALU.subtract).then_inc(sem("m_x_lo"), 1)

            def m_logits(b, u):
                v.wait_ge(sem("m_logit"), b + 1)
                v.tensor_tensor(LOGIT.rearrange("p (b j) e -> p b j e", j=J)[:, b, :, :],
                                PS[:, 4 + u, 0:J * E].rearrange("p (j e) -> p j e", e=E),
                                ROW[:, NROW - E:NROW].unsqueeze(1).broadcast_to([P, J, E]), ALU.add).then_inc(sem("m_logit_read"), 1)

            pipeline(v, [(m_norm, 0), (m_x_lo, 1), (m_logits, 1)])

            mine = LOGIT.unsqueeze(3).broadcast_to([P, T, E, E])
            other = LOGIT.unsqueeze(2).broadcast_to([P, T, E, E])
            chain_r = Chain(v, sem("m_rank"), 29)
            chain_r.begin(0)
            v.wait_ge(sem("m_logit_read"), NB)
            v.wait_ge(sem("router_loaded"), 64)
            chain_r.done(v.tensor_tensor(ABOVE, other, mine, ALU.is_gt))
            chain_r.done(v.tensor_tensor(TIED, other, mine, ALU.is_equal))
            chain_r.done(v.tensor_reduce(TOP, LOGIT, AX.X, ALU.max))
            chain_r.wait()
            chain_r.done(v.tensor_tensor(TIED, TIED, LOWER[:, :, :].unsqueeze(1).broadcast_to([P, T, E, E]), ALU.mult))
            v.tensor_tensor(LOGIT, LOGIT, TOP.unsqueeze(2).broadcast_to([P, T, E]), ALU.subtract).then_inc(sem("m_centred"), 1)
            chain_r.wait()
            chain_r.done(v.tensor_tensor(TIED, TIED, ABOVE, ALU.add))
            chain_r.wait()
            chain_r.done(v.tensor_reduce(RANK, TIED, AX.X, ALU.add))
            chain_r.wait()
            v.tensor_scalar(TAKEN.rearrange("p e t -> p t e"), RANK, TOPK - 0.5, None, ALU.is_lt).then_inc(sem("m_taken"), 1)
            for k in range(TOPK):
                chain_r.done(v.tensor_scalar(IS[k], RANK, float(k), None, ALU.is_equal))
            v.wait_ge(sem("m_exp"), 1)
            chain_r.wait()
            for k in range(TOPK):
                chain_r.done(v.tensor_tensor(PICKED[k], IS[k], LOGIT_E, ALU.mult))
            chain_r.wait()
            for k in range(TOPK):
                chain_r.done(v.tensor_reduce(CW[:, k, :], PICKED[k], AX.X, ALU.add))
            chain_r.wait()
            chain_r.done(v.tensor_tensor(SHARE, CW[:, 0, :], CW[:, 1, :], ALU.add))
            chain_r.wait()
            chain_r.done(v.reciprocal(SHARE, SHARE))
            chain_r.wait()
            v.tensor_tensor(CW, CW, SHARE.unsqueeze(1).broadcast_to([P, TOPK, T]), ALU.mult).then_inc(sem("m_cw"), 1)
            v.wait_ge(sem("m_counted"), 1)
            in_group = PS[:, 6, 0:E * T].rearrange("p (e t) -> p e t", t=T)
            group = PS[:, 7, 0:E * T]
            chain_r.done(v.tensor_tensor_scan(SUMS.rearrange("p e t -> p (e t)"), KEEP, group, 0.0, ALU.mult, ALU.add))
            chain_r.wait()
            chain_r.done(v.tensor_tensor(POS, in_group, SUMS, ALU.add))
            chain_r.done(v.tensor_scalar(NTILES, SUMS[:, :, T - 1], 1.0 / TILE, 0.5 - 0.5 / TILE, ALU.mult, ALU.add))
            chain_r.wait()
            chain_r.done(v.tensor_tensor(POS, POS, group.rearrange("p (e t) -> p e t", t=T), ALU.subtract))
            chain_r.done(v.tensor_scalar(NTILES, NTILES, ROUND, None, ALU.add))
            chain_r.wait()
            chain_r.done(v.tensor_scalar(NTILES, NTILES, -ROUND, None, ALU.add))
            chain_r.wait()
            chain_r.done(v.tensor_tensor_scan(UPTO, ONES[:, 0:E], NTILES, 0.0, ALU.mult, ALU.add))
            chain_r.wait()
            chain_r.done(v.tensor_tensor(FIRST, UPTO, NTILES, ALU.subtract))
            chain_r.done(v.tensor_tensor(BELOW[0:1], UPTO[0:1].unsqueeze(1).broadcast_to([1, NT, E]),
                                         NUMBER[0:1].unsqueeze(2).broadcast_to([1, NT, E]), ALU.is_le))
            chain_r.wait()
            chain_r.done(v.tensor_scalar(FIRST, FIRST, float(TILE), None, ALU.mult))
            chain_r.done(v.tensor_reduce(EXPERT[0:1], BELOW[0:1], AX.X, ALU.add))
            chain_r.wait()
            chain_r.done(v.tensor_tensor(POS, POS, FIRST.unsqueeze(2).broadcast_to([P, E, T]), ALU.add))
            chain_r.done(v.tensor_scalar(EXPERT[0:1], EXPERT[0:1], E - 1.0, None, ALU.min))
            chain_r.wait()
            v.tensor_copy(EXPERTU, EXPERT[0:1]).then_inc(sem("m_routed"), 1)
            for k in range(TOPK):
                chain_r.done(v.tensor_tensor(PICKED[k], IS[k], POS.rearrange("p e t -> p t e"), ALU.mult))
            chain_r.wait()
            chain_r.end()
            for k in range(TOPK):
                v.tensor_reduce(SLOT[:, k, :], PICKED[k], AX.X, ALU.add).then_inc(sem("m_slot"), 1)
            v.wait_ge(sem("m_slot"), TOPK + earlier("m_slot"))
            v.tensor_copy(SLOTU, SLOT.rearrange("p k t -> p (k t)")).then_inc(sem("m_slots"), 1)
            v.wait_ge(sem("m_cw"), 1)

            def gate(first):
                def step(b, u):
                    n, u = b + first, (u + first) % 2
                    for m in range(HID // P):
                        v.wait_ge(sem("m_silu"), n * 4 + (m + 1))
                        v.tensor_tensor(HB[u][:, m, :], SILU[:, m, :], bank(m)[:, 1, :], ALU.mult).then_inc(sem("m_h"), 1)
                return step

            def h_lo(first):
                def step(b, u):
                    n, u = b + first, (u + first) % 2
                    v.wait_ge(sem("m_h_hi"), n + 3)
                    v.tensor_tensor(HS[u][1], HB[u], f(HS[u][0]), ALU.subtract).then_inc(sem("m_h_lo"), 1)
                return step

            def shared_add(first):
                def step(b, u):
                    n, u = b + first, (u + first) % 2
                    v.wait_ge(sem("m_y"), n + 3)
                    v.tensor_tensor(X[:, b, :, :], X[:, b, :, :], bank(4 + u), ALU.add).then_inc(sem("m_acc"), 1)
                return step

            def g_x_lo(n, u):
                v.wait_ge(sem("m_g_hi"), n + 1)
                v.tensor_tensor(XGS[1], bank(6), f(XGS[0]), ALU.subtract).then_inc(sem("m_g_lo"), 1)

            def g_copy(n, u):
                v.wait_ge(sem("m_y"), n + (TILES0 + 3))
                if not (isinstance(n, int) and n < 2):
                    v.wait_ge(sem(f"m_stored{u}"), (n - u) * 8)
                v.tensor_copy(YT[u], bank(4 + u)).then_inc(sem("m_acc"), 1)

            def routed_add(b, u):
                v.wait_ge(sem(f"m_back{u}"), (b - u) * (J * TOPK * 8) + J * TOPK * 16)
                v.wait_ge(sem("m_acc"), b + (SHARED1 + 3))
                for j in range(J):
                    v.scalar_tensor_tensor(X[:, b, j, :], BACK[0].rearrange("p (b j) d -> p b j d", j=J)[:, b, j, :],
                                           CW[:, 0, :].rearrange("p (b j) -> p b j", j=J)[:, b, j:j + 1],
                                           X[:, b, j, :], ALU.mult, ALU.add).then_inc(sem("m_first"), 1)
                v.wait_ge(sem("m_first"), (b + 1) * J + earlier("m_first"))
                for j in range(J):
                    ins = v.scalar_tensor_tensor(X[:, b, j, :], BACK[1].rearrange("p (b j) d -> p b j d", j=J)[:, b, j, :],
                                                 CW[:, 1, :].rearrange("p (b j) -> p b j", j=J)[:, b, j:j + 1],
                                                 X[:, b, j, :], ALU.mult, ALU.add)
                ins.then_inc(sem("m_done"), 1)

            pipeline(v, [(gate(SHARED0), 0), (h_lo(SHARED0), 0), (shared_add(SHARED0), 1)])
            pipeline(v, [(gate(TILES0), 1), (g_x_lo, 0), (h_lo(TILES0), 1), (g_copy, 2)], n=NT)
            pipeline(v, [(gate(SHARED1), 0), (h_lo(SHARED1), 0), (shared_add(SHARED1), 1), (routed_add, 1)])


def arrange(inputs):
    import numpy as np

    g = {k: np.asarray(v) for k, v in inputs.items()}

    def kn(w):
        k, n = w.shape
        return w.reshape(k // P, P, n).transpose(1, 0, 2).reshape(P, -1)

    def lanes(w):
        return w.reshape(-1, P).T

    def lanes64(w):
        return np.concatenate([w.reshape(1, NS), w.reshape(1, NS)], axis=1).reshape(P, 1)

    mats = {
        "wk": g["L0_attn_Wk"].T, "wv": g["L0_attn_Wv"].T, "wr": g["L0_attn_Wr"].T, "wo": g["L0_attn_Wo"].T,
        "wkey": g["L0_attn_Wkey"].T, "wval": g["L0_attn_Wval"].T, "wrec": g["L0_attn_Wrec"].T,
        "w_in": g["L1_attn_W_in"], "w_dt": g["L1_attn_W_dt"], "w_out": g["L1_attn_W_out"], "w_xp": g["L1_attn_W_xp"],
    }
    for n in range(2):
        for s in "qkv":
            mats[f"a{s}{n}"] = g[f"L{n}_xattn_W{s}"].T
    mats["ao0"] = g["L0_xattn_Wo"].T
    vecs = {
        "ln1_w": "L0_attn_ln1_w", "ln1_b": "L0_attn_ln1_b", "ln2_w": "L0_attn_ln2_w", "ln2_b": "L0_attn_ln2_b",
        "tmk": "L0_attn_att_tmk", "tmv": "L0_attn_att_tmv", "tmr": "L0_attn_att_tmr",
        "decay": "L0_attn_time_decay", "first": "L0_attn_time_first", "ftmk": "L0_attn_ffn_tmk",
        "ftmr": "L0_attn_ffn_tmr", "bq0": "L0_xattn_bq", "bk0": "L0_xattn_bk", "bq1": "L1_xattn_bq",
        "bk1": "L1_xattn_bk", "b_in": "L1_attn_b_in", "b_dt": "L1_attn_b_dt",
    }
    cols = [lanes(g[vecs[n]].reshape(-1)) if n in vecs else lanes64(g["L1_attn_b_xp" if n == "b_xp" else "L1_attn_A_log"])
            for n in VECS]
    rows = [g["L0_xattn_bv"], g["L0_xattn_bo"], g["L1_attn_b_out"], g["L1_attn_D"], g["L1_xattn_bv"], g["L1_xattn_bo"],
            g["L1_ffn_expert_bias"]]
    r = {
        "x": g["x"].reshape(NB, J, P, D).transpose(2, 0, 1, 3),
        "vec": np.concatenate(cols, axis=1),
        "row": np.concatenate(rows),
        "ident": np.eye(P, dtype=np.float32),
        "mask": np.repeat(np.eye(HC, dtype=np.float32), DK, axis=0),
        "lower": np.tril(np.ones((E, E), np.float32), -1),
        "earlier": np.triu(np.ones((P, P), np.float32), 1),
        "keep": np.tile((np.arange(T) > 0).astype(np.float32), E),
        "number": np.arange(NT, dtype=np.float32),
    }
    w1 = np.concatenate([g["L1_ffn_w1"], g["L1_ffn_sw1"]])
    w3 = np.concatenate([g["L1_ffn_w3"], g["L1_ffn_sw3"]])
    w2 = np.concatenate([g["L1_ffn_w2"], g["L1_ffn_sw2"]])
    r["moe"] = np.stack([np.concatenate([kn(w1[e].T), kn(w3[e].T), kn(w2[e].T)], axis=1) for e in range(NE)])
    r["router"] = g["L1_ffn_router_w"].T.reshape(C, P, E).transpose(1, 0, 2)
    r["rhs_t"] = g["L0_ffn_rhs"].T.reshape(C, P, D).transpose(1, 0, 2)
    r["we"] = g["L1_xattn_We"].reshape(E, C, P, D).transpose(2, 1, 0, 3).reshape(P, NB, J, D)
    r["wo2"] = g["L1_xattn_Wo"].T.reshape(C, P, D).transpose(1, 0, 2)
    r["be"] = g["L1_xattn_be"].reshape(E, C, P).transpose(2, 1, 0)
    context = np.zeros((P, C, NB, KP), np.float32)
    context[..., :KEYS] = g["ctx_1024"].reshape(NB, KEYS, C, P).transpose(3, 2, 0, 1)
    r["ctx"] = context
    for n, (_, ws) in enumerate(GROUPS):
        r[f"g{n}"] = np.concatenate([kn(mats[name]) for name, _, _ in ws], axis=1)
    return {k: np.ascontiguousarray(v) for k, v in r.items()}


def kernel(**inputs):
    import numpy as np
    import concourse.bacc as bacc
    from concourse.bass_utils import run_bass_kernel_spmd

    nc = bacc.Bacc("TRN2", target_bir_lowering=False, num_devices=1)
    arrays = arrange(inputs)
    used = {}
    for name, v in arrays.items():
        used[name] = nc.dram_tensor(f"in_{name}", v.shape, mybir.dt.from_np(v.dtype), kind="ExternalInput").ap()
    out = nc.dram_tensor("out_x", (P, NB, J, D), F32, kind="ExternalOutput").ap()
    rows_in = nc.dram_tensor("rows_in", (NT * TILE, D), F32).ap()
    rows_out = nc.dram_tensor("rows_out", (NT * TILE, D), F32).ap()
    build(nc, used, out, rows_in, rows_out)
    r = run_bass_kernel_spmd(nc, [{f"in_{k}": v for k, v in arrays.items()}], core_ids=[0])
    y = np.asarray(r.results[0]["out_x"])
    return y.reshape(P, NB, J, D).transpose(1, 2, 0, 3).reshape(NB, S, D)
```
